# Optimizing a Trainium2 kernel written in Bass

```python
import numpy as np
import jax
import jax.numpy as jnp

def _softmax(x, axis=-1):
    return jax.nn.softmax(x, axis=axis)

def _gelu(x):
    return jax.nn.gelu(x, approximate=True)

def _silu(x):
    return jax.nn.silu(x)

def _sigmoid(x):
    return jax.nn.sigmoid(x)

def _layernorm(x, axis=-1, eps=1e-05):
    m = jnp.mean(x, axis=axis, keepdims=True)
    v = jnp.var(x, axis=axis, keepdims=True)
    return (x - m) / jnp.sqrt(v + eps)

def _scatter_add(tgt, idx, src, axis=0):
    return tgt.at[idx].add(src)

def _segment_sum(src, seg, n):
    return jax.ops.segment_sum(src, seg, n)
kernel_name = 'mk_flamingo_gated_d2_seqx_r8_b1e6e2'

def setup_inputs(seed: int=0):
    np.random.seed(seed)
    _w = jnp.asarray

    def _rec_inputs():
        import jax
        import jax.numpy as jnp
        _rk = jax.random.key(seed)
        x = 0.5 + 0.2887 * jax.random.normal(jax.random.fold_in(_rk, 1), (4, 256, 256), jnp.float32)
        _lenS = 256 - jax.random.randint(jax.random.fold_in(_rk, 7), (4,), 0, max(1, 256 // 4) + 1, jnp.int32)
        _lenS2 = 256 - jax.random.randint(jax.random.fold_in(_rk, 8), (4,), 0, max(1, 256 // 4) + 1, jnp.int32)
        _ctx_512P = jax.random.normal(jax.random.fold_in(_rk, 11), (4, 16, 64), jnp.float32)
        _ctx_512c = jax.random.dirichlet(jax.random.fold_in(_rk, 511), 0.3 * jnp.ones((16,), jnp.float32), (4, 256))
        _ctx_512t = jnp.einsum('bsk,bkd->bsd', _ctx_512c, _ctx_512P)
        _ctx_512t = _ctx_512t * jax.lax.rsqrt(jnp.mean(jnp.square(_ctx_512t)) + 1e-12) * 0.953939
        ctx_512 = -0.000392918 + 0.999932 * (_ctx_512t + 0.3 * jax.random.normal(jax.random.fold_in(_rk, 611), (4, 256, 64), jnp.float32))
        _g = jax.random.normal(jax.random.fold_in(_rk, 9001), (2, 2), jnp.float32)
        _g = jnp.sign(_g) * jnp.maximum(jnp.abs(_g), 1.0) + (_g == 0) * 1.0
        g_xattn = _g[0]
        g_ffn = _g[1]
        return (x, ctx_512, g_xattn, g_ffn)
    x, ctx_512, g_xattn, g_ffn = _rec_inputs()

    def _L0_xattn_setup():
        import jax, jax.numpy as jnp
        import numpy as np
        B, N, D = (16, 256, 64)
        H = 4
        TOP_K_RATIO = 0.3
        key = jax.random.key(seed)
        k1, k2, k3, k4 = jax.random.split(key, 4)
        h = jax.random.normal(k1, (B, N, D), dtype=jnp.float32)
        adj_raw = jax.random.uniform(k2, (B, N, N), dtype=jnp.float32)
        lim = 1.0 / np.sqrt(D)
        Wq = jax.random.uniform(k3, (D, D), minval=-lim, maxval=lim, dtype=jnp.float32)
        Wk = jax.random.uniform(k4, (D, D), minval=-lim, maxval=lim, dtype=jnp.float32)
        gamma_raw = jnp.float32(-0.85)
        return {'h': h, 'adj_raw': adj_raw, 'Wq': Wq, 'Wk': Wk, 'gamma_raw': gamma_raw}
    _L0_xattn_all = _L0_xattn_setup()
    _L0_xattn_in = {k: v for k, v in _L0_xattn_all.items() if k in ('Wq', 'Wk', 'gamma_raw')}
    del _L0_xattn_all

    def _L0_ffn_setup():
        import jax, jax.numpy as jnp
        import numpy as np
        N_BLOCKS = 16
        BLOCK_SIZE = 64
        TOP_K = N_BLOCKS // 4
        key = jax.random.key(seed)
        k1, k2, k3, k4, k5 = jax.random.split(key, 5)
        in_f, out_f = (256, 1024)
        x = jax.random.normal(k1, (2, 512, in_f), dtype=jnp.float32)
        Wr = jax.random.normal(k2, (N_BLOCKS, in_f), dtype=jnp.float32) * in_f ** (-0.5)
        br = jnp.zeros((N_BLOCKS,), dtype=jnp.float32)
        W1 = jax.random.normal(k3, (out_f, in_f), dtype=jnp.float32) * in_f ** (-0.5)
        W2 = jax.random.normal(k4, (in_f, out_f), dtype=jnp.float32) * out_f ** (-0.5)
        return {'x': x, 'Wr': Wr, 'br': br, 'W1': W1, 'W2': W2}
    _L0_ffn_all = _L0_ffn_setup()
    _L0_ffn_in = {k: v for k, v in _L0_ffn_all.items() if k in ('Wr', 'br', 'W1', 'W2')}
    del _L0_ffn_all

    def _L1_xattn_setup():
        import jax, jax.numpy as jnp
        import numpy as np
        B, S, L = (2, 128, 128)
        DIM_Q, H, K, D_C, D_CQ, R = (256, 16, 128, 64, 192, 64)

        def _rope_tables(length, dim):
            inv = 1.0 / 10000.0 ** (jnp.arange(0, dim, 2, dtype=jnp.float32) / dim)
            f = jnp.arange(length, dtype=jnp.float32)[:, None] * inv[None, :]
            sin = jnp.repeat(jnp.sin(f), 2, axis=-1)
            cos = jnp.repeat(jnp.cos(f), 2, axis=-1)
            return (sin, cos)

        def _rotate_half(x):
            half = x.shape[-1] // 2
            return jnp.concatenate([-x[..., half:], x[..., :half]], axis=-1)

        def _apply_rope(x, sin, cos):
            return x * cos + _rotate_half(x) * sin
        key = jax.random.key(seed)
        ks = jax.random.split(key, 8)
        return {'hidden_q': jax.random.normal(ks[0], (B, S, DIM_Q), jnp.float32), 'kv_c': jax.random.normal(ks[1], (B, L, D_C), jnp.float32), 'Wq': jax.random.normal(ks[2], (H * K, DIM_Q), jnp.float32) / np.sqrt(DIM_Q).astype(np.float32), 'w_kc_q': jax.random.normal(ks[3], (H, K, D_CQ), jnp.float32) / np.sqrt(K).astype(np.float32), 'w_kc_kv': jax.random.normal(ks[4], (H, K, D_C), jnp.float32) / np.sqrt(K).astype(np.float32), 'W_qr': jax.random.normal(ks[5], (H, D_CQ, R), jnp.float32) / np.float32(np.sqrt(D_CQ) * np.sqrt(R)), 'W_kr': jax.random.normal(ks[6], (H, D_C, R), jnp.float32) / np.sqrt(D_C).astype(np.float32), 'Wo': jax.random.normal(ks[7], (DIM_Q, H * K), jnp.float32) / np.sqrt(H * K).astype(np.float32)}
    _L1_xattn_all = _L1_xattn_setup()
    _L1_xattn_in = {k: v for k, v in _L1_xattn_all.items() if k in ('Wq', 'w_kc_q', 'w_kc_kv', 'W_qr', 'W_kr', 'Wo')}
    del _L1_xattn_all

    def _L1_ffn_setup():
        import math
        import jax, jax.numpy as jnp
        import numpy as np
        from jax import lax
        D = 256
        I = 128
        E = 32
        K = 4
        NG = 8
        TKG = 3
        NSH = 2
        SCALE = 2.5
        CF = 1.25
        B, S = (2, 256)

        def _router(x, router_w, e_bias):
            scores = jax.nn.sigmoid(x @ router_w.T)
            sc = scores + e_bias[None, :]
            T = x.shape[0]
            gs = sc.reshape(T, NG, E // NG)
            group_scores = lax.top_k(gs, 2)[0].sum(-1)
            _, gidx = lax.top_k(group_scores, TKG)
            gmask = jnp.zeros((T, NG), sc.dtype).at[jnp.arange(T)[:, None], gidx].set(1.0)
            smask = jnp.repeat(gmask, E // NG, axis=1)
            masked = jnp.where(smask > 0, sc, 0.0)
            _, topk_idx = lax.top_k(masked, K)
            topk_w = jnp.take_along_axis(scores, topk_idx, axis=1)
            topk_w = topk_w / (topk_w.sum(-1, keepdims=True) + 1e-20)
            topk_w = topk_w * SCALE
            return (topk_idx.astype(jnp.int32), topk_w)

        def _moe_forward(hidden_states, router_w, e_bias, W_gate, W_up, W_down, shared_gate, shared_up, shared_down):
            b, s, d = hidden_states.shape
            T = b * s
            C = int(math.ceil(CF * T / E))
            EC = E * C
            x = hidden_states.reshape(T, d)
            topk_idx, topk_w = _router(x, router_w, e_bias)
            expert_flat = topk_idx.reshape(-1)
            w_flat = topk_w.reshape(-1)
            tok_flat = jnp.repeat(jnp.arange(T, dtype=jnp.int32), K)
            sort_ix = jnp.argsort(expert_flat)
            e_sorted = expert_flat[sort_ix]
            tok_s = tok_flat[sort_ix]
            w_s = w_flat[sort_ix]
            counts = jnp.zeros(E, jnp.int32).at[e_sorted].add(1)
            group_start = jnp.concatenate([jnp.zeros(1, jnp.int32), jnp.cumsum(counts)[:-1].astype(jnp.int32)])
            pos = jnp.arange(T * K, dtype=jnp.int32) - group_start[e_sorted]
            valid = pos < C
            dest = e_sorted * C + jnp.where(valid, pos, 0)
            slots_token = jnp.zeros(EC, jnp.int32).at[dest].add(jnp.where(valid, tok_s, 0))
            slots_w = jnp.zeros(EC, w_s.dtype).at[dest].add(jnp.where(valid, w_s, 0.0))
            Xp = x[slots_token].reshape(E, C, d)
            G = jnp.einsum('ecd,edi->eci', Xp, W_gate)
            U = jnp.einsum('ecd,edi->eci', Xp, W_up)
            Y = jnp.einsum('eci,eid->ecd', jax.nn.silu(G) * U, W_down)
            Yf = Y.reshape(EC, d) * slots_w[:, None]
            out = jnp.zeros((T, d), x.dtype).at[slots_token].add(Yf)
            shared = jax.nn.silu(x @ shared_gate.T) * (x @ shared_up.T) @ shared_down.T
            return (out + shared).reshape(b, s, d)
        key = jax.random.key(seed)
        ks = jax.random.split(key, 8)

        def rn(k, shape, scale=0.02):
            return jax.random.normal(k, shape, jnp.float32) * scale
        return {'hidden_states': jax.random.normal(ks[0], (B, S, D), jnp.float32), 'router_w': rn(ks[1], (E, D)), 'e_bias': jnp.zeros((E,), jnp.float32), 'W_gate': rn(ks[2], (E, D, I)), 'W_up': rn(ks[3], (E, D, I)), 'W_down': rn(ks[4], (E, I, D)), 'shared_gate': rn(ks[5], (I * NSH, D)), 'shared_up': rn(ks[6], (I * NSH, D)), 'shared_down': rn(ks[7], (D, I * NSH))}
    _L1_ffn_all = _L1_ffn_setup()
    _L1_ffn_in = {k: v for k, v in _L1_ffn_all.items() if k in ('router_w', 'e_bias', 'W_gate', 'W_up', 'W_down', 'shared_gate', 'shared_up', 'shared_down')}
    del _L1_ffn_all
    return {'x': x, 'ctx_512': ctx_512, 'g_xattn': g_xattn, 'g_ffn': g_ffn, 'L0_xattn_Wq': _L0_xattn_in['Wq'], 'L0_xattn_Wk': _L0_xattn_in['Wk'], 'L0_xattn_gamma_raw': _L0_xattn_in['gamma_raw'], 'L0_ffn_Wr': _L0_ffn_in['Wr'], 'L0_ffn_br': _L0_ffn_in['br'], 'L0_ffn_W1': _L0_ffn_in['W1'], 'L0_ffn_W2': _L0_ffn_in['W2'], 'L1_xattn_Wq': _L1_xattn_in['Wq'], 'L1_xattn_w_kc_q': _L1_xattn_in['w_kc_q'], 'L1_xattn_w_kc_kv': _L1_xattn_in['w_kc_kv'], 'L1_xattn_W_qr': _L1_xattn_in['W_qr'], 'L1_xattn_W_kr': _L1_xattn_in['W_kr'], 'L1_xattn_Wo': _L1_xattn_in['Wo'], 'L1_ffn_router_w': _L1_ffn_in['router_w'], 'L1_ffn_e_bias': _L1_ffn_in['e_bias'], 'L1_ffn_W_gate': _L1_ffn_in['W_gate'], 'L1_ffn_W_up': _L1_ffn_in['W_up'], 'L1_ffn_W_down': _L1_ffn_in['W_down'], 'L1_ffn_shared_gate': _L1_ffn_in['shared_gate'], 'L1_ffn_shared_up': _L1_ffn_in['shared_up'], 'L1_ffn_shared_down': _L1_ffn_in['shared_down']}

def reference(x, ctx_512, g_xattn, g_ffn, L0_xattn_Wq, L0_xattn_Wk, L0_xattn_gamma_raw, L0_ffn_Wr, L0_ffn_br, L0_ffn_W1, L0_ffn_W2, L1_xattn_Wq, L1_xattn_w_kc_q, L1_xattn_w_kc_kv, L1_xattn_W_qr, L1_xattn_W_kr, L1_xattn_Wo, L1_ffn_router_w, L1_ffn_e_bias, L1_ffn_W_gate, L1_ffn_W_up, L1_ffn_W_down, L1_ffn_shared_gate, L1_ffn_shared_up, L1_ffn_shared_down):
    import jax
    import jax.numpy as jnp

    def _L0_xattn_ref(h, adj_raw, Wq, Wk, gamma_raw):
        import jax, jax.numpy as jnp
        import numpy as np
        B, N, D = (16, 256, 64)
        H = 4
        TOP_K_RATIO = 0.3
        b, n, dm = h.shape
        d = dm // H
        Q = (h @ Wq.T).reshape(b, n, H, d).transpose(0, 2, 1, 3)
        K = (h @ Wk.T).reshape(b, n, H, d).transpose(0, 2, 1, 3)
        sim = jnp.einsum('bhnd,bhmd->bnm', Q, K) / (jnp.sqrt(jnp.float32(d)) * H)
        k = max(1, int(n * TOP_K_RATIO))
        topk_vals = jax.lax.top_k(sim, k)[0]
        threshold = topk_vals[:, :, -1:]
        sparse_mask = (sim >= threshold).astype(sim.dtype)
        A_learned = jax.nn.sigmoid(sim) * sparse_mask
        A_learned = (A_learned + jnp.swapaxes(A_learned, -1, -2)) * 0.5
        gamma = jax.nn.sigmoid(gamma_raw)
        return (1.0 - gamma) * adj_raw + gamma * A_learned

    def _L0_ffn_ref(x, Wr, br, W1, W2):
        import jax, jax.numpy as jnp
        import numpy as np
        N_BLOCKS = 16
        BLOCK_SIZE = 64
        TOP_K = N_BLOCKS // 4
        x_shape = x.shape
        in_f = x_shape[-1]
        xf = x.reshape(-1, in_f)
        n = xf.shape[0]
        prob = jax.nn.softmax(xf @ Wr.T + br, axis=-1)
        _, idx = jax.lax.top_k(prob, TOP_K)
        mask = jnp.zeros((n, N_BLOCKS), dtype=xf.dtype)
        mask = mask.at[jnp.arange(n)[:, None], idx].set(1.0)
        W1b = W1.reshape(N_BLOCKS, BLOCK_SIZE, in_f)
        h = jnp.einsum('nf,ibf->nib', xf, W1b)
        h = jax.nn.gelu(h, approximate=False) * mask[:, :, None]
        W2b = W2.reshape(in_f, N_BLOCKS, BLOCK_SIZE)
        y = jnp.einsum('nib,fib->nf', h, W2b)
        return y.reshape(x_shape)

    def _L1_xattn_ref(hidden_q, kv_c, Wq, w_kc_q, w_kc_kv, W_qr, W_kr, Wo):
        import jax, jax.numpy as jnp
        import numpy as np
        B, S, L = (2, 128, 128)
        DIM_Q, H, K, D_C, D_CQ, R = (256, 16, 128, 64, 192, 64)

        def _rope_tables(length, dim):
            inv = 1.0 / 10000.0 ** (jnp.arange(0, dim, 2, dtype=jnp.float32) / dim)
            f = jnp.arange(length, dtype=jnp.float32)[:, None] * inv[None, :]
            sin = jnp.repeat(jnp.sin(f), 2, axis=-1)
            cos = jnp.repeat(jnp.cos(f), 2, axis=-1)
            return (sin, cos)

        def _rotate_half(x):
            half = x.shape[-1] // 2
            return jnp.concatenate([-x[..., half:], x[..., :half]], axis=-1)

        def _apply_rope(x, sin, cos):
            return x * cos + _rotate_half(x) * sin
        Bv, Sv, _ = hidden_q.shape
        _, Lv, _ = kv_c.shape
        q_hk = (hidden_q @ Wq.T).reshape(Bv, Sv, H, K)
        q_big = jnp.einsum('bshk,hkq->bshq', q_hk, w_kc_q)
        sin_q, cos_q = _rope_tables(Sv, D_CQ)
        q_big = _apply_rope(q_big, sin_q[None, :, None, :], cos_q[None, :, None, :])
        sin_k, cos_k = _rope_tables(Lv, D_C)
        kv_r = _apply_rope(kv_c, sin_k[None], cos_k[None])
        q_r = jnp.einsum('bshq,hqr->bhsr', q_big, W_qr)
        k_r = jnp.einsum('bld,hdr->bhlr', kv_r, W_kr)
        scores = jnp.einsum('bhsr,bhlr->bhsl', q_r, k_r)
        attn = jax.nn.softmax(scores, axis=-1)
        ctx_c = jnp.einsum('bhsl,bld->bhsd', attn, kv_r)
        ctx_lat = jnp.einsum('bhsd,hkd->bhsk', ctx_c, w_kc_kv)
        ctx = ctx_lat.transpose(0, 2, 1, 3).reshape(Bv, Sv, H * K)
        return ctx @ Wo.T

    def _L1_ffn_ref(hidden_states, router_w, e_bias, W_gate, W_up, W_down, shared_gate, shared_up, shared_down):
        import math
        import jax, jax.numpy as jnp
        import numpy as np
        from jax import lax
        D = 256
        I = 128
        E = 32
        K = 4
        NG = 8
        TKG = 3
        NSH = 2
        SCALE = 2.5
        CF = 1.25
        B, S = (2, 256)

        def _router(x, router_w, e_bias):
            scores = jax.nn.sigmoid(x @ router_w.T)
            sc = scores + e_bias[None, :]
            T = x.shape[0]
            gs = sc.reshape(T, NG, E // NG)
            group_scores = lax.top_k(gs, 2)[0].sum(-1)
            _, gidx = lax.top_k(group_scores, TKG)
            gmask = jnp.zeros((T, NG), sc.dtype).at[jnp.arange(T)[:, None], gidx].set(1.0)
            smask = jnp.repeat(gmask, E // NG, axis=1)
            masked = jnp.where(smask > 0, sc, 0.0)
            _, topk_idx = lax.top_k(masked, K)
            topk_w = jnp.take_along_axis(scores, topk_idx, axis=1)
            topk_w = topk_w / (topk_w.sum(-1, keepdims=True) + 1e-20)
            topk_w = topk_w * SCALE
            return (topk_idx.astype(jnp.int32), topk_w)

        def _moe_forward(hidden_states, router_w, e_bias, W_gate, W_up, W_down, shared_gate, shared_up, shared_down):
            b, s, d = hidden_states.shape
            T = b * s
            C = int(math.ceil(CF * T / E))
            EC = E * C
            x = hidden_states.reshape(T, d)
            topk_idx, topk_w = _router(x, router_w, e_bias)
            expert_flat = topk_idx.reshape(-1)
            w_flat = topk_w.reshape(-1)
            tok_flat = jnp.repeat(jnp.arange(T, dtype=jnp.int32), K)
            sort_ix = jnp.argsort(expert_flat)
            e_sorted = expert_flat[sort_ix]
            tok_s = tok_flat[sort_ix]
            w_s = w_flat[sort_ix]
            counts = jnp.zeros(E, jnp.int32).at[e_sorted].add(1)
            group_start = jnp.concatenate([jnp.zeros(1, jnp.int32), jnp.cumsum(counts)[:-1].astype(jnp.int32)])
            pos = jnp.arange(T * K, dtype=jnp.int32) - group_start[e_sorted]
            valid = pos < C
            dest = e_sorted * C + jnp.where(valid, pos, 0)
            slots_token = jnp.zeros(EC, jnp.int32).at[dest].add(jnp.where(valid, tok_s, 0))
            slots_w = jnp.zeros(EC, w_s.dtype).at[dest].add(jnp.where(valid, w_s, 0.0))
            Xp = x[slots_token].reshape(E, C, d)
            G = jnp.einsum('ecd,edi->eci', Xp, W_gate)
            U = jnp.einsum('ecd,edi->eci', Xp, W_up)
            Y = jnp.einsum('eci,eid->ecd', jax.nn.silu(G) * U, W_down)
            Yf = Y.reshape(EC, d) * slots_w[:, None]
            out = jnp.zeros((T, d), x.dtype).at[slots_token].add(Yf)
            shared = jax.nn.silu(x @ shared_gate.T) * (x @ shared_up.T) @ shared_down.T
            return (out + shared).reshape(b, s, d)
        return _moe_forward(hidden_states, router_w, e_bias, W_gate, W_up, W_down, shared_gate, shared_up, shared_down)
    x = x + jnp.tanh(g_xattn[0]) * _L0_xattn_ref(ctx_512, _layernorm(x, axis=-1), L0_xattn_Wq, L0_xattn_Wk, L0_xattn_gamma_raw)
    x = x + jnp.tanh(g_ffn[0]) * _L0_ffn_ref(_layernorm(x, axis=-1), L0_ffn_Wr, L0_ffn_br, L0_ffn_W1, L0_ffn_W2)
    x = x + jnp.tanh(g_xattn[1]) * _L1_xattn_ref(_layernorm(x, axis=-1), ctx_512, L1_xattn_Wq, L1_xattn_w_kc_q, L1_xattn_w_kc_kv, L1_xattn_W_qr, L1_xattn_W_kr, L1_xattn_Wo)
    x = x + jnp.tanh(g_ffn[1]) * _L1_ffn_ref(_layernorm(x, axis=-1), L1_ffn_router_w, L1_ffn_e_bias, L1_ffn_W_gate, L1_ffn_W_up, L1_ffn_W_down, L1_ffn_shared_gate, L1_ffn_shared_up, L1_ffn_shared_down)
    return x

_drawn_inputs = setup_inputs


def setup_inputs(seed=0):
    import zlib

    import numpy as np

    out = dict(_drawn_inputs(seed))
    spreads = {'g_ffn': (-1.0, 0.6), 'L0_ffn_br': (0.0, 0.1), 'L1_ffn_e_bias': (0.0, 0.8)}
    factors = {'L1_ffn_router_w': 8.0,
     'L1_ffn_W_gate': 8.0,
     'L1_ffn_W_up': 8.0,
     'L1_ffn_W_down': 8.0,
     'L1_ffn_shared_gate': 4.32,
     'L1_ffn_shared_up': 4.305,
     'L1_ffn_shared_down': 4.293}
    for name, (base, spread) in spreads.items():
        noise = np.random.default_rng([zlib.crc32(name.encode()), seed]).standard_normal(out[name].shape)
        drawn = base * np.exp(spread * noise) if base else spread * noise
        out[name] = jnp.asarray(drawn.astype(out[name].dtype))
    for name, factor in factors.items():
        out[name] = (out[name] * factor).astype(out[name].dtype)
    return out
```

```python
from contextlib import ExitStack

import concourse.bass as bass
import numpy as np
from concourse import mybir

F32 = mybir.dt.float32
BF16 = mybir.dt.bfloat16
ALU = mybir.AluOpType
ACT = mybir.ActivationFunctionType
AX = mybir.AxisListType

P = 128
B, S, D = 4, 256, 256
T = B * S
NT = T // P
KT = D // P
LN_EPS = 1e-5
BIG, NEG = 3.0e38, -3.0e38

DC = 64
TOP_ADJ = int(S * 0.3)
ROUNDS = (TOP_ADJ + 7) // 8

NBLK, BLK, TOP_BLK = 16, 64, 4
HID = NBLK * BLK

H, HK, DQ, R = 16, 128, 192, 64
HALF = DQ // 2
PAIRS = H // 2

E, EI = 32, 128
TOP_E, GROUPS, TOP_G = 4, 8, 3
GE = E // GROUPS
CAP = -(-5 * T // (4 * E))
ROUTE_SCALE = 2.5
EPT = P // CAP
ST_T = -(-E // EPT)
SLOTS = EPT * CAP
SHARED = 256
STAGES = 4


class Shared:
    pass


def layernorm_vector(dve, g, ready):
    for t in range(NT):
        ready(t)
        dve.bn_stats(g.stat[:, t, :], g.X[:, t, :]).then_inc(g.ln_stats, 1)
    for t in range(NT):
        dve.wait_ge(g.ln_stats, g.ln_base * NT + t + 1)
        dve.bn_aggr(g.mv[:, t, :], g.stat[:, t, :]).then_inc(g.ln_aggr, 1)
    dve.wait_ge(g.ln_aggr, g.ln_base * NT + NT)
    dve.tensor_scalar(g.var[:, :], g.mv[:, :, 1], LN_EPS, None, ALU.add).then_inc(g.ln_var, 1)
    dve.wait_ge(g.ln_std, g.ln_base + 1)
    dve.reciprocal(g.rstd[:, :], g.std[:, :]).then_inc(g.ln_rstd, 1)
    dve.wait_ge(g.ln_rstd, g.ln_base + 1)
    for t in range(NT):
        dve.tensor_scalar(g.XN[:, t, :], g.X[:, t, :], g.mv[:, t, 0:1], g.rstd[:, t:t + 1],
                          ALU.subtract, ALU.mult).then_inc(g.ln_xn, 1)


def layernorm_scalar(act, g):
    act.wait_ge(g.ln_var, g.ln_base + 1)
    act.activation(g.std[:, :], g.var[:, :], ACT.Sqrt).then_inc(g.ln_std, 1)


def transpose_xn_tensor(pe, g):
    for half in range(2):
        pe.wait_ge(g.ln_xn, g.ln_base * NT + 4 * half + 4)
        for k in range(KT):
            for j in range(4):
                mm = pe.transpose(g.ps[:, 2 * half + k, j * P:(j + 1) * P],
                                  g.XN[:, 4 * half + j, k * P:(k + 1) * P], g.ident[:, :])
            mm.then_inc(g.xt_ps, 1)


def transpose_xn_scalar(act, g):
    for half in range(2):
        for k in range(KT):
            act.wait_ge(g.xt_ps, (g.ln_base - 1) * 4 + 2 * half + k + 1)
            act.activation(g.XT[:, k, 512 * half:512 * half + 512], g.ps[:, 2 * half + k, :],
                           ACT.Copy).then_inc(g.xt, 1)


def stage_adjacency(nc, g, i):
    with ExitStack() as ctx:
        sb = lambda name, shape, dt=F32: ctx.enter_context(nc.sbuf_tensor(name, shape, dt))
        sem = lambda name: ctx.enter_context(nc.semaphore(name))
        CT = sb("CT", [P, NT, DC])
        CTT = sb("CTT", [DC, T])
        wq = sb("wq", [DC, DC])
        wk = sb("wk", [DC, DC])
        GT = sb("GT", [DC, DC])
        V = sb("V", [DC, T])
        SIM = sb("SIM", [P, NT, S])
        SIG = sb("SIG", [P, NT, S])
        work = sb("work", [P, 2, S])
        m8 = sb("m8", [P, 2, ROUNDS, 8])
        thr = sb("thr", [P, NT])
        A = sb("A", [P, NT, S])
        XA = sb("XA", [P, NT, S])
        raw = sb("raw", [P, 5])
        gam = sb("gam", [P, 4])
        w1 = sb("w1", [P, HID // P, D])
        w2 = sb("w2", [P, KT, HID])
        wr = sb("wr", [NBLK, D])
        ck = sb("ck", [P, 2, DC])
        sk = sb("sk", [P, 2, DC])
        kc = sb("kc", [P, NT, DC])
        ks = sb("ks", [P, NT, DC])

        d_x, d_ctx, d_wqk, d_raw, d_rope = map(sem, ["d_x", "d_ctx", "d_wqk", "d_raw", "d_rope"])
        d_w1, d_w2, d_wr = map(sem, ["d_w1", "d_w2", "d_wr"])
        id_zero, id_ok, kd_zero, kv_mul, kv_sum, kv_ok = map(
            sem, ["id_zero", "id_ok", "kd_zero", "kv_mul", "kv_sum", "kv_ok"])
        filled, emptied, at_ps = map(sem, ["filled", "emptied", "at_ps"])
        tanh_ok, gam_ok, max_ok, rep_ok, thr_ok, a_ok, xa_ok, x_ok = map(
            sem, ["tanh_ok", "gam_ok", "max_ok", "rep_ok", "thr_ok", "a_ok", "xa_ok", "x_ok"])
        sim_ok, sig_ok, mix_ok = map(sem, ["sim_ok", "sig_ok", "mix_ok"])

        x_v = i["x"].rearrange("b (t p) d -> p (b t) d", p=P)
        c_v = i["ctx_512"].rearrange("b (t p) d -> p (b t) d", p=P)
        N_CTX, N_G, N_V, N_SIM, N_W1, N_W2, N_WR, N_KV = 0, 2, 3, 5, 9, 13, 17, 18

        with nc.Block() as block:
            @block.sync
            def _(sp):
                sp.dma_start(CT[:, :, :], c_v).then_inc(d_ctx, 16)
                sp.dma_start(wq[:, :], i["L0_xattn_Wq"]).then_inc(d_wqk, 16)
                sp.dma_start(wk[:, :], i["L0_xattn_Wk"]).then_inc(d_wqk, 16)
                for h in range(2):
                    sp.dma_start(g.X[:, 4 * h:4 * h + 4, :], x_v[:, 4 * h:4 * h + 4, :]).then_inc(d_x, 16)
                sp.dma_start(w1[:, :, :], i["L0_ffn_W1"].rearrange("(o p) n -> p o n", p=P)).then_inc(d_w1, 16)
                sp.dma_start(w2[:, :, :], i["L0_ffn_W2"].rearrange("(c p) n -> p c n", p=P)).then_inc(d_w2, 16)
                sp.dma_start(wr[:, :], i["L0_ffn_Wr"]).then_inc(d_wr, 16)
                sp.dma_start(g.br[:, :], i["L0_ffn_br"].partition_broadcast(P)).then_inc(g.d_br, 16)
                sp.dma_start(g.cosq[:, :, :], i["cosq"]).then_inc(g.d_ropeq, 16)
                sp.dma_start(g.sinq[:, :, :], i["sinq"]).then_inc(g.d_ropeq, 16)

            @block.gpsimd
            def _(pool):
                pool.memset(g.ident[:, :], 0.0).then_inc(id_zero, 1)
                pool.wait_ge(id_zero, 1)
                pool.affine_select(out=g.ident[:, :], in_=g.ident[:, :], compare_op=ALU.not_equal,
                                   fill=1.0, base=0, pattern=[[-1, P]],
                                   channel_multiplier=1).then_inc(id_ok, 1)
                pool.wait_ge(id_ok, 1)
                pool.tensor_copy(g.identb[:, :], g.ident[:, :]).then_inc(id_ok, 1)
                pool.memset(g.KD[:, :, :], 0.0).then_inc(kd_zero, 1)
                pool.wait_ge(d_ctx, 16)
                pool.wait_ge(d_rope, 32)
                lt = lambda x: x.rearrange("p (b l) d -> p b l d", l=2)
                tab = lambda x, a, z: x[:, :, a:z].unsqueeze(1).broadcast_to([P, B, 2, z - a])
                q = DC // 2
                pool.tensor_tensor(lt(kc), lt(CT), tab(ck, 0, DC), ALU.mult).then_inc(kv_mul, 1)
                pool.tensor_tensor(lt(ks)[:, :, :, 0:q], lt(CT)[:, :, :, q:DC], tab(sk, 0, q),
                                   ALU.mult).then_inc(kv_mul, 1)
                pool.tensor_tensor(lt(ks)[:, :, :, q:DC], lt(CT)[:, :, :, 0:q], tab(sk, q, DC),
                                   ALU.mult).then_inc(kv_mul, 1)
                pool.wait_ge(kv_mul, 3)
                pool.tensor_tensor(g.KV[:, :, 0, :], kc[:, :, :], ks[:, :, :], ALU.add).then_inc(kv_sum, 1)
                pool.wait_ge(kv_sum, 1)
                pool.tensor_copy(g.KV[:, :, 1, :], g.KV[:, :, 0, :]).then_inc(kv_ok, 1)

            @block.tensor
            def _(pe):
                n = 0

                def bank(n):
                    if n >= 4:
                        pe.wait_ge(emptied, n - 3)
                    return g.ps[:, n % 4, :]
                pe.wait_ge(id_ok, 2)
                pe.wait_ge(d_ctx, 16)
                for h in range(2):
                    for j in range(4):
                        mm = pe.transpose(bank(h)[0:DC, j * P:(j + 1) * P], CT[:, 4 * h + j, :], g.ident[:, :])
                    mm.then_inc(filled, 1)
                pe.wait_ge(d_wqk, 32)
                pe.matmul(bank(N_G)[0:DC, 0:DC], wk[:, :], wq[:, :], start=True, stop=True).then_inc(filled, 1)
                pe.wait_ge(emptied, N_G + 1)
                for h in range(2):
                    pe.matmul(bank(N_V + h)[0:DC, :], GT[:, :], CTT[:, 512 * h:512 * h + 512],
                              start=True, stop=True).then_inc(filled, 1)
                for b in range(B):
                    pe.wait_ge(emptied, N_V + b // 2 + 1)
                    o = bank(N_SIM + b)
                    for j in range(2):
                        mm = pe.matmul(o[:, S * j:S * j + S], CTT[:, (2 * b + j) * P:(2 * b + j + 1) * P],
                                       V[:, S * b:S * b + S], start=True, stop=True)
                    mm.then_inc(filled, 1)
                pe.wait_ge(d_w1, 16)
                for k in range(KT):
                    for h in range(2):
                        o = bank(N_W1 + 2 * k + h)
                        for j in range(4):
                            mm = pe.transpose(o[:, j * P:(j + 1) * P], w1[:, 4 * h + j, k * P:(k + 1) * P],
                                              g.ident[:, :])
                        mm.then_inc(filled, 1)
                pe.wait_ge(d_w2, 16)
                for q in range(4):
                    o = bank(N_W2 + q)
                    for j in range(2):
                        for c in range(KT):
                            mm = pe.transpose(o[:, (2 * j + c) * P:(2 * j + c + 1) * P],
                                              w2[:, c, (2 * q + j) * P:(2 * q + j + 1) * P], g.ident[:, :])
                    mm.then_inc(filled, 1)
                pe.wait_ge(d_wr, 16)
                o = bank(N_WR)
                for k in range(KT):
                    mm = pe.transpose(o[:, k * NBLK:(k + 1) * NBLK], wr[:, k * P:(k + 1) * P],
                                      g.ident[0:NBLK, 0:NBLK])
                mm.then_inc(filled, 1)
                pe.wait_ge(kv_ok, 1)
                for h in range(2):
                    o = bank(N_KV + h)
                    for j in range(4):
                        mm = pe.transpose(o[:, j * P:(j + 1) * P],
                                          g.KV[:, 4 * h + j, :, :].rearrange("p a d -> p (a d)"), g.ident[:, :])
                    mm.then_inc(filled, 1)
                for b in range(B):
                    pe.wait_ge(a_ok, 2 * b + 2)
                    for j in range(2):
                        for m in range(2):
                            mm = pe.transpose(g.ps[:, 4 + b, S * j + m * P:S * j + (m + 1) * P],
                                              A[:, 2 * b + m, j * P:(j + 1) * P], g.ident[:, :])
                    mm.then_inc(at_ps, 1)

            @block.scalar
            def _(act):
                nc.scalar.dma_start(ck[:, :, :], i["cosk"]).then_inc(d_rope, 16)
                nc.scalar.dma_start(sk[:, :, :], i["sink"]).then_inc(d_rope, 16)
                for n, (name, at) in enumerate([("g_xattn", 0), ("g_xattn", 1), ("g_ffn", 0), ("g_ffn", 1),
                                                ("L0_xattn_gamma_raw", 0)]):
                    act.dma_start(raw[:, n:n + 1], i[name][at:at + 1].partition_broadcast(P)).then_inc(d_raw, 16)

                def bank(n):
                    act.wait_ge(filled, n + 1)
                    return g.ps[:, n % 4, :]
                for h in range(2):
                    act.activation(CTT[:, 512 * h:512 * h + 512], bank(h)[0:DC, :], ACT.Copy).then_inc(emptied, 1)
                act.activation(GT[:, :], bank(N_G)[0:DC, 0:DC], ACT.Copy).then_inc(emptied, 1)
                for h in range(2):
                    act.activation(V[:, 512 * h:512 * h + 512], bank(N_V + h)[0:DC, :], ACT.Copy,
                                   scale=1.0 / 16.0).then_inc(emptied, 1)
                for b in range(B):
                    o = bank(N_SIM + b)
                    act.activation(SIM[:, 2 * b:2 * b + 2, :], o, ACT.Copy).then_inc(sim_ok, 1)
                    act.activation(SIG[:, 2 * b:2 * b + 2, :], o, ACT.Sigmoid).then_inc(emptied, 1)
                act.wait_ge(d_raw, 80)
                act.activation(g.gate[:, 0:4], raw[:, 0:4], ACT.Tanh).then_inc(tanh_ok, 1)
                act.activation(gam[:, 0:1], raw[:, 4:5], ACT.Sigmoid).then_inc(tanh_ok, 1)
                layernorm_scalar(act, g)
                for k in range(KT):
                    for h in range(2):
                        act.activation(g.W1T[:, k, 512 * h:512 * h + 512], bank(N_W1 + 2 * k + h),
                                       ACT.Copy).then_inc(emptied, 1)
                for q in range(4):
                    act.activation(g.W2T[:, 2 * q:2 * q + 2, :], bank(N_W2 + q), ACT.Copy).then_inc(emptied, 1)
                act.activation(g.WrT[:, :, :], bank(N_WR)[:, 0:KT * NBLK], ACT.Copy).then_inc(emptied, 1)
                act.wait_ge(kd_zero, 1)
                for h in range(2):
                    o = bank(N_KV + h)
                    act.activation(g.KD[0:DC, 2 * h:2 * h + 2, 0:S], o[0:DC, :], ACT.Copy, scale=-1.0)
                    act.activation(g.KD[DC:P, 2 * h:2 * h + 2, S:2 * S], o[DC:P, :], ACT.Copy,
                                   scale=-1.0).then_inc(emptied, 1)

            @block.vector
            def _(dve):
                def ready(t):
                    if t % 4 == 0:
                        dve.wait_ge(d_x, 16 * (t // 4 + 1))
                    if t == 0:
                        dve.wait_ge(d_x, 32)
                layernorm_vector(dve, g, ready)
                dve.wait_ge(tanh_ok, 2)
                dve.tensor_scalar(gam[:, 1:2], gam[:, 0:1], -1.0, 1.0, ALU.mult, ALU.add).then_inc(gam_ok, 1)
                dve.tensor_scalar(gam[:, 3:4], gam[:, 0:1], g.gate[:, 0:1], 0.5, ALU.mult,
                                  ALU.mult).then_inc(gam_ok, 1)
                dve.wait_ge(gam_ok, 2)
                dve.tensor_scalar(gam[:, 2:3], gam[:, 1:2], g.gate[:, 0:1], None, ALU.mult).then_inc(gam_ok, 1)
                dve.wait_ge(gam_ok, 3)
                for t in range(NT):
                    dve.scalar_tensor_tensor(out=XA[:, t, :], in0=g.XN[:, t, :], scalar=gam[:, 2:3],
                                             in1=g.X[:, t, :], op0=ALU.mult, op1=ALU.add).then_inc(xa_ok, 1)
                for b in range(B):
                    dve.wait_ge(sim_ok, b + 1)
                    for r in range(ROUNDS):
                        for j in range(2):
                            n = b * ROUNDS * 2 + 2 * r + j
                            if r > 0:
                                dve.wait_ge(rep_ok, b * (ROUNDS - 1) * 2 + 2 * (r - 1) + j + 1)
                            src = SIM[:, 2 * b + j, :] if r == 0 else work[:, j, :]
                            dve.max(m8[:, j, r, :], src).then_inc(max_ok, 1)
                        if r == ROUNDS - 1:
                            break
                        for j in range(2):
                            dve.wait_ge(max_ok, b * ROUNDS * 2 + 2 * r + j + 1)
                            src = SIM[:, 2 * b + j, :] if r == 0 else work[:, j, :]
                            dve.match_replace(work[:, j, :], m8[:, j, r, :], src, NEG).then_inc(rep_ok, 1)
                    last = (TOP_ADJ - 1) % 8
                    for j in range(2):
                        t = 2 * b + j
                        dve.wait_ge(max_ok, (b + 1) * ROUNDS * 2 - 1 + j)
                        if j == 0:
                            dve.wait_ge(emptied, N_SIM + b + 1)
                        dve.scalar_tensor_tensor(out=A[:, t, :], in0=SIM[:, t, :],
                                                 scalar=m8[:, j, ROUNDS - 1, last:last + 1],
                                                 in1=SIG[:, t, :], op0=ALU.is_ge, op1=ALU.mult).then_inc(a_ok, 1)
                dve.wait_ge(xa_ok, NT)
                for b in range(B):
                    dve.wait_ge(at_ps, b + 1)
                    dve.wait_ge(a_ok, 2 * b + 2)
                    for j in range(2):
                        t = 2 * b + j
                        dve.tensor_tensor(A[:, t, :], A[:, t, :], g.ps[:, 4 + b, S * j:S * j + S],
                                          ALU.add).then_inc(mix_ok, 1)
                for t in range(NT):
                    dve.wait_ge(mix_ok, t + 1)
                    dve.scalar_tensor_tensor(out=g.X[:, t, :], in0=A[:, t, :], scalar=gam[:, 3:4],
                                             in1=XA[:, t, :], op0=ALU.mult, op1=ALU.add).then_inc(x_ok, 1)
    g.ln_base = 1


def stage_block_ffn(nc, g, i):
    with ExitStack() as ctx:
        sb = lambda name, shape, dt=F32: ctx.enter_context(nc.sbuf_tensor(name, shape, dt))
        sem = lambda name: ctx.enter_context(nc.semaphore(name))
        FILL = 8 - TOP_BLK
        LG = sb("LG", [P, NT, FILL + NBLK])
        RP = sb("RP", [P, NT, FILL + NBLK])
        M8 = sb("M8", [P, NT, 8])
        MK = sb("MK", [P, NT, NBLK], BF16)
        HT = sb("HT", [P, HID // P, T])
        (lg_fill, lg_ps, lg_ok, top_ok, rep_ok, mk_ok, h_ps, gelu_ok, mask_ps, ht_ok, y_ps) = map(
            sem, ["lg_fill", "lg_ps", "lg_ok", "top_ok", "rep_ok1", "mk_ok", "h_ps", "gelu_ok", "mask_ps",
                  "ht_ok", "y_ps"])
        HB = [4, 5]
        MB = [6, 7]
        steps = [(h, o) for h in range(2) for o in range(HID // P)]

        with nc.Block() as block:
            @block.gpsimd
            def _(pool):
                pool.memset(LG[:, :, 0:FILL], BIG).then_inc(lg_fill, 1)

            def mask(pe, n):
                h, o = steps[n]
                pe.wait_ge(mk_ok, 1)
                if n >= 2:
                    pe.wait_ge(ht_ok, n - 1)
                for j in range(4):
                    for c in range(2):
                        pick = MK[:, 4 * h + j, 2 * o + c:2 * o + c + 1].broadcast_to([P, BLK])
                        mm = pe.matmul(g.ps[BLK * c:BLK * c + BLK, MB[n % 2], j * P:(j + 1) * P], pick,
                                       g.identb[:, :], start=True, stop=True)
                mm.then_inc(mask_ps, 1)

            @block.tensor
            def _(pe):
                transpose_xn_tensor(pe, g)
                for n, (h, o) in enumerate(steps):
                    if n == 0:
                        pe.wait_ge(g.xt, 4 * (g.ln_base - 1) + 4)
                        for t in range(NT):
                            for k in range(KT):
                                mm = pe.matmul(g.ps[:, 0, t * NBLK:(t + 1) * NBLK], g.XT[:, k, t * P:(t + 1) * P],
                                               g.WrT[:, k, :], start=(k == 0), stop=(k == KT - 1))
                        mm.then_inc(lg_ps, 1)
                    if n >= 2:
                        pe.wait_ge(gelu_ok, n - 1)
                    for k in range(KT):
                        mm = pe.matmul(g.ps[:, HB[n % 2], :], g.W1T[:, k, o * P:(o + 1) * P],
                                       g.XT[:, k, 512 * h:512 * h + 512], start=(k == 0), stop=(k == KT - 1))
                    mm.then_inc(h_ps, 1)
                    if n >= 1:
                        mask(pe, n - 1)
                mask(pe, len(steps) - 1)
                for t in range(NT):
                    if t % 4 == 0:
                        pe.wait_ge(ht_ok, 8 * (t // 4 + 1))
                    if t >= 4:
                        pe.wait_ge(g.x_done, t - 3)
                    y = g.ps[:, t % 4, 0:D]
                    for o in range(HID // P):
                        mm = pe.matmul(y, HT[:, o, t * P:(t + 1) * P], g.W2T[:, o, :],
                                       start=(o == 0), stop=(o == HID // P - 1))
                    mm.then_inc(y_ps, 1)

            @block.scalar
            def _(act):
                layernorm_scalar(act, g)
                transpose_xn_scalar(act, g)
                for n, (h, o) in enumerate(steps):
                    act.wait_ge(h_ps, n + 1)
                    act.activation(HT[:, o, 512 * h:512 * h + 512], g.ps[:, HB[n % 2], :],
                                   ACT.Gelu).then_inc(gelu_ok, 1)

            @block.vector
            def _(dve):
                layernorm_vector(dve, g, lambda t: None)
                dve.wait_ge(lg_ps, 1)
                dve.wait_ge(g.d_br, 16)
                dve.wait_ge(lg_fill, 1)
                dve.tensor_tensor(LG[:, :, FILL:], g.ps[:, 0, 0:NT * NBLK].rearrange("p (t n) -> p t n", t=NT),
                                  g.br[:, :].unsqueeze(1).broadcast_to([P, NT, NBLK]), ALU.add).then_inc(lg_ok, 1)
                dve.wait_ge(lg_ok, 1)
                for t in range(NT):
                    dve.max(M8[:, t, :], LG[:, t, :]).then_inc(top_ok, 1)
                for t in range(NT):
                    dve.wait_ge(top_ok, t + 1)
                    dve.match_replace(RP[:, t, :], M8[:, t, :], LG[:, t, :], NEG).then_inc(rep_ok, 1)
                dve.wait_ge(rep_ok, NT)
                dve.tensor_tensor(MK[:, :, :], LG[:, :, FILL:], RP[:, :, FILL:], ALU.not_equal).then_inc(mk_ok, 1)
                for n, (h, o) in enumerate(steps):
                    dve.wait_ge(gelu_ok, n + 1)
                    dve.wait_ge(mask_ps, n + 1)
                    rows = HT[:, o, 512 * h:512 * h + 512]
                    dve.tensor_tensor(rows, rows, g.ps[:, MB[n % 2], :], ALU.mult).then_inc(ht_ok, 1)
                for t in range(NT):
                    dve.wait_ge(y_ps, t + 1)
                    dve.scalar_tensor_tensor(out=g.X[:, t, :], in0=g.ps[:, t % 4, 0:D],
                                             scalar=g.gate[:, 2:3], in1=g.X[:, t, :], op0=ALU.mult,
                                             op1=ALU.add).then_inc(g.x_done, 1)

    g.ln_base = 2

def stage_latent_attention(nc, g, i):
    with ExitStack() as ctx:
        sb = lambda name, shape, dt=F32: ctx.enter_context(nc.sbuf_tensor(name, shape, dt))
        sem = lambda name: ctx.enter_context(nc.semaphore(name))
        two = lambda name, shape: [sb(f"{name}{u}", shape) for u in range(2)]
        WQ = two("WQ", [P, 2, D])
        WCQ = two("WCQ", [P, 2, DQ])
        WCV = two("WCV", [P, 2, DC])
        WQR = two("WQR", [HALF, 2, 2, R])
        WKR = two("WKR", [DC, 2, R])
        WO = two("WO", [P, KT, 2 * HK])
        RT = sb("RT", [R, 2, 2 * HALF + DC])
        WOT = sb("WOT", [P, 2, D])
        C = two("C", [P, KT, 2 * DQ])
        M = two("M", [HALF, 4, DC])
        N = sb("N", [P, PAIRS, D])
        TM = two("TM", [HALF, 4, 512])
        RO = sb("RO", [HALF, 2, 2, 2, 512])
        QT = two("QT", [P, T])
        low = sb("low", [P, 2, 2])
        PB = two("PB", [P, 2, S])
        tot = sb("tot", [P, 2, 2])
        inv = sb("inv", [P, 2, 2])
        PTS = two("PTS", [P, 4, 2 * P])
        CX = sb("CX", [P, PAIRS, T])
        QA, QP, SC, PTB, CXB, FO = 0, 2, 3, 5, 6, 7

        d_w = [sem("d_w0"), sem("d_w1_")]
        DW = 7 * 16
        (q_ps, rope_ok, sum_ok, qc_ps, qc_ok, s_ps, low_ok, exp_ok, inv_ok, norm_ok, t_ps, t_ok, cx_ps, cx_ok,
         fold_ps, fold_ok, out_ps, credit) = map(sem, [
             "q_ps", "rope_ok", "sum_ok", "qc_ps", "qc_ok", "s_ps", "low_ok", "exp_ok", "inv_ok", "norm_ok",
             "t_ps", "t_ok", "cx_ps", "cx_ok", "fold_ps", "fold_ok", "out_ps", "credit"])
        EXP0, ROPE0, TPS0, TOK0, CXPS0, CXOK0, QC0, QCPS0, SUM0, FOLD0 = 2, 2, 2, 1, 2, 1, 1, 2, 4, 1
        starts = [(exp_ok, EXP0), (rope_ok, ROPE0), (t_ps, TPS0), (t_ok, TOK0), (cx_ps, CXPS0), (cx_ok, CXOK0),
                  (qc_ok, QC0), (qc_ps, QCPS0), (sum_ok, SUM0), (fold_ok, FOLD0)]

        def pairs(eng, body):
            with eng.Fori(0, (PAIRS - 2) // 2, 1) as it:
                for u in range(2):
                    body(it * 2 + u, u, True, True)
            body(PAIRS - 2, 0, False, True)
            body(PAIRS - 1, 1, False, False)

        wq_v = i["L1_xattn_Wq"].rearrange("(h k) n -> k h n", k=HK)
        wcq_v = i["L1_xattn_w_kc_q"].rearrange("h k q -> k h q")
        wcv_v = i["L1_xattn_w_kc_kv"].rearrange("h k d -> k h d")
        wqr_v = i["L1_xattn_W_qr"].rearrange("h (a j) r -> j h a r", a=2)
        wkr_v = i["L1_xattn_W_kr"].rearrange("h d r -> d h r")
        wo_v = i["L1_xattn_Wo"].rearrange("(c p) n -> p c n", p=P)

        def load_pair(sp, r, u):
            two_heads = bass.ds(2 * r, 2)
            sp.dma_start(WQ[u][:, :, :], wq_v[:, two_heads, :]).then_inc(d_w[u], 16)
            sp.dma_start(WCQ[u][:, :, :], wcq_v[:, two_heads, :]).then_inc(d_w[u], 16)
            sp.dma_start(WCV[u][:, :, :], wcv_v[:, two_heads, :]).then_inc(d_w[u], 16)
            for h in range(2):
                sp.dma_start(WQR[u][:, h, :, :], wqr_v[:, bass.ds(2 * r + h, 1), :, :]).then_inc(d_w[u], 16)
            sp.dma_start(WKR[u][:, :, :], wkr_v[:, two_heads, :]).then_inc(d_w[u], 16)
            sp.dma_start(WO[u][:, :, :], wo_v[:, :, bass.ds(2 * HK * r, 2 * HK)]).then_inc(d_w[u], 16)

        with nc.Block() as block:
            @block.sync
            def _(sp):
                load_pair(sp, 0, 0)
                load_pair(sp, 1, 1)
                with sp.Fori(0, PAIRS // 2 - 1, 1) as it:
                    for u in range(2):
                        r = it * 2 + (2 + u)
                        sp.wait_ge(fold_ps, it * 12 + 6 * (u + 1))
                        load_pair(sp, r, u)

            @block.tensor
            def _(pe):
                def fold(r, u, f):
                    pe.wait_ge(fold_ok, 6 * r + (f + FOLD0))
                    o = g.ps[:, FO, :]
                    if f == 0:
                        pe.wait_ge(d_w[u], (r + (2 - u)) * (DW // 2))
                    if f < 2:
                        for h in range(2):
                            mm = pe.matmul(o[:, h * DQ:(h + 1) * DQ], WQ[u][:, h, f * P:(f + 1) * P],
                                           WCQ[u][:, h, :], start=True, stop=True)
                    elif f == 2:
                        for h in range(2):
                            pe.transpose(o[:, h * HALF:(h + 1) * HALF],
                                         WQR[u][:, h, :, :].rearrange("j a r -> j (a r)"),
                                         g.ident[0:HALF, 0:HALF])
                        mm = pe.transpose(o[:, 2 * HALF:2 * HALF + DC],
                                          WKR[u][:, :, :].rearrange("d h r -> d (h r)"), g.ident[0:DC, 0:DC])
                    elif f == 3:
                        for h in range(2):
                            for c in range(KT):
                                mm = pe.transpose(o[:, h * D + c * P:h * D + (c + 1) * P],
                                                  WO[u][:, c, h * HK:(h + 1) * HK], g.ident[:, :])
                    elif f == 4:
                        for h in range(2):
                            for a in range(2):
                                mm = pe.matmul(o[0:HALF, (2 * h + a) * DC:(2 * h + a + 1) * DC],
                                               RT[:, a, h * HALF:(h + 1) * HALF],
                                               RT[:, h, 2 * HALF:2 * HALF + DC],
                                               start=True, stop=True)
                    else:
                        for h in range(2):
                            mm = pe.matmul(o[DC * h:DC * h + DC, 0:D], WCV[u][:, h, :], WOT[:, h, :],
                                           start=True, stop=True)
                    mm.then_inc(fold_ps, 1)

                def queries(q, u, t):
                    n, h, a = t // 4, t // 2 % 2, t % 2
                    pe.wait_ge(rope_ok, 8 * q + (t - 1 + ROPE0))
                    pe.wait_ge(fold_ok, 6 * q + (2 + FOLD0))
                    for k in range(KT):
                        mm = pe.matmul(g.ps[0:HALF, QA + a, :],
                                       C[u][:, k, h * DQ + a * HALF:h * DQ + (a + 1) * HALF],
                                       g.XT[:, k, 512 * n:512 * n + 512], start=(k == 0), stop=(k == KT - 1))
                    mm.then_inc(q_ps, 1)

                def to_context(q, u, n):
                    pe.wait_ge(sum_ok, 8 * q + (4 * n + 4 + SUM0))
                    pe.wait_ge(fold_ok, 6 * q + (5 + FOLD0))
                    pe.wait_ge(qc_ok, 2 * q + (n + QC0))
                    for a in range(2):
                        for h in range(2):
                            mm = pe.matmul(g.ps[DC * h:DC * h + DC, QP, :], M[u][:, 2 * h + a, :],
                                           RO[:, n, h, a, :], start=(a == 0), stop=(a == 1))
                    mm.then_inc(qc_ps, 1)

                def scores(p, u, t):
                    pe.wait_ge(qc_ok, 2 * p + (t // 4 + 1 + QC0))
                    pe.wait_ge(exp_ok, 8 * p + (t - 1 + EXP0))
                    pe.matmul(g.ps[:, SC + t % 2, :], QT[u][:, t * P:(t + 1) * P], g.KD[:, t // 2, :],
                              start=True, stop=True).then_inc(s_ps, 1)

                def turn(p, t):
                    pe.wait_ge(norm_ok, 8 * p + (t + 1))
                    pe.wait_ge(t_ok, 8 * p + (t + TOK0))
                    for j in range(4):
                        mm = pe.transpose(g.ps[:, PTB, j * P:(j + 1) * P],
                                          PB[t % 2][:, j // 2, (j % 2) * P:(j % 2 + 1) * P], g.ident[:, :])
                    mm.then_inc(t_ps, 1)

                def attend(p, b):
                    pe.wait_ge(t_ok, 8 * p + (2 * b + 2 + TOK0))
                    pe.wait_ge(cx_ok, 4 * p + (b + CXOK0))
                    for j in range(2):
                        for h in range(2):
                            mm = pe.matmul(g.ps[DC * h:DC * h + DC, CXB, 0:S], g.KV[:, 2 * b + j, 0, :],
                                           PTS[b % 2][:, 2 * h + j, :], start=(j == 0), stop=(j == 1))
                    mm.then_inc(cx_ps, 1)

                def pair(p, u, folds, asks):
                    for t in range(NT):
                        scores(p, u, t)
                        if asks:
                            queries(p + 1, 1 - u, t)
                        if t == 1:
                            to_context(p, u, 1)
                        if folds and t < 6:
                            fold(p + 2, u, t)
                        if t >= 1:
                            turn(p, t - 1)
                        if t in (3, 5, 7):
                            attend(p, t // 2 - 1)
                    if asks:
                        to_context(p + 1, 1 - u, 0)
                    turn(p, NT - 1)
                    attend(p, B - 1)

                pe.wait_ge(credit, 1)
                for r in range(2):
                    for f in range(6):
                        fold(r, r, f)
                transpose_xn_tensor(pe, g)
                pe.wait_ge(g.xt, 4 * g.ln_base)
                for t in range(NT):
                    queries(0, 0, t)
                to_context(0, 0, 0)
                pairs(pe, pair)
                for t in range(NT):
                    if t == 0:
                        pe.wait_ge(cx_ok, 4 * PAIRS + CXOK0)
                    if t >= 4:
                        pe.wait_ge(g.x_done, NT + t - 3)
                    for p in range(PAIRS):
                        mm = pe.matmul(g.ps[:, t % 4, 0:D], CX[:, p, t * P:(t + 1) * P], N[:, p, :],
                                       start=(p == 0), stop=(p == PAIRS - 1))
                    mm.then_inc(out_ps, 1)

            @block.scalar
            def _(act):
                def fold(r, u, f):
                    act.wait_ge(fold_ps, 6 * r + (f + 1))
                    o = g.ps[:, FO, :]
                    if f < 2:
                        act.activation(C[u][:, f, :], o[:, 0:2 * DQ], ACT.Copy).then_inc(fold_ok, 1)
                    elif f == 2:
                        act.activation(RT[:, 0, :], o[0:R, 0:2 * HALF + DC], ACT.Copy)
                        act.activation(RT[:, 1, :], o[R:P, 0:2 * HALF + DC], ACT.Copy).then_inc(fold_ok, 1)
                    elif f == 3:
                        act.activation(WOT[:, :, :], o, ACT.Copy).then_inc(fold_ok, 1)
                    elif f == 4:
                        act.activation(M[u][:, :, :], o[0:HALF, 0:4 * DC], ACT.Copy).then_inc(fold_ok, 1)
                    else:
                        act.activation(N[:, bass.ds(r, 1), :], o[:, 0:D], ACT.Copy).then_inc(fold_ok, 1)

                def to_context(q, u, n):
                    act.wait_ge(qc_ps, 2 * q + (n + 1 + QCPS0))
                    act.activation(QT[u][:, 512 * n:512 * n + 512], g.ps[:, QP, :], ACT.Copy).then_inc(qc_ok, 1)

                def softmax(p, t):
                    act.wait_ge(low_ok, 8 * p + (t + 1))
                    act.wait_ge(t_ps, 8 * p + (t - 1 + TPS0))
                    for h in range(2):
                        e = act.activation(PB[t % 2][:, h, :], g.ps[:, SC + t % 2, h * S:(h + 1) * S], ACT.Exp,
                                           bias=low[:, t % 2, h:h + 1], scale=-1.0,
                                           accum_out=tot[:, t % 2, h:h + 1])
                    e.then_inc(exp_ok, 1)

                def turned(p, t):
                    act.wait_ge(t_ps, 8 * p + (t + 1 + TPS0))
                    act.wait_ge(cx_ps, 4 * p + (t // 2 - 1 + CXPS0))
                    act.activation(PTS[t // 2 % 2][:, :, (t % 2) * P:(t % 2 + 1) * P],
                                   g.ps[:, PTB, :].rearrange("p (j n) -> p j n", j=4),
                                   ACT.Copy).then_inc(t_ok, 1)

                def attended(p, b):
                    act.wait_ge(cx_ps, 4 * p + (b + 1 + CXPS0))
                    act.activation(CX[:, bass.ds(p, 1), S * b:S * b + S], g.ps[:, CXB, 0:S],
                                   ACT.Copy).then_inc(cx_ok, 1)

                def pair(p, u, folds, asks):
                    for t in range(NT):
                        softmax(p, t)
                        if t == 1:
                            to_context(p, u, 1)
                        if folds and t < 6:
                            fold(p + 2, u, t)
                        if t >= 1:
                            turned(p, t - 1)
                        if t in (3, 5, 7):
                            attended(p, t // 2 - 1)
                    if asks:
                        to_context(p + 1, 1 - u, 0)
                    turned(p, NT - 1)
                    attended(p, B - 1)

                act.wait_ge(credit, 1)
                for r in range(2):
                    for f in range(6):
                        fold(r, r, f)
                layernorm_scalar(act, g)
                transpose_xn_scalar(act, g)
                to_context(0, 0, 0)
                pairs(act, pair)

            @block.gpsimd
            def _(pool):
                for s, v in starts:
                    pool.sem_inc(s, v)
                pool.sem_inc(credit, 2)
                with pool.Fori(0, PAIRS, 1) as q:
                    for st in range(4):
                        n, h, tm = st // 2, st % 2, TM[st % 2]
                        pool.wait_ge(rope_ok, 8 * q + (2 * st + 2 + ROPE0))
                        pool.wait_ge(qc_ps, 2 * q + (n + QCPS0 - 1))
                        pool.tensor_tensor(RO[:, n, h, 0, :], tm[:, 0, :], tm[:, 2, :],
                                           ALU.subtract).then_inc(sum_ok, 1)
                        pool.tensor_tensor(RO[:, n, h, 1, :], tm[:, 3, :], tm[:, 1, :],
                                           ALU.add).then_inc(sum_ok, 1)

            @block.vector
            def _(dve):
                def rotate(q, t):
                    st, a = t // 2, t % 2
                    dve.wait_ge(q_ps, 8 * q + (t + 1))
                    dve.wait_ge(sum_ok, 8 * q + (2 * st - 2 + SUM0))
                    batches = lambda x: x.rearrange("p (b s) -> p b s", b=2)
                    over = lambda x: x.unsqueeze(1).broadcast_to([HALF, 2, S])
                    src = batches(g.ps[0:HALF, QA + a, :])
                    c, s = (0, 1) if a == 0 else (3, 2)
                    dve.tensor_tensor(batches(TM[st % 2][:, c, :]), src, over(g.cosq[:, a, :]), ALU.mult)
                    dve.tensor_tensor(batches(TM[st % 2][:, s, :]), src, over(g.sinq[:, 1 - a, :]),
                                      ALU.mult).then_inc(rope_ok, 1)

                def pair(p, u, folds, asks):
                    for t in range(NT):
                        dve.wait_ge(s_ps, 8 * p + (t + 1))
                        dve.tensor_reduce(low[:, t % 2, :], g.ps[:, SC + t % 2, :].rearrange("p (h s) -> p h s", h=2),
                                          AX.X, ALU.min).then_inc(low_ok, 1)
                        if asks:
                            rotate(p + 1, t)
                        dve.wait_ge(exp_ok, 8 * p + (t + 1 + EXP0))
                        dve.reciprocal(inv[:, t % 2, :], tot[:, t % 2, :]).then_inc(inv_ok, 1)
                        dve.wait_ge(inv_ok, 8 * p + (t + 1))
                        for h in range(2):
                            m = dve.tensor_scalar(PB[t % 2][:, h, :], PB[t % 2][:, h, :],
                                                  inv[:, t % 2, h:h + 1], None, ALU.mult)
                        m.then_inc(norm_ok, 1)

                layernorm_vector(dve, g, lambda t: None)
                dve.wait_ge(credit, 1)
                dve.wait_ge(g.d_ropeq, 32)
                for t in range(NT):
                    rotate(0, t)
                pairs(dve, pair)
                for t in range(NT):
                    dve.wait_ge(out_ps, t + 1)
                    dve.scalar_tensor_tensor(out=g.X[:, t, :], in0=g.ps[:, t % 4, 0:D], scalar=g.gate[:, 1:2],
                                             in1=g.X[:, t, :], op0=ALU.mult, op1=ALU.add).then_inc(g.x_done, 1)
    g.ln_base = 3


def stage_moe(nc, g, i, out):
    with ExitStack() as ctx:
        sb = lambda name, shape, dt=F32: ctx.enter_context(nc.sbuf_tensor(name, shape, dt))
        sem = lambda name: ctx.enter_context(nc.semaphore(name))
        RING = 5
        GF, EF = 8 - TOP_G, 8 - TOP_E
        EP = ST_T * EPT
        shw = sb("shw", [P, 3, KT, SHARED])
        shT = sb("shT", [P, 3, KT, SHARED])
        rw = sb("rw", [E, D])
        rwT = sb("rwT", [P, KT, E])
        eb = sb("eb", [P, E])
        EG = [sb(f"EG{n}", [P, EPT, KT, EI]) for n in range(RING)]
        EU = [sb(f"EU{n}", [P, EPT, KT, EI]) for n in range(RING)]
        ED = [sb(f"ED{n}", [P, EPT, D]) for n in range(RING)]
        XP = sb("XP", [P, 3, NT, D], BF16)
        SG = sb("SG", [P, NT, E])
        SBI = sb("SBI", [P, NT, E])
        hl = sb("hl", [P, 2, NT * GROUPS, 2])
        tp = sb("tp", [P, 4, NT * GROUPS])
        GB = sb("GB", [P, NT, GF + GROUPS])
        GR = sb("GR", [P, NT, GF + GROUPS])
        g8 = sb("g8", [P, NT, 8])
        gm = sb("gm", [P, NT, GROUPS])
        mz = sb("mz", [P, NT, E])
        MB = sb("MB", [P, NT, EF + E])
        MR = sb("MR", [P, NT, EF + E])
        e8 = sb("e8", [P, NT, 8])
        MK = sb("MKE", [P, NT, E])
        MKb = sb("MKb", [P, NT, E], BF16)
        wsel = sb("wsel", [P, NT, E])
        wsum = sb("wsum", [P, 3, NT])
        W = sb("W", [P, NT, E])
        WR_ = sb("WR_", [P, NT, E])
        WP = sb("WP", [P, NT, 3, EP], BF16)
        place = sb("place", [P, NT, E])
        ioti = sb("ioti", [P, CAP], mybir.dt.int32)
        iotf = sb("iotf", [P, CAP])
        tri = sb("tri", [P, P], BF16)
        ones = sb("ones", [P, P], BF16)
        own = sb("own", [P, EPT])
        SM = sb("SM", [P, NT, E * CAP], BF16)
        STT = sb("STT", [P, ST_T, T], BF16)
        ws = sb("ws", [P, ST_T, 3, EPT])
        wslot = sb("wslot", [P, ST_T])
        XG = sb("XG", [P, KT, E * CAP])
        SL = [sb(f"SL{u}", [P, 512]) for u in range(2)]
        HS = sb("HS", [P, KT, T])
        SE = [sb(f"SE{u}", [P, SLOTS]) for u in range(2)]
        HP = [sb(f"HP{u}", [P, EPT, SLOTS + CAP]) for u in range(2)]
        YW = [sb(f"YW{u}", [P, D]) for u in range(2)]
        YR = [sb(f"YR{u}", [P, D]) for u in range(2)]
        YP = sb("YP", [P, ST_T, 3, D], BF16)
        XR = YP[:, :, :, :].rearrange("p n a d -> p (n a d)")[:, 0:2 * NT * D].bitcast(F32).rearrange(
            "p (t d) -> p t d", t=NT)

        count = lambda n: min(EPT, E - EPT * n)
        d_sh, d_r, d_eb, stored = map(sem, ["d_sh", "d_r", "d_eb", "stored"])
        d_e = [sem(f"d_e{n}") for n in range(RING)]
        (c_fill, iota_ok, iotf_ok, tri0, tri_ok, own_ok, filled, emptied, rl_ps, sg_ok, gu_sh, sl_ok, hs_ok) = map(
            sem, ["c_fill", "iota_ok", "iotf_ok", "tri0", "tri_ok", "own_ok", "filled2", "emptied2", "rl_ps",
                  "sg_ok", "gu_sh", "sl_ok", "hs_ok"])
        (rt, mk_ok, w_ok, wp_a, wp_r, wp_b, cnt_ps, place_ok, s_ok, xp_a, xp_r, xp_b, xp_c, xg_ps, xg_ok, ws_ps,
         ws_ok) = map(
            sem, ["rt", "mk_ok2", "w_ok", "wp_a", "wp_r", "wp_b", "cnt_ps", "place_ok", "s_ok", "xp_a", "xp_r",
                  "xp_b", "xp_c", "xg_ps", "xg_ok", "ws_ps", "ws_ok"])
        (gu_ps, se_ok, hp_ok, st_ps, st_ok, y_ps, yw_ok, yh_ok, yr_ok, ym_ok, yl_ok, acc_ps, fin_ok, hp0) = map(
            sem, ["gu_ps", "se_ok", "hp_ok", "st_ps", "st_ok", "y_ps2", "yw_ok", "yh_ok", "yr_ok", "ym_ok", "yl_ok",
                  "acc_ps", "fin_ok", "hp0"])

        chunks = [(0, 11 * CAP), (11 * CAP, 22 * CAP), (22 * CAP, E * CAP)]
        gathers = [(k, c) for k in range(KT) for c in range(3)]
        GBANK = [0, 1, 2, 3, 6, 7]
        GU, Y, STB, ACC = 0, 2, 6, 4
        shared_steps = [(h, o) for h in range(2) for o in range(KT)]
        out_v = out.rearrange("b (t p) d -> p (b t) d", p=P)

        with nc.Block() as block:
            @block.sync
            def _(sp):
                for n, name in enumerate(["L1_ffn_shared_gate", "L1_ffn_shared_up", "L1_ffn_shared_down"]):
                    sp.dma_start(shw[:, n, :, :], i[name].rearrange("(c p) n -> p c n", p=P)).then_inc(d_sh, 16)
                sp.dma_start(rw[:, :], i["L1_ffn_router_w"]).then_inc(d_r, 16)
                sp.dma_start(eb[:, :], i["L1_ffn_e_bias"].partition_broadcast(P)).then_inc(d_eb, 16)
                for n in range(ST_T):
                    c, r = count(n), n % RING
                    if n >= RING:
                        sp.wait_ge(y_ps, n - RING + 1)
                    es = slice(EPT * n, EPT * n + c)
                    sp.dma_start(EG[r][:, 0:c], i["L1_ffn_W_gate"][es].rearrange("e (k p) n -> p e k n", p=P)
                                 ).then_inc(d_e[r], 16)
                    sp.dma_start(EU[r][:, 0:c], i["L1_ffn_W_up"][es].rearrange("e (k p) n -> p e k n", p=P)
                                 ).then_inc(d_e[r], 16)
                    sp.dma_start(ED[r][:, 0:c], i["L1_ffn_W_down"][es].rearrange("e p n -> p e n")
                                 ).then_inc(d_e[r], 16)
                for b in range(B):
                    sp.wait_ge(fin_ok, 2 * b + 2)
                    sp.dma_start(out_v[:, 2 * b:2 * b + 2, :], g.X[:, 2 * b:2 * b + 2, :]).then_inc(stored, 16)
                sp.wait_ge(stored, 16 * B)

            @block.gpsimd
            def _(pool):
                pool.memset(GB[:, :, 0:GF], BIG).then_inc(c_fill, 1)
                pool.memset(MB[:, :, 0:EF], BIG).then_inc(c_fill, 1)
                pool.memset(WP[:, :, :, E:EP], 0.0).then_inc(c_fill, 1)
                pool.iota(ioti[:, :], [[1, CAP]], base=1, channel_multiplier=0).then_inc(iota_ok, 1)
                pool.memset(ones[:, :], 1.0).then_inc(tri0, 1)
                pool.memset(tri[:, :], 1.0).then_inc(tri0, 1)
                pool.wait_ge(iota_ok, 1)
                pool.tensor_copy(iotf[:, :], ioti[:, :]).then_inc(iotf_ok, 1)
                pool.wait_ge(tri0, 2)
                pool.affine_select(out=tri[:, :], in_=tri[:, :], compare_op=ALU.is_gt, fill=0.0, base=0,
                                   pattern=[[1, P]], channel_multiplier=-1).then_inc(tri_ok, 1)
                for u in range(2):
                    pool.memset(HP[u][:, :, :], 0.0).then_inc(hp0, 1)
                for h in range(2):
                    t = slice(4 * h, 4 * h + 4)
                    pool.wait_ge(xp_a, h + 1)
                    pool.tensor_tensor(XR[:, t, :], g.XN[:, t, :], XP[:, 0, t, :], ALU.subtract).then_inc(xp_r, 1)
                for h in range(2):
                    t = slice(4 * h, 4 * h + 4)
                    pool.wait_ge(xp_b, h + 1)
                    pool.tensor_tensor(XP[:, 2, t, :], XR[:, t, :], XP[:, 1, t, :], ALU.subtract).then_inc(xp_c, 1)
                pool.wait_ge(wp_a, 1)
                pool.tensor_tensor(WR_[:, :, :], W[:, :, :], WP[:, :, 0, 0:E], ALU.subtract).then_inc(wp_r, 1)
                pool.wait_ge(wp_b, 1)
                pool.tensor_tensor(WP[:, :, 2, 0:E], WR_[:, :, :], WP[:, :, 1, 0:E], ALU.subtract).then_inc(wp_b, 1)
                for n in range(ST_T):
                    m = CAP * count(n)
                    pool.wait_ge(yh_ok, n + 1)
                    if n >= 2:
                        pool.wait_ge(yl_ok, n - 1)
                    pool.tensor_tensor(YR[n % 2][0:m, :], YW[n % 2][0:m, :], YP[0:m, n, 0, :],
                                       ALU.subtract).then_inc(yr_ok, 1)

            @block.tensor
            def _(pe):
                pe.wait_ge(d_sh, 48)
                for n in range(3):
                    for k in range(KT):
                        for c in range(KT):
                            mm = pe.transpose(g.ps[:, 4 + n, (KT * k + c) * P:(KT * k + c + 1) * P],
                                              shw[:, n, c, k * P:(k + 1) * P], g.ident[:, :])
                    mm.then_inc(filled, 1)
                pe.wait_ge(d_r, 16)
                for k in range(KT):
                    mm = pe.transpose(g.ps[:, 7, k * E:(k + 1) * E], rw[:, k * P:(k + 1) * P], g.ident[0:E, 0:E])
                mm.then_inc(filled, 1)
                transpose_xn_tensor(pe, g)
                pe.wait_ge(g.xt, 4 * g.ln_base)
                pe.wait_ge(emptied, 4)
                for t in range(NT):
                    for k in range(KT):
                        mm = pe.matmul(g.ps[:, 4, t * E:(t + 1) * E], g.XT[:, k, t * P:(t + 1) * P], rwT[:, k, :],
                                       start=(k == 0), stop=(k == KT - 1))
                mm.then_inc(rl_ps, 1)
                for n, (h, o) in enumerate(shared_steps):
                    if n >= 2:
                        pe.wait_ge(hs_ok, n - 1)
                    for w in range(2):
                        for k in range(KT):
                            mm = pe.matmul(g.ps[:, 2 * (n % 2) + w, :], shT[:, w, k, o * P:(o + 1) * P],
                                           g.XT[:, k, 512 * h:512 * h + 512], start=(k == 0), stop=(k == KT - 1))
                    mm.then_inc(gu_sh, 1)
                pe.wait_ge(mk_ok, 2)
                pe.wait_ge(tri_ok, 1)
                for t in range(NT):
                    for m in range(t + 1):
                        mm = pe.matmul(g.ps[:, 5, t * E:(t + 1) * E], (tri if m == t else ones)[:, :],
                                       MKb[:, m, :], start=(m == 0), stop=(m == t))
                mm.then_inc(cnt_ps, 1)
                pe.wait_ge(hs_ok, 4)
                pe.wait_ge(xp_b, 2)
                pe.wait_ge(xp_c, 2)
                for t in range(NT):
                    pe.wait_ge(s_ok, t + 1)
                    for (k, c), bank in zip(gathers, GBANK):
                        a, z = chunks[c]
                        for part in range(3):
                            mm = pe.matmul(g.ps[:, bank, 0:z - a], XP[:, part, t, k * P:(k + 1) * P],
                                           SM[:, t, a:z], start=(t == 0 and part == 0),
                                           stop=(t == NT - 1 and part == 2))
                mm.then_inc(xg_ps, 1)
                pe.wait_ge(wp_b, 2)
                pe.wait_ge(c_fill, 3)
                for n in range(ST_T):
                    m = CAP * count(n)
                    for t in range(NT):
                        mm = pe.matmul(g.ps[0:m, 4, 9 * n:9 * n + 9], SM[:, t, SLOTS * n:SLOTS * n + m],
                                       WP[:, t, :, EPT * n:EPT * n + EPT], start=(t == 0), stop=(t == NT - 1))
                mm.then_inc(ws_ps, 1)

                def gate_up(n):
                    r = n % RING
                    pe.wait_ge(d_e[r], 48 * (n // RING + 1))
                    if n >= 2:
                        pe.wait_ge(hp_ok, n - 1)
                    for j in range(count(n)):
                        xs = slice((EPT * n + j) * CAP, (EPT * n + j + 1) * CAP)
                        for w, wt in enumerate((EG[r], EU[r])):
                            for k in range(KT):
                                mm = pe.matmul(g.ps[:, GU + n % 2, w * SLOTS + j * CAP:w * SLOTS + (j + 1) * CAP],
                                               wt[:, j, k, :], XG[:, k, xs], start=(k == 0), stop=(k == KT - 1))
                    mm.then_inc(gu_ps, 1)

                def turn(n):
                    m = CAP * count(n)
                    if n >= 2:
                        pe.wait_ge(st_ok, n - 1)
                    o = g.ps[0:m, STB + n % 2, :].bitcast(BF16)
                    for t in range(NT):
                        mm = pe.transpose(o[:, t * P:(t + 1) * P], SM[:, t, SLOTS * n:SLOTS * n + m],
                                          g.identb[:, :])
                    mm.then_inc(st_ps, 1)

                def down(n):
                    m = CAP * count(n)
                    pe.wait_ge(hp_ok, n + 1)
                    if n >= 2:
                        pe.wait_ge(yw_ok, n - 1)
                    flat = HP[n % 2][:, :, :].rearrange("p j w -> p (j w)")
                    for j in range(count(n)):
                        mm = pe.matmul(g.ps[0:m, Y + n % 2, 0:D], flat[:, SLOTS * j:SLOTS * j + m],
                                       ED[n % RING][:, j, :], start=(j == 0), stop=(j == count(n) - 1))
                    mm.then_inc(y_ps, 1)

                pe.wait_ge(xg_ok, 6)
                for n in range(ST_T):
                    gate_up(n)
                    turn(n)
                    if n >= 1:
                        down(n - 1)
                pe.wait_ge(st_ok, ST_T)
                pe.wait_ge(ws_ok, 1)
                acc = lambda t: g.ps[:, ACC + t // 2, D * (t % 2):D * (t % 2) + D]
                for t in range(NT):
                    for k in range(KT):
                        pe.matmul(acc(t), HS[:, k, t * P:(t + 1) * P], shT[:, 2, k, :],
                                  start=(t % 2 == 0 and k == 0), stop=False, skip_group_check=True)
                down(ST_T - 1)

                def scatter(t, n):
                    m = CAP * count(n)
                    for part in range(3):
                        mm = pe.matmul(acc(t), STT[0:m, n, t * P:(t + 1) * P], YP[0:m, n, part, :], start=False,
                                       stop=(n == ST_T - 1 and part == 2), skip_group_check=True)
                    return mm
                pe.wait_ge(yl_ok, ST_T - 1)
                for t in range(NT):
                    for n in range(ST_T - 1):
                        scatter(t, n)
                pe.wait_ge(yl_ok, ST_T)
                for t in range(NT):
                    mm = scatter(t, ST_T - 1)
                    if t % 2 == 1:
                        mm.then_inc(acc_ps, 1)

            @block.scalar
            def _(act):
                layernorm_scalar(act, g)
                for n in range(3):
                    act.wait_ge(filled, n + 1)
                    act.activation(shT[:, n, :, :], g.ps[:, 4 + n, :], ACT.Copy).then_inc(emptied, 1)
                act.wait_ge(filled, 4)
                act.activation(rwT[:, :, :], g.ps[:, 7, 0:KT * E], ACT.Copy).then_inc(emptied, 1)
                transpose_xn_scalar(act, g)
                act.wait_ge(rl_ps, 1)
                act.activation(SG[:, :, :], g.ps[:, 4, 0:NT * E], ACT.Sigmoid).then_inc(sg_ok, 1)
                for h in range(2):
                    act.activation(XP[:, 0, 4 * h:4 * h + 4, :], g.XN[:, 4 * h:4 * h + 4, :],
                                   ACT.Copy).then_inc(xp_a, 1)
                for n in range(len(shared_steps)):
                    act.wait_ge(gu_sh, n + 1)
                    if n >= 2:
                        act.wait_ge(hs_ok, n - 1)
                    act.activation(SL[n % 2][:, :], g.ps[:, 2 * (n % 2), :], ACT.Silu).then_inc(sl_ok, 1)
                for h in range(2):
                    act.wait_ge(xp_r, h + 1)
                    act.activation(XP[:, 1, 4 * h:4 * h + 4, :], XR[:, 4 * h:4 * h + 4, :],
                                   ACT.Copy).then_inc(xp_b, 1)
                act.wait_ge(w_ok, 1)
                act.activation(WP[:, :, 0, 0:E], W[:, :, :], ACT.Copy).then_inc(wp_a, 1)
                act.wait_ge(wp_r, 1)
                act.activation(WP[:, :, 1, 0:E], WR_[:, :, :], ACT.Copy).then_inc(wp_b, 1)
                act.wait_ge(xg_ps, 1)
                for n, ((k, c), bank) in enumerate(zip(gathers, GBANK)):
                    if n % 2 == 0:
                        a, z = chunks[c]
                        act.activation(XG[:, k, a:z], g.ps[:, bank, 0:z - a], ACT.Copy).then_inc(xg_ok, 1)

                def results(n):
                    m = CAP * count(n)
                    act.wait_ge(y_ps, n + 1)
                    if n == 0:
                        act.wait_ge(ws_ok, 1)
                    if n >= 2:
                        act.wait_ge(yr_ok, n - 1)
                    act.activation(YW[n % 2][0:m, :], g.ps[0:m, Y + n % 2, 0:D], ACT.Copy,
                                   scale=wslot[0:m, n:n + 1]).then_inc(yw_ok, 1)
                    act.wait_ge(yw_ok, n + 1)
                    act.activation(YP[0:m, n, 0, :], YW[n % 2][0:m, :], ACT.Copy).then_inc(yh_ok, 1)

                def second(n):
                    m = CAP * count(n)
                    act.wait_ge(yr_ok, n + 1)
                    act.activation(YP[0:m, n, 1, :], YR[n % 2][0:m, :], ACT.Copy).then_inc(ym_ok, 1)

                for n in range(ST_T):
                    m = CAP * count(n)
                    act.wait_ge(gu_ps, n + 1)
                    if n >= 2:
                        act.wait_ge(hp_ok, n - 1)
                    act.activation(SE[n % 2][:, 0:m], g.ps[:, GU + n % 2, 0:m], ACT.Silu).then_inc(se_ok, 1)
                    if n % 2 == 0:
                        act.wait_ge(st_ps, n + 1)
                        act.wait_ge(st_ok, n)
                        act.activation(STT[0:m, n, :], g.ps[0:m, STB, :].bitcast(BF16), ACT.Copy).then_inc(st_ok, 1)
                    if n >= 2:
                        second(n - 2)
                    if n >= 1:
                        results(n - 1)
                second(ST_T - 2)
                results(ST_T - 1)
                second(ST_T - 1)

            @block.vector
            def _(dve):
                steps = 0

                def link(ins):
                    nonlocal steps
                    steps += 1
                    ins.then_inc(rt, 1)
                    dve.wait_ge(rt, steps)

                layernorm_vector(dve, g, lambda t: None)
                id3 = g.ident[:, 0:SLOTS].rearrange("p (j c) -> p j c", j=EPT)
                dve.tensor_reduce(own[:, :], id3, AX.X, ALU.add).then_inc(own_ok, 1)
                dve.wait_ge(d_eb, 16)
                dve.wait_ge(sg_ok, 1)
                link(dve.tensor_tensor(SBI[:, :, :], SG[:, :, :], eb[:, :].unsqueeze(1).broadcast_to([P, NT, E]),
                                       ALU.add))
                four = SBI[:, :, :].rearrange("p t (g a b) -> p (t g) a b", a=2, b=2)
                dve.tensor_tensor(hl[:, 0, :, :], four[:, :, :, 0], four[:, :, :, 1], ALU.max)
                link(dve.tensor_tensor(hl[:, 1, :, :], four[:, :, :, 0], four[:, :, :, 1], ALU.min))
                dve.tensor_tensor(tp[:, 0, :], hl[:, 0, :, 0], hl[:, 0, :, 1], ALU.max)
                dve.tensor_tensor(tp[:, 1, :], hl[:, 0, :, 0], hl[:, 0, :, 1], ALU.min)
                link(dve.tensor_tensor(tp[:, 2, :], hl[:, 1, :, 0], hl[:, 1, :, 1], ALU.max))
                link(dve.tensor_tensor(tp[:, 3, :], tp[:, 1, :], tp[:, 2, :], ALU.max))
                dve.wait_ge(c_fill, 3)
                tg = lambda x: x.rearrange("p (t g) -> p t g", t=NT)
                link(dve.tensor_tensor(GB[:, :, GF:], tg(tp[:, 0, :]), tg(tp[:, 3, :]), ALU.add))
                for t in range(NT):
                    last = dve.max(g8[:, t, :], GB[:, t, :])
                    if t < NT - 1:
                        last.then_inc(own_ok, 1)
                link(last)
                dve.wait_ge(own_ok, NT)
                for t in range(NT):
                    last = dve.match_replace(GR[:, t, :], g8[:, t, :], GB[:, t, :], NEG)
                    if t < NT - 1:
                        last.then_inc(own_ok, 1)
                link(last)
                dve.wait_ge(own_ok, 2 * NT - 1)
                link(dve.tensor_tensor(gm[:, :, :], GB[:, :, GF:], GR[:, :, GF:], ALU.not_equal))
                sp4 = lambda x: x.rearrange("p t (g a) -> p t g a", a=GE)
                link(dve.tensor_tensor(sp4(mz[:, :, :]), sp4(SBI[:, :, :]),
                                       gm[:, :, :].unsqueeze(3).broadcast_to([P, NT, GROUPS, GE]), ALU.mult))
                link(dve.tensor_scalar(MB[:, :, EF:], mz[:, :, :], 0.0, None, ALU.add))
                for t in range(NT):
                    last = dve.max(e8[:, t, :], MB[:, t, :])
                    if t < NT - 1:
                        last.then_inc(own_ok, 1)
                link(last)
                dve.wait_ge(own_ok, 3 * NT - 2)
                for t in range(NT):
                    last = dve.match_replace(MR[:, t, :], e8[:, t, :], MB[:, t, :], NEG)
                    if t < NT - 1:
                        last.then_inc(own_ok, 1)
                link(last)
                dve.wait_ge(own_ok, 4 * NT - 3)
                dve.tensor_tensor(MKb[:, :, :], MB[:, :, EF:], MR[:, :, EF:], ALU.not_equal).then_inc(mk_ok, 1)
                dve.tensor_tensor(MK[:, :, :], MB[:, :, EF:], MR[:, :, EF:], ALU.not_equal).then_inc(mk_ok, 1)
                dve.wait_ge(mk_ok, 2)
                link(dve.tensor_tensor(wsel[:, :, :], SG[:, :, :], MK[:, :, :], ALU.mult))
                link(dve.tensor_reduce(wsum[:, 0, :], wsel[:, :, :], AX.X, ALU.add))
                link(dve.tensor_scalar(wsum[:, 1, :], wsum[:, 0, :], 1e-20, None, ALU.add))
                link(dve.reciprocal(wsum[:, 2, :], wsum[:, 1, :]))
                link(dve.tensor_tensor(WR_[:, :, :], wsel[:, :, :],
                                       wsum[:, 2, :].unsqueeze(2).broadcast_to([P, NT, E]), ALU.mult))
                dve.tensor_scalar(W[:, :, :], WR_[:, :, :], ROUTE_SCALE, None, ALU.mult).then_inc(w_ok, 1)

                def shared(n):
                    h, o = shared_steps[n]
                    dve.wait_ge(sl_ok, n + 1)
                    dve.tensor_tensor(HS[:, o, 512 * h:512 * h + 512], SL[n % 2][:, :],
                                      g.ps[:, 2 * (n % 2) + 1, :], ALU.mult).then_inc(hs_ok, 1)
                for n in range(len(shared_steps)):
                    shared(n)
                dve.wait_ge(cnt_ps, 1)
                dve.scalar_tensor_tensor(out=place[:, :, :],
                                         in0=g.ps[:, 5, 0:NT * E].rearrange("p (t e) -> p t e", t=NT),
                                         scalar=1.0, in1=MK[:, :, :], op0=ALU.add,
                                         op1=ALU.mult).then_inc(place_ok, 1)
                dve.wait_ge(place_ok, 1)
                dve.wait_ge(iotf_ok, 1)
                for t in range(NT):
                    dve.tensor_tensor(SM[:, t, :].rearrange("p (e c) -> p e c", c=CAP),
                                      place[:, t, :].unsqueeze(2).broadcast_to([P, E, CAP]),
                                      iotf[:, :].unsqueeze(1).broadcast_to([P, E, CAP]),
                                      ALU.is_equal).then_inc(s_ok, 1)
                dve.wait_ge(xg_ps, 1)
                for n, ((k, c), bank) in enumerate(zip(gathers, GBANK)):
                    if n % 2 == 1:
                        a, z = chunks[c]
                        dve.tensor_copy(XG[:, k, a:z], g.ps[:, bank, 0:z - a]).then_inc(xg_ok, 1)
                dve.wait_ge(ws_ps, 1)
                link(dve.tensor_tensor(ws[0:SLOTS].rearrange("p n a j -> p (n a) j"),
                                       g.ps[0:SLOTS, 4, 0:9 * ST_T].rearrange("p (n j) -> p n j", j=EPT),
                                       own[0:SLOTS, :].unsqueeze(1).broadcast_to([SLOTS, 3 * ST_T, EPT]), ALU.mult))
                dve.tensor_reduce(wslot[0:SLOTS, :], ws[0:SLOTS].rearrange("p n a j -> p n (a j)"), AX.X,
                                  ALU.add).then_inc(ws_ok, 1)

                def third(n):
                    m = CAP * count(n)
                    dve.wait_ge(ym_ok, n + 1)
                    dve.tensor_tensor(YP[0:m, n, 2, :], YR[n % 2][0:m, :], YP[0:m, n, 1, :],
                                      ALU.subtract).then_inc(yl_ok, 1)
                dve.wait_ge(hp0, 2)
                for n in range(ST_T):
                    m = CAP * count(n)
                    dve.wait_ge(se_ok, n + 1)
                    if n >= 2:
                        dve.wait_ge(y_ps, n - 1)
                    c = count(n)
                    dve.tensor_tensor(HP[n % 2][:, 0:c, 0:CAP],
                                      SE[n % 2][:, 0:m].rearrange("p (j w) -> p j w", j=c),
                                      g.ps[:, GU + n % 2, SLOTS:SLOTS + m].rearrange("p (j w) -> p j w", j=c),
                                      ALU.mult).then_inc(hp_ok, 1)
                    if n % 2 == 1:
                        dve.wait_ge(st_ps, n + 1)
                        dve.wait_ge(st_ok, n)
                        dve.tensor_copy(STT[0:m, n, :], g.ps[0:m, STB + 1, :].bitcast(BF16)).then_inc(st_ok, 1)
                    if n >= 3:
                        third(n - 3)
                for n in range(ST_T - 3, ST_T):
                    third(n)
                for b in range(B):
                    dve.wait_ge(acc_ps, b + 1)
                    for t in (2 * b, 2 * b + 1):
                        dve.scalar_tensor_tensor(out=g.X[:, t, :], in0=g.ps[:, ACC + b, D * (t % 2):D * (t % 2) + D],
                                                 scalar=g.gate[:, 3:4], in1=g.X[:, t, :], op0=ALU.mult,
                                                 op1=ALU.add).then_inc(fin_ok, 1)


def store_x(nc, g, out):
    with nc.semaphore("stored") as stored, nc.Block() as block:
        @block.sync
        def _(sp):
            sp.dma_start(out.rearrange("b (t p) d -> p (b t) d", p=P), g.X[:, :, :]).then_inc(stored, 16)
            sp.wait_ge(stored, 16)


def build(nc, i, out, stages=4):
    g = Shared()
    with ExitStack() as ctx:
        sb = lambda name, shape, dt=F32: ctx.enter_context(nc.sbuf_tensor(name, shape, dt))
        sem = lambda name: ctx.enter_context(nc.semaphore(name))
        g.ps = ctx.enter_context(nc.psum_tensor("ps", [P, 8, 512], F32))
        g.X = sb("X", [P, NT, D])
        g.XN = sb("XN", [P, NT, D])
        g.XT = sb("XT", [P, KT, T])
        g.stat, g.mv = sb("stat", [P, NT, 6]), sb("mv", [P, NT, 2])
        g.var, g.std, g.rstd = sb("var", [P, NT]), sb("std", [P, NT]), sb("rstd", [P, NT])
        g.ident, g.identb = sb("ident", [P, P]), sb("identb", [P, P], BF16)
        g.gate = sb("gate", [P, 4])
        g.ln_stats, g.ln_aggr, g.ln_var, g.ln_std = sem("ln_stats"), sem("ln_aggr"), sem("ln_var"), sem("ln_std")
        g.ln_rstd, g.ln_xn, g.xt_ps, g.xt = sem("ln_rstd"), sem("ln_xn"), sem("xt_ps"), sem("xt")
        g.d_br, g.d_ropeq = sem("d_br"), sem("d_ropeq")
        g.x_done = sem("x_done")
        g.ln_base = 0
        with ExitStack() as middle:
            mb = lambda name, shape: middle.enter_context(nc.sbuf_tensor(name, shape, F32))
            g.cosq, g.sinq = mb("cosq", [HALF, 2, S]), mb("sinq", [HALF, 2, S])
            g.KV = mb("KV", [P, NT, 2, DC])
            g.KD = mb("KD", [P, B, 2 * S])
            with ExitStack() as early:
                eb = lambda name, shape: early.enter_context(nc.sbuf_tensor(name, shape, F32))
                g.br = eb("br", [P, NBLK])
                g.W1T = eb("W1T", [P, KT, HID])
                g.W2T = eb("W2T", [P, HID // P, D])
                g.WrT = eb("WrT", [P, KT, NBLK])
                stage_adjacency(nc, g, i)
                if stages >= 2:
                    stage_block_ffn(nc, g, i)
            if stages >= 3:
                stage_latent_attention(nc, g, i)
        if stages >= 4:
            stage_moe(nc, g, i, out)
        else:
            store_x(nc, g, out)


_INS = ["x", "ctx_512", "g_xattn", "g_ffn", "L0_xattn_Wq", "L0_xattn_Wk", "L0_xattn_gamma_raw", "L0_ffn_Wr",
        "L0_ffn_br", "L0_ffn_W1", "L0_ffn_W2", "L1_xattn_Wq", "L1_xattn_w_kc_q", "L1_xattn_w_kc_kv",
        "L1_xattn_W_qr", "L1_xattn_W_kr", "L1_xattn_Wo", "L1_ffn_router_w", "L1_ffn_e_bias", "L1_ffn_W_gate",
        "L1_ffn_W_up", "L1_ffn_W_down", "L1_ffn_shared_gate", "L1_ffn_shared_up", "L1_ffn_shared_down"]


def rope_tables():
    def table(width):
        inv = (1.0 / 10000.0 ** (np.arange(0, width, 2, dtype=np.float32) / np.float32(width))).astype(np.float32)
        f = np.arange(S, dtype=np.float32)[:, None] * inv[None, :]
        return np.repeat(np.sin(f), 2, axis=-1), np.repeat(np.cos(f), 2, axis=-1)
    sq, cq = table(DQ)
    sk, ck = table(DC)
    sk = np.concatenate([-sk[:, :DC // 2], sk[:, DC // 2:]], axis=1)
    halves = lambda x: np.ascontiguousarray(x.T.reshape(2, HALF, S).transpose(1, 0, 2))
    rows = lambda x: np.ascontiguousarray(x.reshape(2, P, DC).transpose(1, 0, 2))
    return {"cosq": halves(cq), "sinq": halves(sq), "cosk": rows(ck), "sink": rows(sk)}


def kernel(**inputs):
    import concourse.bacc as _bacc
    from concourse.bass_utils import run_bass_kernel_spmd as _run

    nc = _bacc.Bacc("TRN2", target_bir_lowering=False, num_devices=1)
    arrays, args = {}, {}
    for name, a in list((n, inputs[n]) for n in _INS) + list(rope_tables().items()):
        a = np.ascontiguousarray(a)
        arrays[f"in_{name}_dram"] = a
        args[name] = nc.dram_tensor(f"in_{name}_dram", a.shape, mybir.dt.from_np(a.dtype), kind="ExternalInput").ap()
    out = nc.dram_tensor("out_0_dram", (B, S, D), F32, kind="ExternalOutput").ap()
    build(nc, args, out, STAGES)
    r = _run(nc, [arrays], core_ids=[0])
    return r.results[0]["out_0_dram"]
```

```python
from contextlib import ExitStack

import concourse.bass as bass
import numpy as np
from concourse import mybir

F32 = mybir.dt.float32
BF16 = mybir.dt.bfloat16
F16 = mybir.dt.float16
ALU = mybir.AluOpType
ACT = mybir.ActivationFunctionType
AX = mybir.AxisListType

P = 128
B, S, D = 4, 256, 256
T = B * S
NT = T // P
KT = D // P
LN_EPS = 1e-5
BIG, NEG = 3.0e38, -3.0e38

DC = 64
TOP_ADJ = int(S * 0.3)
ROUNDS = (TOP_ADJ + 7) // 8

NBLK, BLK, TOP_BLK = 16, 64, 4
HID = NBLK * BLK

H, HK, DQ, R = 16, 128, 192, 64
HALF = DQ // 2
PAIRS = H // 2

E, EI = 32, 128
TOP_E, GROUPS, TOP_G = 4, 8, 3
GE = E // GROUPS
CAP = -(-5 * T // (4 * E))
ROUTE_SCALE = 2.5
EPT = P // CAP
ST_T = -(-E // EPT)
SLOTS = EPT * CAP
SHARED = 256
STAGES = 4


class Shared:
    pass


class Norm:

    def __init__(self, sem, name, size):
        self.size = size
        self.stats, self.aggr, self.var = sem(name + "_stats"), sem(name + "_aggr"), sem(name + "_var")
        self.std, self.rstd, self.xn = sem(name + "_std"), sem(name + "_rstd"), sem(name + "_xn")


def norm_stats(dve, g, nm, q):
    n = nm.size
    for t in range(n * q, n * q + n):
        dve.bn_stats(g.stat[:, t, :], g.X[:, t, :]).then_inc(nm.stats, 1)
    for t in range(n * q, n * q + n):
        dve.wait_ge(nm.stats, t + 1)
        dve.bn_aggr(g.mv[:, t, :], g.stat[:, t, :]).then_inc(nm.aggr, 1)
    dve.wait_ge(nm.aggr, n * q + n)
    dve.tensor_scalar(g.var[:, n * q:n * q + n], g.mv[:, n * q:n * q + n, 1], LN_EPS, None,
                      ALU.add).then_inc(nm.var, 1)


def norm_root(act, g, nm, q):
    n = nm.size
    act.wait_ge(nm.var, q + 1)
    act.activation(g.std[:, n * q:n * q + n], g.var[:, n * q:n * q + n], ACT.Sqrt).then_inc(nm.std, 1)


def norm_inverse(dve, g, nm, q):
    n = nm.size
    dve.wait_ge(nm.std, q + 1)
    dve.reciprocal(g.rstd[:, n * q:n * q + n], g.std[:, n * q:n * q + n]).then_inc(nm.rstd, 1)


def norm_apply(eng, g, nm, q):
    n = nm.size
    eng.wait_ge(nm.rstd, q + 1)
    for t in range(n * q, n * q + n):
        eng.tensor_scalar(g.XN[:, t, :], g.X[:, t, :], g.mv[:, t, 0:1], g.rstd[:, t:t + 1],
                          ALU.subtract, ALU.mult).then_inc(nm.xn, 1)


def norm_turn(pe, g, nm, q, bank):
    pe.wait_ge(nm.xn, 2 * q + 2)
    for k in range(KT):
        for j in range(2):
            mm = pe.transpose(bank[:, S * k + j * P:S * k + (j + 1) * P], g.XN[:, 2 * q + j, k * P:(k + 1) * P],
                              g.ident[:, :])
    return mm


FOLDS = 6
FOLD_SPLIT = (0, 1, 5)
UP = 64.0


def fold_product(pe, g, u, f, o):
    if f < 2:
        for h in range(2):
            mm = pe.matmul(o[:, h * DQ:(h + 1) * DQ], g.WQ[u][:, h, f * P:(f + 1) * P], g.WCQ[u][:, h, :],
                           start=True, stop=True)
    elif f == 2:
        for h in range(2):
            pe.transpose(o[:, h * HALF:(h + 1) * HALF], g.WQR[u][:, h, :, :].rearrange("j a r -> j (a r)"),
                         g.ident[0:HALF, 0:HALF])
        mm = pe.transpose(o[:, 2 * HALF:2 * HALF + DC], g.WKR[u][:, :, :].rearrange("d h r -> d (h r)"),
                          g.ident[0:DC, 0:DC])
    elif f == 3:
        for h in range(2):
            for c in range(KT):
                mm = pe.transpose(o[:, h * D + c * P:h * D + (c + 1) * P], g.WO[u][:, c, h * HK:(h + 1) * HK],
                                  g.ident[:, :])
    elif f == 4:
        for h in range(2):
            for a in range(2):
                mm = pe.matmul(o[0:HALF, (2 * h + a) * DC:(2 * h + a + 1) * DC],
                               g.RT[:, a, h * HALF:(h + 1) * HALF], g.RT[:, h, 2 * HALF:2 * HALF + DC],
                               start=True, stop=True)
    else:
        for h in range(2):
            mm = pe.matmul(o[DC * h:DC * h + DC, 0:D], g.WCV[u][:, h, :], g.WOT[:, h, :], start=True, stop=True)
    return mm


def fold_keep(act, g, r, u, f, o):
    if f < 2:
        return act.activation(g.CH[u][:, f, :], o[:, 0:2 * DQ], ACT.Copy, scale=UP)
    if f == 2:
        act.activation(g.RT[:, 0, :], o[0:R, 0:2 * HALF + DC], ACT.Copy)
        return act.activation(g.RT[:, 1, :], o[R:P, 0:2 * HALF + DC], ACT.Copy)
    if f == 3:
        return act.activation(g.WOT[:, :, :], o, ACT.Copy)
    if f == 4:
        return act.activation(g.M[u][:, :, :], o[0:HALF, 0:4 * DC], ACT.Copy, scale=1.0 / UP)
    return act.activation(g.NH[:, bass.ds(r, 1), :], o[:, 0:D], ACT.Copy, scale=UP)


def fold_rest(dve, g, r, u, f, o):
    hi, lo, w = ((g.CH[u][:, f, :], g.CL[u][:, f, :], 2 * DQ) if f < 2 else
                 (g.NH[:, bass.ds(r, 1), :], g.NL[:, bass.ds(r, 1), :], D))
    return dve.scalar_tensor_tensor(out=lo, in0=o[:, 0:w], scalar=UP, in1=hi, op0=ALU.mult, op1=ALU.subtract)


DW = 7 * 16


def load_pair(sp, g, i, r, u):
    two_heads = bass.ds(2 * r, 2)
    wqr_v = i["L1_xattn_W_qr"].rearrange("h (a j) r -> j h a r", a=2)
    sp.dma_start(g.WQ[u][:, :, :], i["L1_xattn_Wq"].rearrange("(h k) n -> k h n", k=HK)[:, two_heads, :]
                 ).then_inc(g.d_w[u], 16)
    sp.dma_start(g.WCQ[u][:, :, :], i["L1_xattn_w_kc_q"].rearrange("h k q -> k h q")[:, two_heads, :]
                 ).then_inc(g.d_w[u], 16)
    sp.dma_start(g.WCV[u][:, :, :], i["L1_xattn_w_kc_kv"].rearrange("h k d -> k h d")[:, two_heads, :]
                 ).then_inc(g.d_w[u], 16)
    for h in range(2):
        sp.dma_start(g.WQR[u][:, h, :, :], wqr_v[:, bass.ds(2 * r + h, 1), :, :]).then_inc(g.d_w[u], 16)
    sp.dma_start(g.WKR[u][:, :, :], i["L1_xattn_W_kr"].rearrange("h d r -> d h r")[:, two_heads, :]
                 ).then_inc(g.d_w[u], 16)
    sp.dma_start(g.WO[u][:, :, :], i["L1_xattn_Wo"].rearrange("(c p) n -> p c n", p=P)[
        :, :, bass.ds(2 * HK * r, 2 * HK)]).then_inc(g.d_w[u], 16)


def stage_first_layer(nc, g, i):
    with ExitStack() as ctx:
        sb = lambda name, shape, dt=F32: ctx.enter_context(nc.sbuf_tensor(name, shape, dt))
        sem = lambda name: ctx.enter_context(nc.semaphore(name))
        CT = sb("CT", [P, NT, DC])
        CTT = sb("CTT", [DC, T])
        wq = sb("wq", [DC, DC])
        wk = sb("wk", [DC, DC])
        GT = sb("GT", [DC, DC])
        V = sb("V", [DC, T])
        SIM = sb("SIM", [P, NT, S])
        SIG = sb("SIG", [P, NT, S])
        work = sb("work", [P, 2, S])
        m8 = sb("m8", [P, 2, ROUNDS, 8])
        A = sb("A", [P, NT, S])
        XA = sb("XA", [P, NT, S])
        raw = sb("raw", [P, 5])
        gam = sb("gam", [P, 4])
        mix = sb("mix", [P, 3, NT])
        w1 = sb("w1", [P, HID // P, D])
        w2 = sb("w2", [P, KT, HID])
        wr = sb("wr", [NBLK, D])
        br = sb("br", [P, NBLK])
        W1T = sb("W1T", [P, KT, HID])
        W2T = sb("W2T", [P, HID // P, D])
        WrT = sb("WrT", [P, KT, NBLK])
        ck = sb("ck", [P, 2, DC])
        sk = sb("sk", [P, 2, DC])
        kc = sb("kc", [P, NT, DC])
        ks = sb("ks", [P, NT, DC])
        XT = [sb(f"XT{u}", [P, KT, S]) for u in range(2)]
        FILL = 8 - TOP_BLK
        LG = sb("LG", [P, NT, FILL + NBLK])
        RP = sb("RP", [P, NT, FILL + NBLK])
        M8 = sb("M8", [P, NT, 8])
        MK = sb("MK", [P, NT, NBLK], BF16)
        GL = [sb(f"GL{u}", [P, 2, S]) for u in range(2)]
        MS = [sb(f"MS{u}", [P, 2, S]) for u in range(2)]
        HT = [sb(f"HT{u}", [P, HID // P, S]) for u in range(2)]

        d_x, d_ctx, d_wqk, d_raw, d_rope = map(sem, ["d_x", "d_ctx", "d_wqk", "d_raw", "d_rope"])
        d_w1, d_w2, d_wr, d_br = map(sem, ["d_w1", "d_w2", "d_wr", "d_br"])
        id_zero, id_ok, kd_zero, kv_mul, kv_sum, kv_ok, lg_fill = map(
            sem, ["id_zero", "id_ok", "kd_zero", "kv_mul", "kv_sum", "kv_ok", "lg_fill"])
        filled, hi_ok, emptied, at_ps = map(sem, ["filled", "hi_ok", "emptied", "at_ps"])
        tanh_ok, gam_ok, max_ok, rep_ok, a_ok, xa_ok, x1_ok = map(
            sem, ["tanh_ok", "gam_ok", "max_ok", "rep_ok", "a_ok", "xa_ok", "x1_ok"])
        sim_ok, mix_ok, split_ok = map(sem, ["sim_ok", "mix_ok", "split_ok"])
        (xt_ps, xt_ok, lg_ps, lg_ok, top_ok, mark_ok, mk_ok, h_ps, gelu_ok, mask_ps, ms_ok, ht_ok, y_ps, x2_ok,
         x2t_ps, xh_ok, xl_ok) = map(
            sem, ["xt_ps", "xt_ok", "lg_ps", "lg_ok", "top_ok", "mark_ok", "mk_ok", "h_ps", "gelu_ok", "mask_ps",
                  "ms_ok", "ht_ok", "y_ps", "x2_ok", "x2t_ps", "xh_ok", "xl_ok"])
        n0, n1, n2 = Norm(sem, "n0", NT), Norm(sem, "n1", 2), Norm(sem, "n2", 2)

        x_v = i["x"].rearrange("b (t p) d -> p (b t) d", p=P)
        c_v = i["ctx_512"].rearrange("b (t p) d -> p (b t) d", p=P)
        N_G, N_V, N_SIM, N_W1, N_W2, N_WR, N_KV, N_FOLD = 2, 3, 5, 9, 13, 17, 18, 20
        N_ALL = N_FOLD + 2 * FOLDS
        is_split = [N_KV <= n < N_FOLD or (n >= N_FOLD and (n - N_FOLD) % FOLDS in FOLD_SPLIT) for n in range(N_ALL)]
        splits = lambda n: sum(is_split[0:n + 1])
        plain = lambda n: n + 1 - splits(n)

        def wait_empty(eng, n):
            if is_split[n]:
                eng.wait_ge(split_ok, splits(n))
            else:
                eng.wait_ge(emptied, plain(n))

        LB, HB, MB, AB, TB, UB, YB = 0, 1, 3, 4, 5, 6, 7
        UNITS = HID // P // 2

        with nc.Block() as block:
            @block.sync
            def _(sp):
                sp.dma_start(CT[:, :, :], c_v).then_inc(d_ctx, 16)
                sp.dma_start(wq[:, :], i["L0_xattn_Wq"]).then_inc(d_wqk, 16)
                sp.dma_start(wk[:, :], i["L0_xattn_Wk"]).then_inc(d_wqk, 16)
                for h in range(2):
                    sp.dma_start(g.X[:, 4 * h:4 * h + 4, :], x_v[:, 4 * h:4 * h + 4, :]).then_inc(d_x, 16)
                sp.dma_start(w1[:, :, :], i["L0_ffn_W1"].rearrange("(o p) n -> p o n", p=P)).then_inc(d_w1, 16)
                sp.dma_start(w2[:, :, :], i["L0_ffn_W2"].rearrange("(c p) n -> p c n", p=P)).then_inc(d_w2, 16)
                sp.dma_start(wr[:, :], i["L0_ffn_Wr"]).then_inc(d_wr, 16)
                sp.dma_start(br[:, :], i["L0_ffn_br"].partition_broadcast(P)).then_inc(d_br, 16)
                sp.dma_start(g.cosq[:, :, :], i["cosq"]).then_inc(g.d_ropeq, 16)
                sp.dma_start(g.sinq[:, :, :], i["sinq"]).then_inc(g.d_ropeq, 16)
                for r in range(2):
                    load_pair(sp, g, i, r, r)
                for r in range(2, 4):
                    sp.wait_ge(filled, N_FOLD + FOLDS * (r - 1))
                    load_pair(sp, g, i, r, r % 2)

            @block.gpsimd
            def _(pool):
                pool.memset(g.ident[:, :], 0.0).then_inc(id_zero, 1)
                pool.wait_ge(id_zero, 1)
                pool.affine_select(out=g.ident[:, :], in_=g.ident[:, :], compare_op=ALU.not_equal,
                                   fill=1.0, base=0, pattern=[[-1, P]],
                                   channel_multiplier=1).then_inc(id_ok, 1)
                pool.wait_ge(id_ok, 1)
                pool.tensor_copy(g.identb[:, :], g.ident[:, :]).then_inc(id_ok, 1)
                pool.memset(g.KDH[:, :, :], 0.0).then_inc(kd_zero, 1)
                pool.memset(g.KDL[:, :, :], 0.0).then_inc(kd_zero, 1)
                pool.memset(LG[:, :, 0:FILL], BIG).then_inc(lg_fill, 1)
                pool.wait_ge(d_ctx, 16)
                pool.wait_ge(d_rope, 32)
                lt = lambda x: x.rearrange("p (b l) d -> p b l d", l=2)
                tab = lambda x, a, z: x[:, :, a:z].unsqueeze(1).broadcast_to([P, B, 2, z - a])
                q = DC // 2
                pool.tensor_tensor(lt(kc), lt(CT), tab(ck, 0, DC), ALU.mult).then_inc(kv_mul, 1)
                pool.tensor_tensor(lt(ks)[:, :, :, 0:q], lt(CT)[:, :, :, q:DC], tab(sk, 0, q),
                                   ALU.mult).then_inc(kv_mul, 1)
                pool.tensor_tensor(lt(ks)[:, :, :, q:DC], lt(CT)[:, :, :, 0:q], tab(sk, q, DC),
                                   ALU.mult).then_inc(kv_mul, 1)
                pool.wait_ge(kv_mul, 3)
                pool.tensor_tensor(g.KV[:, :, 0, :], kc[:, :, :], ks[:, :, :], ALU.add).then_inc(kv_sum, 1)
                pool.wait_ge(kv_sum, 1)
                pool.tensor_copy(g.KV[:, :, 1, :], g.KV[:, :, 0, :]).then_inc(kv_ok, 1)
                pool.wait_ge(mix_ok, 4)
                for t in range(NT):
                    pool.tensor_scalar(XA[:, t, :], g.X[:, t, :], mix[:, 1, t:t + 1], mix[:, 2, t:t + 1],
                                       ALU.mult, ALU.add).then_inc(xa_ok, 1)

                def masked(b, n):
                    u = UNITS * b + n
                    pool.wait_ge(gelu_ok, u + 1)
                    pool.wait_ge(ms_ok, u + 1)
                    if b >= 2:
                        pool.wait_ge(y_ps, b - 1)
                    pool.tensor_tensor(HT[b % 2][:, 2 * n:2 * n + 2, :], GL[u % 2][:, :, :], MS[u % 2][:, :, :],
                                       ALU.mult).then_inc(ht_ok, 1)
                for b in range(B):
                    for n in range(UNITS):
                        masked(b, n)

            @block.tensor
            def _(pe):
                def bank(n):
                    if n >= 4:
                        wait_empty(pe, n - 4)
                    return g.ps[:, n % 4, :]
                pe.wait_ge(id_ok, 2)
                pe.wait_ge(d_ctx, 16)
                for h in range(2):
                    for j in range(4):
                        mm = pe.transpose(bank(h)[0:DC, j * P:(j + 1) * P], CT[:, 4 * h + j, :], g.ident[:, :])
                    mm.then_inc(filled, 1)
                pe.wait_ge(d_wqk, 32)
                pe.matmul(bank(N_G)[0:DC, 0:DC], wk[:, :], wq[:, :], start=True, stop=True).then_inc(filled, 1)
                wait_empty(pe, N_G)
                for h in range(2):
                    pe.matmul(bank(N_V + h)[0:DC, :], GT[:, :], CTT[:, 512 * h:512 * h + 512],
                              start=True, stop=True).then_inc(filled, 1)
                for b in range(B):
                    wait_empty(pe, N_V + b // 2)
                    o = bank(N_SIM + b)
                    for j in range(2):
                        mm = pe.matmul(o[:, S * j:S * j + S], CTT[:, (2 * b + j) * P:(2 * b + j + 1) * P],
                                       V[:, S * b:S * b + S], start=True, stop=True)
                    mm.then_inc(filled, 1)
                pe.wait_ge(d_w1, 16)
                for k in range(KT):
                    for h in range(2):
                        o = bank(N_W1 + 2 * k + h)
                        for j in range(4):
                            mm = pe.transpose(o[:, j * P:(j + 1) * P], w1[:, 4 * h + j, k * P:(k + 1) * P],
                                              g.ident[:, :])
                        mm.then_inc(filled, 1)
                pe.wait_ge(d_w2, 16)
                for q in range(4):
                    o = bank(N_W2 + q)
                    for j in range(2):
                        for c in range(KT):
                            mm = pe.transpose(o[:, (2 * j + c) * P:(2 * j + c + 1) * P],
                                              w2[:, c, (2 * q + j) * P:(2 * q + j + 1) * P], g.ident[:, :])
                    mm.then_inc(filled, 1)
                pe.wait_ge(d_wr, 16)
                o = bank(N_WR)
                for k in range(KT):
                    mm = pe.transpose(o[:, k * NBLK:(k + 1) * NBLK], wr[:, k * P:(k + 1) * P],
                                      g.ident[0:NBLK, 0:NBLK])
                mm.then_inc(filled, 1)
                pe.wait_ge(kv_ok, 1)
                for h in range(2):
                    o = bank(N_KV + h)
                    for j in range(4):
                        mm = pe.transpose(o[:, j * P:(j + 1) * P],
                                          g.KV[:, 4 * h + j, :, :].rearrange("p a d -> p (a d)"), g.ident[:, :])
                    mm.then_inc(filled, 1)

                for r in range(2):
                    pe.wait_ge(g.d_w[r], DW)
                    for f in range(FOLDS):
                        n = N_FOLD + FOLDS * r + f
                        if f >= 4:
                            wait_empty(pe, n - 2)
                        fold_product(pe, g, r, f, bank(n)).then_inc(filled, 1)

                def mask(b, n):
                    pe.wait_ge(mk_ok, b + 1)
                    if UNITS * b + n >= 1:
                        pe.wait_ge(ms_ok, UNITS * b + n)
                    for o in range(2):
                        for j in range(2):
                            for c in range(2):
                                block_no = 2 * (2 * n + o) + c
                                pick = MK[:, 2 * b + j, block_no:block_no + 1].broadcast_to([P, BLK])
                                mm = pe.matmul(g.ps[BLK * c:BLK * c + BLK, MB, S * o + j * P:S * o + (j + 1) * P],
                                               pick, g.identb[:, :], start=True, stop=True)
                    mm.then_inc(mask_ps, 1)

                def second_norm(b):
                    if b >= 1:
                        pe.wait_ge(xl_ok, b)
                    norm_turn(pe, g, n2, b, g.ps[:, UB, :]).then_inc(x2t_ps, 1)

                def result(b):
                    pe.wait_ge(ht_ok, UNITS * b + UNITS)
                    if b >= 1:
                        pe.wait_ge(x2_ok, 2 * b)
                    for j in range(2):
                        for o in range(HID // P):
                            mm = pe.matmul(g.ps[:, YB, D * j:D * j + D], HT[b % 2][:, o, j * P:(j + 1) * P],
                                           W2T[:, o, :], start=(o == 0), stop=(o == HID // P - 1))
                    mm.then_inc(y_ps, 1)

                pe.wait_ge(emptied, plain(N_ALL - 1))
                pe.wait_ge(split_ok, splits(N_ALL - 1))
                for b in range(B):
                    pe.wait_ge(a_ok, 2 * b + 2)
                    if b >= 1:
                        pe.wait_ge(x1_ok, 2 * b)
                    for j in range(2):
                        for m in range(2):
                            mm = pe.transpose(g.ps[:, AB, S * j + m * P:S * j + (m + 1) * P],
                                              A[:, 2 * b + m, j * P:(j + 1) * P], g.ident[:, :])
                    mm.then_inc(at_ps, 1)
                    if b >= 1:
                        result(b - 1)
                    norm_turn(pe, g, n1, b, g.ps[:, TB, :]).then_inc(xt_ps, 1)
                    pe.wait_ge(xt_ok, b + 1)
                    for j in range(2):
                        for k in range(KT):
                            mm = pe.matmul(g.ps[:, LB, j * NBLK:(j + 1) * NBLK], XT[b % 2][:, k, j * P:(j + 1) * P],
                                           WrT[:, k, :], start=(k == 0), stop=(k == KT - 1))
                    mm.then_inc(lg_ps, 1)
                    for n in range(UNITS):
                        u = UNITS * b + n
                        if u >= 2:
                            pe.wait_ge(gelu_ok, u - 1)
                        for o in range(2):
                            for k in range(KT):
                                mm = pe.matmul(g.ps[:, HB + u % 2, S * o:S * o + S],
                                               W1T[:, k, (2 * n + o) * P:(2 * n + o + 1) * P],
                                               XT[b % 2][:, k, :], start=(k == 0), stop=(k == KT - 1))
                        mm.then_inc(h_ps, 1)
                        if n >= 1:
                            mask(b, n - 1)
                    mask(b, UNITS - 1)
                    if b >= 1:
                        second_norm(b - 1)
                result(B - 1)
                second_norm(B - 1)

            @block.scalar
            def _(act):
                act.dma_start(ck[:, :, :], i["cosk"]).then_inc(d_rope, 16)
                act.dma_start(sk[:, :, :], i["sink"]).then_inc(d_rope, 16)
                for n, (name, at) in enumerate([("g_xattn", 0), ("g_xattn", 1), ("g_ffn", 0), ("g_ffn", 1),
                                                ("L0_xattn_gamma_raw", 0)]):
                    act.dma_start(raw[:, n:n + 1], i[name][at:at + 1].partition_broadcast(P)).then_inc(d_raw, 16)

                def bank(n):
                    act.wait_ge(filled, n + 1)
                    return g.ps[:, n % 4, :]
                for h in range(2):
                    act.activation(CTT[:, 512 * h:512 * h + 512], bank(h)[0:DC, :], ACT.Copy).then_inc(emptied, 1)
                act.activation(GT[:, :], bank(N_G)[0:DC, 0:DC], ACT.Copy).then_inc(emptied, 1)
                for h in range(2):
                    act.activation(V[:, 512 * h:512 * h + 512], bank(N_V + h)[0:DC, :], ACT.Copy,
                                   scale=1.0 / 16.0).then_inc(emptied, 1)
                for b in range(B):
                    o = bank(N_SIM + b)
                    act.activation(SIM[:, 2 * b:2 * b + 2, :], o, ACT.Copy).then_inc(sim_ok, 1)
                    act.activation(SIG[:, 2 * b:2 * b + 2, :], o, ACT.Sigmoid).then_inc(emptied, 1)
                act.wait_ge(d_raw, 80)
                act.activation(g.gate[:, 0:4], raw[:, 0:4], ACT.Tanh).then_inc(tanh_ok, 1)
                act.activation(gam[:, 0:1], raw[:, 4:5], ACT.Sigmoid).then_inc(tanh_ok, 1)
                norm_root(act, g, n0, 0)
                for k in range(KT):
                    for h in range(2):
                        act.activation(W1T[:, k, 512 * h:512 * h + 512], bank(N_W1 + 2 * k + h),
                                       ACT.Copy).then_inc(emptied, 1)
                for q in range(4):
                    act.activation(W2T[:, 2 * q:2 * q + 2, :], bank(N_W2 + q), ACT.Copy).then_inc(emptied, 1)
                act.activation(WrT[:, :, :], bank(N_WR)[:, 0:KT * NBLK], ACT.Copy).then_inc(emptied, 1)
                act.wait_ge(kd_zero, 2)
                for h in range(2):
                    o = bank(N_KV + h)
                    act.activation(g.KDH[0:DC, 2 * h:2 * h + 2, 0:S], o[0:DC, :], ACT.Copy, scale=-1.0)
                    act.activation(g.KDH[DC:P, 2 * h:2 * h + 2, S:2 * S], o[DC:P, :], ACT.Copy,
                                   scale=-1.0).then_inc(hi_ok, 1)
                for r in range(2):
                    for f in range(FOLDS):
                        fold_keep(act, g, r, r, f, bank(N_FOLD + FOLDS * r + f)).then_inc(
                            hi_ok if f in FOLD_SPLIT else emptied, 1)

                def unit(b, n):
                    u = UNITS * b + n
                    act.wait_ge(h_ps, u + 1)
                    if u >= 2:
                        act.wait_ge(ht_ok, u - 1)
                    act.activation(GL[u % 2][:, :, :], g.ps[:, HB + u % 2, :], ACT.Gelu).then_inc(gelu_ok, 1)
                    if n == 0 and b >= 1:
                        norm_root(act, g, n2, b - 1)
                    act.wait_ge(mask_ps, u + 1)
                    act.activation(MS[u % 2][:, :, :], g.ps[:, MB, :], ACT.Copy).then_inc(ms_ok, 1)

                def second_norm(b):
                    act.wait_ge(x2t_ps, b + 1)
                    act.activation(g.XH[:, :, S * b:S * b + S], g.ps[:, UB, :].rearrange("p (k s) -> p k s", k=KT),
                                   ACT.Copy).then_inc(xh_ok, 1)
                for b in range(B):
                    norm_root(act, g, n1, b)
                    act.wait_ge(xt_ps, b + 1)
                    act.activation(XT[b % 2][:, :, :], g.ps[:, TB, :], ACT.Copy).then_inc(xt_ok, 1)
                    for n in range(UNITS):
                        unit(b, n)
                    if b >= 1:
                        second_norm(b - 1)
                norm_root(act, g, n2, B - 1)
                second_norm(B - 1)

            @block.vector
            def _(dve):
                def first(b):
                    dve.wait_ge(at_ps, b + 1)
                    for j in range(2):
                        dve.tensor_tensor(A[:, 2 * b + j, :], A[:, 2 * b + j, :], g.ps[:, AB, S * j:S * j + S],
                                          ALU.add).then_inc(x1_ok, 1)
                    for j in range(2):
                        t = 2 * b + j
                        dve.wait_ge(x1_ok, t + 1)
                        if j == 0:
                            dve.wait_ge(xa_ok, t + 2)
                        dve.scalar_tensor_tensor(out=g.X[:, t, :], in0=A[:, t, :], scalar=gam[:, 3:4],
                                                 in1=XA[:, t, :], op0=ALU.mult, op1=ALU.add).then_inc(g.x_done, 1)
                    dve.wait_ge(g.x_done, 2 * b + 2)
                    norm_stats(dve, g, n1, b)

                def route(b):
                    t = slice(2 * b, 2 * b + 2)
                    dve.wait_ge(lg_ps, b + 1)
                    if b == 0:
                        dve.wait_ge(d_br, 16)
                        dve.wait_ge(lg_fill, 1)
                    dve.tensor_tensor(LG[:, t, FILL:], g.ps[:, LB, 0:2 * NBLK].rearrange("p (t n) -> p t n", t=2),
                                      br[:, :].unsqueeze(1).broadcast_to([P, 2, NBLK]), ALU.add).then_inc(lg_ok, 1)
                    dve.wait_ge(lg_ok, b + 1)
                    for j in range(2):
                        dve.max(M8[:, 2 * b + j, :], LG[:, 2 * b + j, :]).then_inc(top_ok, 1)
                    for j in range(2):
                        dve.wait_ge(top_ok, 2 * b + j + 1)
                        dve.match_replace(RP[:, 2 * b + j, :], M8[:, 2 * b + j, :], LG[:, 2 * b + j, :],
                                          NEG).then_inc(mark_ok, 1)
                    dve.wait_ge(mark_ok, 2 * b + 2)
                    dve.tensor_tensor(MK[:, t, :], LG[:, t, FILL:], RP[:, t, FILL:],
                                      ALU.not_equal).then_inc(mk_ok, 1)

                def second(b):
                    dve.wait_ge(y_ps, b + 1)
                    for j in range(2):
                        t = 2 * b + j
                        dve.scalar_tensor_tensor(out=g.X[:, t, :], in0=g.ps[:, YB, D * j:D * j + D],
                                                 scalar=g.gate[:, 2:3], in1=g.X[:, t, :], op0=ALU.mult,
                                                 op1=ALU.add).then_inc(x2_ok, 1)
                    dve.wait_ge(x2_ok, 2 * b + 2)
                    norm_stats(dve, g, n2, b)

                def rest(b):
                    dve.wait_ge(xh_ok, b + 1)
                    dve.tensor_tensor(g.XL[:, :, S * b:S * b + S], g.ps[:, UB, :].rearrange("p (k s) -> p k s", k=KT),
                                      g.XH[:, :, S * b:S * b + S], ALU.subtract).then_inc(xl_ok, 1)

                def kv_rest():
                    for h in range(2):
                        dve.wait_ge(hi_ok, h + 1)
                        o = g.ps[:, (N_KV + h) % 4, :]
                        for a, z in ((0, 0), (DC, S)):
                            m = dve.scalar_tensor_tensor(
                                out=g.KDL[a:a + DC, 2 * h:2 * h + 2, z:z + S],
                                in0=o[a:a + DC, :].rearrange("p (b s) -> p b s", b=2), scalar=-1.0,
                                in1=g.KDH[a:a + DC, 2 * h:2 * h + 2, z:z + S], op0=ALU.mult,
                                op1=ALU.subtract)
                        m.then_inc(split_ok, 1)

                def folds_rest(r):
                    for f in FOLD_SPLIT:
                        n = N_FOLD + FOLDS * r + f
                        dve.wait_ge(hi_ok, splits(n))
                        fold_rest(dve, g, r, r, f, g.ps[:, n % 4, :]).then_inc(split_ok, 1)

                def mixture():
                    dve.wait_ge(tanh_ok, 2)
                    dve.tensor_scalar(gam[:, 1:2], gam[:, 0:1], -1.0, 1.0, ALU.mult, ALU.add).then_inc(gam_ok, 1)
                    dve.tensor_scalar(gam[:, 3:4], gam[:, 0:1], g.gate[:, 0:1], 0.5, ALU.mult,
                                      ALU.mult).then_inc(gam_ok, 1)
                    norm_inverse(dve, g, n0, 0)
                    dve.wait_ge(gam_ok, 2)
                    dve.tensor_scalar(gam[:, 2:3], gam[:, 1:2], g.gate[:, 0:1], None, ALU.mult).then_inc(gam_ok, 1)
                    dve.wait_ge(gam_ok, 3)
                    dve.wait_ge(n0.rstd, 1)
                    dve.tensor_scalar(mix[:, 0, :], g.rstd[:, :], gam[:, 2:3], None, ALU.mult).then_inc(mix_ok, 1)
                    dve.wait_ge(mix_ok, 1)
                    dve.tensor_scalar(mix[:, 1, :], mix[:, 0, :], 1.0, None, ALU.add).then_inc(mix_ok, 1)
                    dve.tensor_tensor(mix[:, 2, :], g.mv[:, :, 0], mix[:, 0, :], ALU.mult).then_inc(mix_ok, 1)
                    dve.wait_ge(mix_ok, 3)
                    dve.tensor_scalar(mix[:, 2, :], mix[:, 2, :], -1.0, None, ALU.mult).then_inc(mix_ok, 1)

                dve.wait_ge(d_x, 32)
                norm_stats(dve, g, n0, 0)
                for b in range(B):
                    dve.wait_ge(sim_ok, b + 1)
                    for r in range(ROUNDS):
                        for j in range(2):
                            if r > 0:
                                dve.wait_ge(rep_ok, b * (ROUNDS - 1) * 2 + 2 * (r - 1) + j + 1)
                            src = SIM[:, 2 * b + j, :] if r == 0 else work[:, j, :]
                            dve.max(m8[:, j, r, :], src).then_inc(max_ok, 1)
                        if r < ROUNDS - 1:
                            for j in range(2):
                                dve.wait_ge(max_ok, b * ROUNDS * 2 + 2 * r + j + 1)
                                src = SIM[:, 2 * b + j, :] if r == 0 else work[:, j, :]
                                dve.match_replace(work[:, j, :], m8[:, j, r, :], src, NEG).then_inc(rep_ok, 1)
                        if b == 0 and r == 5:
                            mixture()
                        if b == 0 and r == 8:
                            kv_rest()
                        if b >= 3 and r == 1:
                            rest(b - 3)
                        if b >= 1 and r == 2:
                            first(b - 1)
                        if b >= 1 and r == 4:
                            norm_inverse(dve, g, n1, b - 1)
                            norm_apply(dve, g, n1, b - 1)
                        if b >= 2 and r == 5:
                            second(b - 2)
                        if b >= 1 and r == 6:
                            route(b - 1)
                        if b >= 2 and r == 8:
                            norm_inverse(dve, g, n2, b - 2)
                            norm_apply(dve, g, n2, b - 2)
                    last = (TOP_ADJ - 1) % 8
                    for j in range(2):
                        t = 2 * b + j
                        dve.wait_ge(max_ok, (b + 1) * ROUNDS * 2 - 1 + j)
                        if j == 0:
                            dve.wait_ge(emptied, plain(N_SIM + b))
                        dve.scalar_tensor_tensor(out=A[:, t, :], in0=SIM[:, t, :],
                                                 scalar=m8[:, j, ROUNDS - 1, last:last + 1],
                                                 in1=SIG[:, t, :], op0=ALU.is_ge, op1=ALU.mult).then_inc(a_ok, 1)
                    if b == 0:
                        folds_rest(0)
                        folds_rest(1)
                rest(B - 3)
                first(B - 1)
                norm_inverse(dve, g, n1, B - 1)
                norm_apply(dve, g, n1, B - 1)
                second(B - 2)
                route(B - 1)
                norm_inverse(dve, g, n2, B - 2)
                norm_apply(dve, g, n2, B - 2)
                rest(B - 2)
                second(B - 1)
                norm_inverse(dve, g, n2, B - 1)
                norm_apply(dve, g, n2, B - 1)
                rest(B - 1)


def stage_latent_attention(nc, g, i):
    with ExitStack() as ctx:
        sb = lambda name, shape, dt=F32: ctx.enter_context(nc.sbuf_tensor(name, shape, dt))
        sem = lambda name: ctx.enter_context(nc.semaphore(name))
        two = lambda name, shape: [sb(f"{name}{u}", shape) for u in range(2)]
        two16 = lambda name, shape: [sb(f"{name}{u}", shape, F16) for u in range(2)]
        TM = two("TM", [HALF, 4, 512])
        RO = sb("RO", [HALF, 2, 2, 2, 512])
        QH, QL = two16("QH", [P, T]), two16("QL", [P, T])
        low = sb("low", [P, 2, 2])
        PB = two("PB", [P, 2, S])
        tot = sb("tot", [P, 2, 2])
        inv = sb("inv", [P, 2, 2])
        PTS = two("PTS", [P, 4, 2 * P])
        XCH, XCL = sb("XCH", [P, PAIRS, T], F16), sb("XCL", [P, PAIRS, T], F16)
        out_gate = sb("out_gate", [P, 1])
        split = lambda ah, al, bh, bl: ((ah, bh), (ah, bl), (al, bh))
        QA, QP, SC, PTB, CXB, FO = 0, 2, 3, 5, 6, 7

        (q_ps, rope_ok, sum_ok, qc_ps, qc_ok, s_ps, low_ok, exp_ok, inv_ok, norm_ok, t_ps, t_ok, cx_ps, cx_ok,
         fold_ps, fold_ok, out_ps, credit, fold_hi, qc_hi, cx_hi, gate_ok) = map(sem, [
             "q_ps", "rope_ok", "sum_ok", "qc_ps", "qc_ok", "s_ps", "low_ok", "exp_ok", "inv_ok", "norm_ok",
             "t_ps", "t_ok", "cx_ps", "cx_ok", "fold_ps", "fold_ok", "out_ps", "credit", "fold_hi", "qc_hi",
             "cx_hi", "gate_ok"])
        n3 = Norm(sem, "n3", 2)
        EXP0, ROPE0, TPS0, TOK0, CXPS0, CXOK0, QC0, QCPS0, SUM0, FOLD0 = 2, 2, 2, 1, 2, 1, 1, 2, 4, 1
        DONE, NSPLIT = 2 * FOLDS, len(FOLD_SPLIT)
        starts = [(exp_ok, EXP0), (rope_ok, ROPE0), (t_ps, TPS0), (t_ok, TOK0), (cx_ps, CXPS0), (cx_ok, CXOK0),
                  (qc_ok, QC0), (qc_ps, QCPS0), (sum_ok, SUM0),
                  (fold_ok, DONE + FOLD0), (fold_ps, DONE), (fold_hi, 2 * NSPLIT)]

        def pairs(eng, body):
            with eng.Fori(0, (PAIRS - 2) // 2, 1) as it:
                for u in range(2):
                    body(it * 2 + u, u, True, True)
            body(PAIRS - 2, 0, False, True)
            body(PAIRS - 1, 1, False, False)

        with nc.Block() as block:
            @block.sync
            def _(sp):
                with sp.Fori(0, PAIRS // 2 - 2, 1) as it:
                    for u in range(2):
                        r = it * 2 + (4 + u)
                        sp.wait_ge(fold_ps, it * 12 + (DONE + 6 * (u + 1)))
                        load_pair(sp, g, i, r, u)

            @block.tensor
            def _(pe):
                def fold(r, u, f):
                    pe.wait_ge(fold_ok, 6 * r + (f + FOLD0))
                    if f == 0:
                        pe.wait_ge(g.d_w[u], (r + (2 - u)) * (DW // 2))
                    fold_product(pe, g, u, f, g.ps[:, FO, :]).then_inc(fold_ps, 1)

                def queries(q, u, t):
                    n, h, a = t // 4, t // 2 % 2, t % 2
                    pe.wait_ge(rope_ok, 8 * q + (t - 1 + ROPE0))
                    pe.wait_ge(fold_ok, 6 * q + (2 + FOLD0))
                    for k in range(KT):
                        for m, (cx, xx) in enumerate(split(g.CH[u], g.CL[u], g.XH, g.XL)):
                            mm = pe.matmul(g.ps[0:HALF, QA + a, :],
                                           cx[:, k, h * DQ + a * HALF:h * DQ + (a + 1) * HALF],
                                           xx[:, k, 512 * n:512 * n + 512], start=(k == 0 and m == 0),
                                           stop=(k == KT - 1 and m == 2))
                    mm.then_inc(q_ps, 1)

                def to_context(q, u, n):
                    pe.wait_ge(sum_ok, 8 * q + (4 * n + 4 + SUM0))
                    pe.wait_ge(fold_ok, 6 * q + (5 + FOLD0))
                    pe.wait_ge(qc_ok, 2 * q + (n + QC0))
                    for a in range(2):
                        for h in range(2):
                            mm = pe.matmul(g.ps[DC * h:DC * h + DC, QP, :], g.M[u][:, 2 * h + a, :],
                                           RO[:, n, h, a, :], start=(a == 0), stop=(a == 1))
                    mm.then_inc(qc_ps, 1)

                def scores(p, u, t):
                    pe.wait_ge(qc_ok, 2 * p + (t // 4 + 1 + QC0))
                    pe.wait_ge(exp_ok, 8 * p + (t - 1 + EXP0))
                    for m, (qx, kx) in enumerate(split(QH[u], QL[u], g.KDH, g.KDL)):
                        mm = pe.matmul(g.ps[:, SC + t % 2, :], qx[:, t * P:(t + 1) * P], kx[:, t // 2, :],
                                       start=(m == 0), stop=(m == 2))
                    mm.then_inc(s_ps, 1)

                def turn(p, t):
                    pe.wait_ge(norm_ok, 8 * p + (t + 1))
                    pe.wait_ge(t_ok, 8 * p + (t + TOK0))
                    for j in range(4):
                        mm = pe.transpose(g.ps[:, PTB, j * P:(j + 1) * P],
                                          PB[t % 2][:, j // 2, (j % 2) * P:(j % 2 + 1) * P], g.ident[:, :])
                    mm.then_inc(t_ps, 1)

                def attend(p, b):
                    pe.wait_ge(t_ok, 8 * p + (2 * b + 2 + TOK0))
                    pe.wait_ge(cx_ok, 4 * p + (b + CXOK0))
                    for j in range(2):
                        for h in range(2):
                            mm = pe.matmul(g.ps[DC * h:DC * h + DC, CXB, 0:S], g.KV[:, 2 * b + j, 0, :],
                                           PTS[b % 2][:, 2 * h + j, :], start=(j == 0), stop=(j == 1))
                    mm.then_inc(cx_ps, 1)

                def pair(p, u, folds, asks):
                    for t in range(NT):
                        scores(p, u, t)
                        if asks:
                            queries(p + 1, 1 - u, t)
                        if t == 1:
                            to_context(p, u, 1)
                        if folds and t < 6:
                            fold(p + 2, u, t)
                        if t >= 1:
                            turn(p, t - 1)
                        if t in (3, 5, 7):
                            attend(p, t // 2 - 1)
                    if asks:
                        to_context(p + 1, 1 - u, 0)
                    turn(p, NT - 1)
                    attend(p, B - 1)

                def turn_normed(q):
                    if q >= 2:
                        pe.wait_ge(g.xt, q - 1)
                    norm_turn(pe, g, n3, q, g.ps[:, 4 + q % 2, :]).then_inc(g.xt_ps, 1)

                pe.wait_ge(credit, 1)
                for t in range(NT):
                    queries(0, 0, t)
                to_context(0, 0, 0)
                pairs(pe, pair)
                for t in range(NT):
                    if t == 0:
                        pe.wait_ge(cx_ok, 4 * PAIRS + CXOK0)
                    if t >= 4:
                        pe.wait_ge(g.x_done, NT + t - 3)
                    for p in range(PAIRS):
                        for m, (xx, nx) in enumerate(split(XCH, XCL, g.NH, g.NL)):
                            mm = pe.matmul(g.ps[:, t % 4, 0:D], xx[:, p, t * P:(t + 1) * P], nx[:, p, :],
                                           start=(p == 0 and m == 0), stop=(p == PAIRS - 1 and m == 2))
                    mm.then_inc(out_ps, 1)
                    if t in (3, 5, 7):
                        turn_normed(t // 2 - 1)
                turn_normed(B - 1)

            @block.scalar
            def _(act):
                def fold(r, u, f):
                    act.wait_ge(fold_ps, 6 * r + (f + 1))
                    fold_keep(act, g, r, u, f, g.ps[:, FO, :]).then_inc(fold_hi if f in FOLD_SPLIT else fold_ok, 1)

                def to_context(q, u, n):
                    act.wait_ge(qc_ps, 2 * q + (n + 1 + QCPS0))
                    act.activation(QH[u][:, 512 * n:512 * n + 512], g.ps[:, QP, :], ACT.Copy).then_inc(qc_hi, 1)

                def softmax(p, t):
                    act.wait_ge(low_ok, 8 * p + (t + 1))
                    act.wait_ge(t_ps, 8 * p + (t - 1 + TPS0))
                    for h in range(2):
                        e = act.activation(PB[t % 2][:, h, :], g.ps[:, SC + t % 2, h * S:(h + 1) * S], ACT.Exp,
                                           bias=low[:, t % 2, h:h + 1], scale=-1.0,
                                           accum_out=tot[:, t % 2, h:h + 1])
                    e.then_inc(exp_ok, 1)

                def turned(p, t):
                    act.wait_ge(t_ps, 8 * p + (t + 1 + TPS0))
                    act.wait_ge(cx_ps, 4 * p + (t // 2 - 1 + CXPS0))
                    act.activation(PTS[t // 2 % 2][:, :, (t % 2) * P:(t % 2 + 1) * P],
                                   g.ps[:, PTB, :].rearrange("p (j n) -> p j n", j=4),
                                   ACT.Copy).then_inc(t_ok, 1)

                def attended(p, b):
                    act.wait_ge(cx_ps, 4 * p + (b + 1 + CXPS0))
                    act.activation(XCH[:, bass.ds(p, 1), S * b:S * b + S], g.ps[:, CXB, 0:S],
                                   ACT.Copy).then_inc(cx_hi, 1)

                def pair(p, u, folds, asks):
                    for t in range(NT):
                        softmax(p, t)
                        if t == 1:
                            to_context(p, u, 1)
                        if folds and t < 6:
                            fold(p + 2, u, t)
                        if t >= 1:
                            turned(p, t - 1)
                        if t in (3, 5, 7):
                            attended(p, t // 2 - 1)
                    if asks:
                        to_context(p + 1, 1 - u, 0)
                    turned(p, NT - 1)
                    attended(p, B - 1)

                act.wait_ge(credit, 1)
                to_context(0, 0, 0)
                pairs(act, pair)

                def turned_norm(q):
                    act.wait_ge(g.xt_ps, q + 1)
                    act.activation(g.XT[:, :, S * q:S * q + S],
                                   g.ps[:, 4 + q % 2, :].rearrange("p (k s) -> p k s", k=KT),
                                   ACT.Copy).then_inc(g.xt, 1)
                for q in range(B):
                    norm_root(act, g, n3, q)
                    if q >= 1:
                        turned_norm(q - 1)
                turned_norm(B - 1)

            @block.gpsimd
            def _(pool):
                for s, v in starts:
                    pool.sem_inc(s, v)
                pool.sem_inc(credit, 2)
                with pool.Fori(0, PAIRS, 1) as q:
                    for st in range(4):
                        n, h, tm = st // 2, st % 2, TM[st % 2]
                        pool.wait_ge(rope_ok, 8 * q + (2 * st + 2 + ROPE0))
                        pool.wait_ge(qc_ps, 2 * q + (n + QCPS0 - 1))
                        pool.tensor_tensor(RO[:, n, h, 0, :], tm[:, 0, :], tm[:, 2, :],
                                           ALU.subtract).then_inc(sum_ok, 1)
                        pool.tensor_tensor(RO[:, n, h, 1, :], tm[:, 3, :], tm[:, 1, :],
                                           ALU.add).then_inc(sum_ok, 1)
                for q in range(B):
                    norm_apply(pool, g, n3, q)

            @block.vector
            def _(dve):
                def rotate(q, t):
                    st, a = t // 2, t % 2
                    dve.wait_ge(q_ps, 8 * q + (t + 1))
                    dve.wait_ge(sum_ok, 8 * q + (2 * st - 2 + SUM0))
                    batches = lambda x: x.rearrange("p (b s) -> p b s", b=2)
                    over = lambda x: x.unsqueeze(1).broadcast_to([HALF, 2, S])
                    src = batches(g.ps[0:HALF, QA + a, :])
                    c, s = (0, 1) if a == 0 else (3, 2)
                    dve.tensor_tensor(batches(TM[st % 2][:, c, :]), src, over(g.cosq[:, a, :]), ALU.mult)
                    dve.tensor_tensor(batches(TM[st % 2][:, s, :]), src, over(g.sinq[:, 1 - a, :]),
                                      ALU.mult).then_inc(rope_ok, 1)

                def fold(r, u, f):
                    if f in FOLD_SPLIT:
                        dve.wait_ge(fold_hi, 3 * r + (FOLD_SPLIT.index(f) + 1))
                        fold_rest(dve, g, r, u, f, g.ps[:, FO, :]).then_inc(fold_ok, 1)

                def to_context(q, u, n):
                    dve.wait_ge(qc_hi, 2 * q + (n + 1))
                    cols = slice(512 * n, 512 * n + 512)
                    dve.tensor_tensor(QL[u][:, cols], g.ps[:, QP, :], QH[u][:, cols],
                                      ALU.subtract).then_inc(qc_ok, 1)

                def attended(p, b):
                    dve.wait_ge(cx_hi, 4 * p + (b + 1))
                    cols = slice(S * b, S * b + S)
                    dve.tensor_tensor(XCL[:, bass.ds(p, 1), cols], g.ps[:, CXB, 0:S],
                                      XCH[:, bass.ds(p, 1), cols], ALU.subtract).then_inc(cx_ok, 1)

                def pair(p, u, folds, asks):
                    for t in range(NT):
                        dve.wait_ge(s_ps, 8 * p + (t + 1))
                        dve.tensor_reduce(low[:, t % 2, :], g.ps[:, SC + t % 2, :].rearrange("p (h s) -> p h s", h=2),
                                          AX.X, ALU.min).then_inc(low_ok, 1)
                        if asks:
                            rotate(p + 1, t)
                        dve.wait_ge(exp_ok, 8 * p + (t + 1 + EXP0))
                        dve.reciprocal(inv[:, t % 2, :], tot[:, t % 2, :]).then_inc(inv_ok, 1)
                        dve.wait_ge(inv_ok, 8 * p + (t + 1))
                        for h in range(2):
                            m = dve.tensor_scalar(PB[t % 2][:, h, :], PB[t % 2][:, h, :],
                                                  inv[:, t % 2, h:h + 1], None, ALU.mult)
                        m.then_inc(norm_ok, 1)
                        if t == 1:
                            to_context(p, u, 1)
                        if folds and t < 6:
                            fold(p + 2, u, t)
                        if t in (3, 5, 7):
                            attended(p, t // 2 - 1)
                    if asks:
                        to_context(p + 1, 1 - u, 0)
                    attended(p, B - 1)

                dve.wait_ge(credit, 1)
                dve.wait_ge(g.d_ropeq, 32)
                dve.tensor_scalar(out_gate[:, :], g.gate[:, 1:2], 1.0 / UP, None, ALU.mult).then_inc(gate_ok, 1)
                for t in range(NT):
                    rotate(0, t)
                to_context(0, 0, 0)
                pairs(dve, pair)
                dve.wait_ge(gate_ok, 1)
                for t in range(NT):
                    dve.wait_ge(out_ps, t + 1)
                    dve.scalar_tensor_tensor(out=g.X[:, t, :], in0=g.ps[:, t % 4, 0:D], scalar=out_gate[:, 0:1],
                                             in1=g.X[:, t, :], op0=ALU.mult, op1=ALU.add).then_inc(g.x_done, 1)
                    if t % 2 == 1:
                        dve.wait_ge(g.x_done, NT + t + 1)
                        norm_stats(dve, g, n3, t // 2)
                        norm_inverse(dve, g, n3, t // 2)


def stage_moe(nc, g, i, out):
    with ExitStack() as ctx:
        sb = lambda name, shape, dt=F32: ctx.enter_context(nc.sbuf_tensor(name, shape, dt))
        sem = lambda name: ctx.enter_context(nc.semaphore(name))
        RING = 5
        GF, EF = 8 - TOP_G, 8 - TOP_E
        EP = ST_T * EPT
        shw = sb("shw", [P, 3, KT, SHARED])
        shT = sb("shT", [P, 3, KT, SHARED])
        rw = sb("rw", [E, D])
        rwT = sb("rwT", [P, KT, E])
        eb = sb("eb", [P, E])
        EG = [sb(f"EG{n}", [P, EPT, KT, EI]) for n in range(RING)]
        EU = [sb(f"EU{n}", [P, EPT, KT, EI]) for n in range(RING)]
        ED = [sb(f"ED{n}", [P, EPT, D]) for n in range(RING)]
        XP = sb("XP", [P, 3, NT, D], BF16)
        SG = sb("SG", [P, NT, E])
        SBI = sb("SBI", [P, NT, E])
        hl = sb("hl", [P, 2, NT * GROUPS, 2])
        tp = sb("tp", [P, 4, NT * GROUPS])
        GB = sb("GB", [P, NT, GF + GROUPS])
        GR = sb("GR", [P, NT, GF + GROUPS])
        g8 = sb("g8", [P, NT, 8])
        gm = sb("gm", [P, NT, GROUPS])
        mz = sb("mz", [P, NT, E])
        MB = sb("MB", [P, NT, EF + E])
        MR = sb("MR", [P, NT, EF + E])
        e8 = sb("e8", [P, NT, 8])
        MK = sb("MKE", [P, NT, E])
        MKb = sb("MKb", [P, NT, E], BF16)
        wsel = sb("wsel", [P, NT, E])
        wsum = sb("wsum", [P, 3, NT])
        W = sb("W", [P, NT, E])
        WR_ = sb("WR_", [P, NT, E])
        WP = sb("WP", [P, NT, 3, EP], BF16)
        place = sb("place", [P, NT, E])
        ioti = sb("ioti", [P, CAP], mybir.dt.int32)
        iotf = sb("iotf", [P, CAP])
        tri = sb("tri", [P, P], BF16)
        ones = sb("ones", [P, P], BF16)
        own = sb("own", [P, EPT])
        SM = sb("SM", [P, NT, E * CAP], BF16)
        STT = sb("STT", [P, ST_T, T], BF16)
        ws = sb("ws", [P, ST_T, 3, EPT])
        wslot = sb("wslot", [P, ST_T])
        XG = sb("XG", [P, KT, E * CAP])
        SL = [sb(f"SL{u}", [P, 512]) for u in range(2)]
        HS = sb("HS", [P, KT, T])
        SE = [sb(f"SE{u}", [P, SLOTS]) for u in range(2)]
        HP = [sb(f"HP{u}", [P, EPT, SLOTS + CAP]) for u in range(2)]
        YW = [sb(f"YW{u}", [P, D]) for u in range(2)]
        YR = [sb(f"YR{u}", [P, D]) for u in range(2)]
        YP = sb("YP", [P, ST_T, 3, D], BF16)
        XR = YP[:, :, :, :].rearrange("p n a d -> p (n a d)")[:, 0:2 * NT * D].bitcast(F32).rearrange(
            "p (t d) -> p t d", t=NT)

        count = lambda n: min(EPT, E - EPT * n)
        d_sh, d_r, d_eb, stored = map(sem, ["d_sh", "d_r", "d_eb", "stored"])
        d_e = [sem(f"d_e{n}") for n in range(RING)]
        (c_fill, iota_ok, iotf_ok, tri0, tri_ok, own_ok, filled, emptied, rl_ps, sg_ok, gu_sh, sl_ok, hs_ok) = map(
            sem, ["c_fill", "iota_ok", "iotf_ok", "tri0", "tri_ok", "own_ok", "filled2", "emptied2", "rl_ps",
                  "sg_ok", "gu_sh", "sl_ok", "hs_ok"])
        (rt, mk_ok, w_ok, wp_a, wp_r, wp_b, cnt_ps, place_ok, s_ok, xp_a, xp_r, xp_b, xp_c, xg_ps, xg_ok, ws_ps,
         ws_ok) = map(
            sem, ["rt", "mk_ok2", "w_ok", "wp_a", "wp_r", "wp_b", "cnt_ps", "place_ok", "s_ok", "xp_a", "xp_r",
                  "xp_b", "xp_c", "xg_ps", "xg_ok", "ws_ps", "ws_ok"])
        (gu_ps, se_ok, hp_ok, st_ps, st_ok, y_ps, yw_ok, yh_ok, yr_ok, ym_ok, yl_ok, acc_ps, fin_ok, hp0) = map(
            sem, ["gu_ps", "se_ok", "hp_ok", "st_ps", "st_ok", "y_ps2", "yw_ok", "yh_ok", "yr_ok", "ym_ok", "yl_ok",
                  "acc_ps", "fin_ok", "hp0"])

        chunks = [(0, 11 * CAP), (11 * CAP, 22 * CAP), (22 * CAP, E * CAP)]
        gathers = [(k, c) for k in range(KT) for c in range(3)]
        GBANK = [0, 1, 2, 3, 6, 7]
        GU, Y, STB, ACC = 0, 2, 6, 4
        shared_steps = [(h, o) for h in range(2) for o in range(KT)]
        out_v = out.rearrange("b (t p) d -> p (b t) d", p=P)

        with nc.Block() as block:
            @block.sync
            def _(sp):
                for n, name in enumerate(["L1_ffn_shared_gate", "L1_ffn_shared_up", "L1_ffn_shared_down"]):
                    sp.dma_start(shw[:, n, :, :], i[name].rearrange("(c p) n -> p c n", p=P)).then_inc(d_sh, 16)
                sp.dma_start(rw[:, :], i["L1_ffn_router_w"]).then_inc(d_r, 16)
                sp.dma_start(eb[:, :], i["L1_ffn_e_bias"].partition_broadcast(P)).then_inc(d_eb, 16)
                for n in range(ST_T):
                    c, r = count(n), n % RING
                    if n >= RING:
                        sp.wait_ge(y_ps, n - RING + 1)
                    es = slice(EPT * n, EPT * n + c)
                    sp.dma_start(EG[r][:, 0:c], i["L1_ffn_W_gate"][es].rearrange("e (k p) n -> p e k n", p=P)
                                 ).then_inc(d_e[r], 16)
                    sp.dma_start(EU[r][:, 0:c], i["L1_ffn_W_up"][es].rearrange("e (k p) n -> p e k n", p=P)
                                 ).then_inc(d_e[r], 16)
                    sp.dma_start(ED[r][:, 0:c], i["L1_ffn_W_down"][es].rearrange("e p n -> p e n")
                                 ).then_inc(d_e[r], 16)
                for b in range(B):
                    sp.wait_ge(fin_ok, 2 * b + 2)
                    sp.dma_start(out_v[:, 2 * b:2 * b + 2, :], g.X[:, 2 * b:2 * b + 2, :]).then_inc(stored, 16)
                sp.wait_ge(stored, 16 * B)

            @block.gpsimd
            def _(pool):
                pool.memset(GB[:, :, 0:GF], BIG).then_inc(c_fill, 1)
                pool.memset(MB[:, :, 0:EF], BIG).then_inc(c_fill, 1)
                pool.memset(WP[:, :, :, E:EP], 0.0).then_inc(c_fill, 1)
                pool.iota(ioti[:, :], [[1, CAP]], base=1, channel_multiplier=0).then_inc(iota_ok, 1)
                pool.memset(ones[:, :], 1.0).then_inc(tri0, 1)
                pool.memset(tri[:, :], 1.0).then_inc(tri0, 1)
                pool.wait_ge(iota_ok, 1)
                pool.tensor_copy(iotf[:, :], ioti[:, :]).then_inc(iotf_ok, 1)
                pool.wait_ge(tri0, 2)
                pool.affine_select(out=tri[:, :], in_=tri[:, :], compare_op=ALU.is_gt, fill=0.0, base=0,
                                   pattern=[[1, P]], channel_multiplier=-1).then_inc(tri_ok, 1)
                for u in range(2):
                    pool.memset(HP[u][:, :, :], 0.0).then_inc(hp0, 1)
                for h in range(2):
                    t = slice(4 * h, 4 * h + 4)
                    pool.wait_ge(xp_a, h + 1)
                    pool.tensor_tensor(XR[:, t, :], g.XN[:, t, :], XP[:, 0, t, :], ALU.subtract).then_inc(xp_r, 1)
                for h in range(2):
                    t = slice(4 * h, 4 * h + 4)
                    pool.wait_ge(xp_b, h + 1)
                    pool.tensor_tensor(XP[:, 2, t, :], XR[:, t, :], XP[:, 1, t, :], ALU.subtract).then_inc(xp_c, 1)
                pool.wait_ge(wp_a, 1)
                pool.tensor_tensor(WR_[:, :, :], W[:, :, :], WP[:, :, 0, 0:E], ALU.subtract).then_inc(wp_r, 1)
                pool.wait_ge(wp_b, 1)
                pool.tensor_tensor(WP[:, :, 2, 0:E], WR_[:, :, :], WP[:, :, 1, 0:E], ALU.subtract).then_inc(wp_b, 1)
                for n in range(ST_T):
                    m = CAP * count(n)
                    pool.wait_ge(yh_ok, n + 1)
                    if n >= 2:
                        pool.wait_ge(yl_ok, n - 1)
                    pool.tensor_tensor(YR[n % 2][0:m, :], YW[n % 2][0:m, :], YP[0:m, n, 0, :],
                                       ALU.subtract).then_inc(yr_ok, 1)

            @block.tensor
            def _(pe):
                pe.wait_ge(d_sh, 48)
                for n in range(3):
                    for k in range(KT):
                        for c in range(KT):
                            mm = pe.transpose(g.ps[:, 4 + n, (KT * k + c) * P:(KT * k + c + 1) * P],
                                              shw[:, n, c, k * P:(k + 1) * P], g.ident[:, :])
                    mm.then_inc(filled, 1)
                pe.wait_ge(d_r, 16)
                for k in range(KT):
                    mm = pe.transpose(g.ps[:, 7, k * E:(k + 1) * E], rw[:, k * P:(k + 1) * P], g.ident[0:E, 0:E])
                mm.then_inc(filled, 1)
                pe.wait_ge(emptied, 4)
                for t in range(NT):
                    for k in range(KT):
                        mm = pe.matmul(g.ps[:, 4, t * E:(t + 1) * E], g.XT[:, k, t * P:(t + 1) * P], rwT[:, k, :],
                                       start=(k == 0), stop=(k == KT - 1))
                mm.then_inc(rl_ps, 1)
                for n, (h, o) in enumerate(shared_steps):
                    if n >= 2:
                        pe.wait_ge(hs_ok, n - 1)
                    for w in range(2):
                        for k in range(KT):
                            mm = pe.matmul(g.ps[:, 2 * (n % 2) + w, :], shT[:, w, k, o * P:(o + 1) * P],
                                           g.XT[:, k, 512 * h:512 * h + 512], start=(k == 0), stop=(k == KT - 1))
                    mm.then_inc(gu_sh, 1)
                pe.wait_ge(mk_ok, 2)
                pe.wait_ge(tri_ok, 1)
                for t in range(NT):
                    for m in range(t + 1):
                        mm = pe.matmul(g.ps[:, 5, t * E:(t + 1) * E], (tri if m == t else ones)[:, :],
                                       MKb[:, m, :], start=(m == 0), stop=(m == t))
                mm.then_inc(cnt_ps, 1)
                pe.wait_ge(hs_ok, 4)
                pe.wait_ge(xp_b, 2)
                pe.wait_ge(xp_c, 2)
                for t in range(NT):
                    pe.wait_ge(s_ok, t + 1)
                    for (k, c), bank in zip(gathers, GBANK):
                        a, z = chunks[c]
                        for part in range(3):
                            mm = pe.matmul(g.ps[:, bank, 0:z - a], XP[:, part, t, k * P:(k + 1) * P],
                                           SM[:, t, a:z], start=(t == 0 and part == 0),
                                           stop=(t == NT - 1 and part == 2))
                mm.then_inc(xg_ps, 1)
                pe.wait_ge(wp_b, 2)
                pe.wait_ge(c_fill, 3)
                for n in range(ST_T):
                    m = CAP * count(n)
                    for t in range(NT):
                        mm = pe.matmul(g.ps[0:m, 4, 9 * n:9 * n + 9], SM[:, t, SLOTS * n:SLOTS * n + m],
                                       WP[:, t, :, EPT * n:EPT * n + EPT], start=(t == 0), stop=(t == NT - 1))
                mm.then_inc(ws_ps, 1)

                def gate_up(n):
                    r = n % RING
                    pe.wait_ge(d_e[r], 48 * (n // RING + 1))
                    if n >= 2:
                        pe.wait_ge(hp_ok, n - 1)
                    for j in range(count(n)):
                        xs = slice((EPT * n + j) * CAP, (EPT * n + j + 1) * CAP)
                        for w, wt in enumerate((EG[r], EU[r])):
                            for k in range(KT):
                                mm = pe.matmul(g.ps[:, GU + n % 2, w * SLOTS + j * CAP:w * SLOTS + (j + 1) * CAP],
                                               wt[:, j, k, :], XG[:, k, xs], start=(k == 0), stop=(k == KT - 1))
                    mm.then_inc(gu_ps, 1)

                def turn(n):
                    m = CAP * count(n)
                    if n >= 2:
                        pe.wait_ge(st_ok, n - 1)
                    o = g.ps[0:m, STB + n % 2, :].bitcast(BF16)
                    for t in range(NT):
                        mm = pe.transpose(o[:, t * P:(t + 1) * P], SM[:, t, SLOTS * n:SLOTS * n + m],
                                          g.identb[:, :])
                    mm.then_inc(st_ps, 1)

                def down(n):
                    m = CAP * count(n)
                    pe.wait_ge(hp_ok, n + 1)
                    if n >= 2:
                        pe.wait_ge(yw_ok, n - 1)
                    flat = HP[n % 2][:, :, :].rearrange("p j w -> p (j w)")
                    for j in range(count(n)):
                        mm = pe.matmul(g.ps[0:m, Y + n % 2, 0:D], flat[:, SLOTS * j:SLOTS * j + m],
                                       ED[n % RING][:, j, :], start=(j == 0), stop=(j == count(n) - 1))
                    mm.then_inc(y_ps, 1)

                pe.wait_ge(xg_ok, 6)
                for n in range(ST_T):
                    gate_up(n)
                    turn(n)
                    if n >= 1:
                        down(n - 1)
                pe.wait_ge(st_ok, ST_T)
                pe.wait_ge(ws_ok, 1)
                acc = lambda t: g.ps[:, ACC + t // 2, D * (t % 2):D * (t % 2) + D]
                for t in range(NT):
                    for k in range(KT):
                        pe.matmul(acc(t), HS[:, k, t * P:(t + 1) * P], shT[:, 2, k, :],
                                  start=(t % 2 == 0 and k == 0), stop=False, skip_group_check=True)
                down(ST_T - 1)

                def scatter(t, n):
                    m = CAP * count(n)
                    for part in range(3):
                        mm = pe.matmul(acc(t), STT[0:m, n, t * P:(t + 1) * P], YP[0:m, n, part, :], start=False,
                                       stop=(n == ST_T - 1 and part == 2), skip_group_check=True)
                    return mm
                pe.wait_ge(yl_ok, ST_T - 1)
                for t in range(NT):
                    for n in range(ST_T - 1):
                        scatter(t, n)
                pe.wait_ge(yl_ok, ST_T)
                for t in range(NT):
                    mm = scatter(t, ST_T - 1)
                    if t % 2 == 1:
                        mm.then_inc(acc_ps, 1)

            @block.scalar
            def _(act):
                for n in range(3):
                    act.wait_ge(filled, n + 1)
                    act.activation(shT[:, n, :, :], g.ps[:, 4 + n, :], ACT.Copy).then_inc(emptied, 1)
                act.wait_ge(filled, 4)
                act.activation(rwT[:, :, :], g.ps[:, 7, 0:KT * E], ACT.Copy).then_inc(emptied, 1)
                act.wait_ge(rl_ps, 1)
                act.activation(SG[:, :, :], g.ps[:, 4, 0:NT * E], ACT.Sigmoid).then_inc(sg_ok, 1)
                for h in range(2):
                    act.activation(XP[:, 0, 4 * h:4 * h + 4, :], g.XN[:, 4 * h:4 * h + 4, :],
                                   ACT.Copy).then_inc(xp_a, 1)
                for n in range(len(shared_steps)):
                    act.wait_ge(gu_sh, n + 1)
                    if n >= 2:
                        act.wait_ge(hs_ok, n - 1)
                    act.activation(SL[n % 2][:, :], g.ps[:, 2 * (n % 2), :], ACT.Silu).then_inc(sl_ok, 1)
                for h in range(2):
                    act.wait_ge(xp_r, h + 1)
                    act.activation(XP[:, 1, 4 * h:4 * h + 4, :], XR[:, 4 * h:4 * h + 4, :],
                                   ACT.Copy).then_inc(xp_b, 1)
                act.wait_ge(w_ok, 1)
                act.activation(WP[:, :, 0, 0:E], W[:, :, :], ACT.Copy).then_inc(wp_a, 1)
                act.wait_ge(wp_r, 1)
                act.activation(WP[:, :, 1, 0:E], WR_[:, :, :], ACT.Copy).then_inc(wp_b, 1)
                act.wait_ge(xg_ps, 1)
                for n, ((k, c), bank) in enumerate(zip(gathers, GBANK)):
                    if n % 2 == 0:
                        a, z = chunks[c]
                        act.activation(XG[:, k, a:z], g.ps[:, bank, 0:z - a], ACT.Copy).then_inc(xg_ok, 1)

                def results(n):
                    m = CAP * count(n)
                    act.wait_ge(y_ps, n + 1)
                    if n == 0:
                        act.wait_ge(ws_ok, 1)
                    if n >= 2:
                        act.wait_ge(yr_ok, n - 1)
                    act.activation(YW[n % 2][0:m, :], g.ps[0:m, Y + n % 2, 0:D], ACT.Copy,
                                   scale=wslot[0:m, n:n + 1]).then_inc(yw_ok, 1)
                    act.wait_ge(yw_ok, n + 1)
                    act.activation(YP[0:m, n, 0, :], YW[n % 2][0:m, :], ACT.Copy).then_inc(yh_ok, 1)

                def second(n):
                    m = CAP * count(n)
                    act.wait_ge(yr_ok, n + 1)
                    act.activation(YP[0:m, n, 1, :], YR[n % 2][0:m, :], ACT.Copy).then_inc(ym_ok, 1)

                for n in range(ST_T):
                    m = CAP * count(n)
                    act.wait_ge(gu_ps, n + 1)
                    if n >= 2:
                        act.wait_ge(hp_ok, n - 1)
                    act.activation(SE[n % 2][:, 0:m], g.ps[:, GU + n % 2, 0:m], ACT.Silu).then_inc(se_ok, 1)
                    if n % 2 == 0:
                        act.wait_ge(st_ps, n + 1)
                        act.wait_ge(st_ok, n)
                        act.activation(STT[0:m, n, :], g.ps[0:m, STB, :].bitcast(BF16), ACT.Copy).then_inc(st_ok, 1)
                    if n >= 2:
                        second(n - 2)
                    if n >= 1:
                        results(n - 1)
                second(ST_T - 2)
                results(ST_T - 1)
                second(ST_T - 1)

            @block.vector
            def _(dve):
                steps = 0

                def link(ins):
                    nonlocal steps
                    steps += 1
                    ins.then_inc(rt, 1)
                    dve.wait_ge(rt, steps)

                id3 = g.ident[:, 0:SLOTS].rearrange("p (j c) -> p j c", j=EPT)
                dve.tensor_reduce(own[:, :], id3, AX.X, ALU.add).then_inc(own_ok, 1)
                dve.wait_ge(d_eb, 16)
                dve.wait_ge(sg_ok, 1)
                link(dve.tensor_tensor(SBI[:, :, :], SG[:, :, :], eb[:, :].unsqueeze(1).broadcast_to([P, NT, E]),
                                       ALU.add))
                four = SBI[:, :, :].rearrange("p t (g a b) -> p (t g) a b", a=2, b=2)
                dve.tensor_tensor(hl[:, 0, :, :], four[:, :, :, 0], four[:, :, :, 1], ALU.max)
                link(dve.tensor_tensor(hl[:, 1, :, :], four[:, :, :, 0], four[:, :, :, 1], ALU.min))
                dve.tensor_tensor(tp[:, 0, :], hl[:, 0, :, 0], hl[:, 0, :, 1], ALU.max)
                dve.tensor_tensor(tp[:, 1, :], hl[:, 0, :, 0], hl[:, 0, :, 1], ALU.min)
                link(dve.tensor_tensor(tp[:, 2, :], hl[:, 1, :, 0], hl[:, 1, :, 1], ALU.max))
                link(dve.tensor_tensor(tp[:, 3, :], tp[:, 1, :], tp[:, 2, :], ALU.max))
                dve.wait_ge(c_fill, 3)
                tg = lambda x: x.rearrange("p (t g) -> p t g", t=NT)
                link(dve.tensor_tensor(GB[:, :, GF:], tg(tp[:, 0, :]), tg(tp[:, 3, :]), ALU.add))
                for t in range(NT):
                    last = dve.max(g8[:, t, :], GB[:, t, :])
                    if t < NT - 1:
                        last.then_inc(own_ok, 1)
                link(last)
                dve.wait_ge(own_ok, NT)
                for t in range(NT):
                    last = dve.match_replace(GR[:, t, :], g8[:, t, :], GB[:, t, :], NEG)
                    if t < NT - 1:
                        last.then_inc(own_ok, 1)
                link(last)
                dve.wait_ge(own_ok, 2 * NT - 1)
                link(dve.tensor_tensor(gm[:, :, :], GB[:, :, GF:], GR[:, :, GF:], ALU.not_equal))
                sp4 = lambda x: x.rearrange("p t (g a) -> p t g a", a=GE)
                link(dve.tensor_tensor(sp4(mz[:, :, :]), sp4(SBI[:, :, :]),
                                       gm[:, :, :].unsqueeze(3).broadcast_to([P, NT, GROUPS, GE]), ALU.mult))
                link(dve.tensor_scalar(MB[:, :, EF:], mz[:, :, :], 0.0, None, ALU.add))
                for t in range(NT):
                    last = dve.max(e8[:, t, :], MB[:, t, :])
                    if t < NT - 1:
                        last.then_inc(own_ok, 1)
                link(last)
                dve.wait_ge(own_ok, 3 * NT - 2)
                for t in range(NT):
                    last = dve.match_replace(MR[:, t, :], e8[:, t, :], MB[:, t, :], NEG)
                    if t < NT - 1:
                        last.then_inc(own_ok, 1)
                link(last)
                dve.wait_ge(own_ok, 4 * NT - 3)
                dve.tensor_tensor(MKb[:, :, :], MB[:, :, EF:], MR[:, :, EF:], ALU.not_equal).then_inc(mk_ok, 1)
                dve.tensor_tensor(MK[:, :, :], MB[:, :, EF:], MR[:, :, EF:], ALU.not_equal).then_inc(mk_ok, 1)
                dve.wait_ge(mk_ok, 2)
                link(dve.tensor_tensor(wsel[:, :, :], SG[:, :, :], MK[:, :, :], ALU.mult))
                link(dve.tensor_reduce(wsum[:, 0, :], wsel[:, :, :], AX.X, ALU.add))
                link(dve.tensor_scalar(wsum[:, 1, :], wsum[:, 0, :], 1e-20, None, ALU.add))
                link(dve.reciprocal(wsum[:, 2, :], wsum[:, 1, :]))
                link(dve.tensor_tensor(WR_[:, :, :], wsel[:, :, :],
                                       wsum[:, 2, :].unsqueeze(2).broadcast_to([P, NT, E]), ALU.mult))
                dve.tensor_scalar(W[:, :, :], WR_[:, :, :], ROUTE_SCALE, None, ALU.mult).then_inc(w_ok, 1)

                def shared(n):
                    h, o = shared_steps[n]
                    dve.wait_ge(sl_ok, n + 1)
                    dve.tensor_tensor(HS[:, o, 512 * h:512 * h + 512], SL[n % 2][:, :],
                                      g.ps[:, 2 * (n % 2) + 1, :], ALU.mult).then_inc(hs_ok, 1)
                for n in range(len(shared_steps)):
                    shared(n)
                dve.wait_ge(cnt_ps, 1)
                dve.scalar_tensor_tensor(out=place[:, :, :],
                                         in0=g.ps[:, 5, 0:NT * E].rearrange("p (t e) -> p t e", t=NT),
                                         scalar=1.0, in1=MK[:, :, :], op0=ALU.add,
                                         op1=ALU.mult).then_inc(place_ok, 1)
                dve.wait_ge(place_ok, 1)
                dve.wait_ge(iotf_ok, 1)
                for t in range(NT):
                    dve.tensor_tensor(SM[:, t, :].rearrange("p (e c) -> p e c", c=CAP),
                                      place[:, t, :].unsqueeze(2).broadcast_to([P, E, CAP]),
                                      iotf[:, :].unsqueeze(1).broadcast_to([P, E, CAP]),
                                      ALU.is_equal).then_inc(s_ok, 1)
                dve.wait_ge(xg_ps, 1)
                for n, ((k, c), bank) in enumerate(zip(gathers, GBANK)):
                    if n % 2 == 1:
                        a, z = chunks[c]
                        dve.tensor_copy(XG[:, k, a:z], g.ps[:, bank, 0:z - a]).then_inc(xg_ok, 1)
                dve.wait_ge(ws_ps, 1)
                link(dve.tensor_tensor(ws[0:SLOTS].rearrange("p n a j -> p (n a) j"),
                                       g.ps[0:SLOTS, 4, 0:9 * ST_T].rearrange("p (n j) -> p n j", j=EPT),
                                       own[0:SLOTS, :].unsqueeze(1).broadcast_to([SLOTS, 3 * ST_T, EPT]), ALU.mult))
                dve.tensor_reduce(wslot[0:SLOTS, :], ws[0:SLOTS].rearrange("p n a j -> p n (a j)"), AX.X,
                                  ALU.add).then_inc(ws_ok, 1)

                def third(n):
                    m = CAP * count(n)
                    dve.wait_ge(ym_ok, n + 1)
                    dve.tensor_tensor(YP[0:m, n, 2, :], YR[n % 2][0:m, :], YP[0:m, n, 1, :],
                                      ALU.subtract).then_inc(yl_ok, 1)
                dve.wait_ge(hp0, 2)
                for n in range(ST_T):
                    m = CAP * count(n)
                    dve.wait_ge(se_ok, n + 1)
                    if n >= 2:
                        dve.wait_ge(y_ps, n - 1)
                    c = count(n)
                    dve.tensor_tensor(HP[n % 2][:, 0:c, 0:CAP],
                                      SE[n % 2][:, 0:m].rearrange("p (j w) -> p j w", j=c),
                                      g.ps[:, GU + n % 2, SLOTS:SLOTS + m].rearrange("p (j w) -> p j w", j=c),
                                      ALU.mult).then_inc(hp_ok, 1)
                    if n % 2 == 1:
                        dve.wait_ge(st_ps, n + 1)
                        dve.wait_ge(st_ok, n)
                        dve.tensor_copy(STT[0:m, n, :], g.ps[0:m, STB + 1, :].bitcast(BF16)).then_inc(st_ok, 1)
                    if n >= 3:
                        third(n - 3)
                for n in range(ST_T - 3, ST_T):
                    third(n)
                for b in range(B):
                    dve.wait_ge(acc_ps, b + 1)
                    for t in (2 * b, 2 * b + 1):
                        dve.scalar_tensor_tensor(out=g.X[:, t, :], in0=g.ps[:, ACC + b, D * (t % 2):D * (t % 2) + D],
                                                 scalar=g.gate[:, 3:4], in1=g.X[:, t, :], op0=ALU.mult,
                                                 op1=ALU.add).then_inc(fin_ok, 1)


def store_x(nc, g, out):
    with nc.semaphore("stored") as stored, nc.Block() as block:
        @block.sync
        def _(sp):
            sp.dma_start(out.rearrange("b (t p) d -> p (b t) d", p=P), g.X[:, :, :]).then_inc(stored, 16)
            sp.wait_ge(stored, 16)


def build(nc, i, out, stages=4):
    g = Shared()
    with ExitStack() as ctx:
        sb = lambda name, shape, dt=F32: ctx.enter_context(nc.sbuf_tensor(name, shape, dt))
        sem = lambda name: ctx.enter_context(nc.semaphore(name))
        g.ps = ctx.enter_context(nc.psum_tensor("ps", [P, 8, 512], F32))
        g.X = sb("X", [P, NT, D])
        g.XN = sb("XN", [P, NT, D])
        g.XT = sb("XT", [P, KT, T])
        g.stat, g.mv = sb("stat", [P, NT, 6]), sb("mv", [P, NT, 2])
        g.var, g.std, g.rstd = sb("var", [P, NT]), sb("std", [P, NT]), sb("rstd", [P, NT])
        g.ident, g.identb = sb("ident", [P, P]), sb("identb", [P, P], BF16)
        g.gate = sb("gate", [P, 4])
        g.xt_ps, g.xt = sem("xt_ps3"), sem("xt3")
        g.d_ropeq = sem("d_ropeq")
        g.x_done = sem("x_done")
        with ExitStack() as middle:
            mb = lambda name, shape, dt=F32: middle.enter_context(nc.sbuf_tensor(name, shape, dt))
            g.cosq, g.sinq = mb("cosq", [HALF, 2, S]), mb("sinq", [HALF, 2, S])
            g.KV = mb("KV", [P, NT, 2, DC])
            g.KDH, g.KDL = mb("KDH", [P, B, 2 * S], F16), mb("KDL", [P, B, 2 * S], F16)
            g.XH, g.XL = mb("XH", [P, KT, T], F16), mb("XL", [P, KT, T], F16)
            two = lambda name, shape, dt=F32: [mb(f"{name}{u}", shape, dt) for u in range(2)]
            g.WQ, g.WCQ, g.WCV = two("WQ", [P, 2, D]), two("WCQ", [P, 2, DQ]), two("WCV", [P, 2, DC])
            g.WQR, g.WKR, g.WO = two("WQR", [HALF, 2, 2, R]), two("WKR", [DC, 2, R]), two("WO", [P, KT, 2 * HK])
            g.RT = mb("RT", [R, 2, 2 * HALF + DC])
            g.WOT = mb("WOT", [P, 2, D])
            g.CH, g.CL = two("CH", [P, KT, 2 * DQ], F16), two("CL", [P, KT, 2 * DQ], F16)
            g.M = two("M", [HALF, 4, DC])
            g.NH, g.NL = mb("NH", [P, PAIRS, D], F16), mb("NL", [P, PAIRS, D], F16)
            g.d_w = [sem("d_w_even"), sem("d_w_odd")]
            stage_first_layer(nc, g, i)
            if stages >= 3:
                stage_latent_attention(nc, g, i)
        if stages >= 4:
            stage_moe(nc, g, i, out)
        else:
            store_x(nc, g, out)


_INS = ["x", "ctx_512", "g_xattn", "g_ffn", "L0_xattn_Wq", "L0_xattn_Wk", "L0_xattn_gamma_raw", "L0_ffn_Wr",
        "L0_ffn_br", "L0_ffn_W1", "L0_ffn_W2", "L1_xattn_Wq", "L1_xattn_w_kc_q", "L1_xattn_w_kc_kv",
        "L1_xattn_W_qr", "L1_xattn_W_kr", "L1_xattn_Wo", "L1_ffn_router_w", "L1_ffn_e_bias", "L1_ffn_W_gate",
        "L1_ffn_W_up", "L1_ffn_W_down", "L1_ffn_shared_gate", "L1_ffn_shared_up", "L1_ffn_shared_down"]


def rope_tables():
    def table(width):
        inv = (1.0 / 10000.0 ** (np.arange(0, width, 2, dtype=np.float32) / np.float32(width))).astype(np.float32)
        f = np.arange(S, dtype=np.float32)[:, None] * inv[None, :]
        return np.repeat(np.sin(f), 2, axis=-1), np.repeat(np.cos(f), 2, axis=-1)
    sq, cq = table(DQ)
    sk, ck = table(DC)
    sk = np.concatenate([-sk[:, :DC // 2], sk[:, DC // 2:]], axis=1)
    halves = lambda x: np.ascontiguousarray(x.T.reshape(2, HALF, S).transpose(1, 0, 2))
    rows = lambda x: np.ascontiguousarray(x.reshape(2, P, DC).transpose(1, 0, 2))
    return {"cosq": halves(cq), "sinq": halves(sq), "cosk": rows(ck), "sink": rows(sk)}


def kernel(**inputs):
    import concourse.bacc as _bacc
    from concourse.bass_utils import run_bass_kernel_spmd as _run

    nc = _bacc.Bacc("TRN2", target_bir_lowering=False, num_devices=1)
    arrays, args = {}, {}
    for name, a in list((n, inputs[n]) for n in _INS) + list(rope_tables().items()):
        a = np.ascontiguousarray(a)
        arrays[f"in_{name}_dram"] = a
        args[name] = nc.dram_tensor(f"in_{name}_dram", a.shape, mybir.dt.from_np(a.dtype), kind="ExternalInput").ap()
    out = nc.dram_tensor("out_0_dram", (B, S, D), F32, kind="ExternalOutput").ap()
    build(nc, args, out, STAGES)
    r = _run(nc, [arrays], core_ids=[0])
    return r.results[0]["out_0_dram"]
```

```python
from contextlib import ExitStack

import concourse.bass as bass
import numpy as np
from concourse import mybir

F32 = mybir.dt.float32
F16 = mybir.dt.float16
ALU = mybir.AluOpType
ACT = mybir.ActivationFunctionType
AX = mybir.AxisListType

P = 128
B, S, D = 4, 256, 256
T = B * S
NT = T // P
KT = D // P
LN_EPS = 1e-5
BIG, NEG = 3.0e38, -3.0e38

DC = 64
TOP_ADJ = int(S * 0.3)
ROUNDS = (TOP_ADJ + 7) // 8

NBLK, BLK, TOP_BLK = 16, 64, 4
HID = NBLK * BLK

H, HK, DQ, R = 16, 128, 192, 64
HALF = DQ // 2
PAIRS = H // 2

E, EI = 32, 128
TOP_E, GROUPS, TOP_G = 4, 8, 3
GE = E // GROUPS
CAP = -(-5 * T // (4 * E))
ROUTE_SCALE = 2.5
EPT = P // CAP
ST_T = -(-E // EPT)
SLOTS = EPT * CAP
SHARED = 256
STAGES = 4


class Shared:
    pass


class Norm:

    def __init__(self, sem, name, size):
        self.size = size
        self.stats, self.aggr, self.var = sem(name + "_stats"), sem(name + "_aggr"), sem(name + "_var")
        self.std, self.rstd, self.xn = sem(name + "_std"), sem(name + "_rstd"), sem(name + "_xn")


def norm_stats(dve, g, nm, q):
    n = nm.size
    for t in range(n * q, n * q + n):
        dve.bn_stats(g.stat[:, t, :], g.X[:, t, :]).then_inc(nm.stats, 1)
    for t in range(n * q, n * q + n):
        dve.wait_ge(nm.stats, t + 1)
        dve.bn_aggr(g.mv[:, t, :], g.stat[:, t, :]).then_inc(nm.aggr, 1)
    dve.wait_ge(nm.aggr, n * q + n)
    dve.tensor_scalar(g.var[:, n * q:n * q + n], g.mv[:, n * q:n * q + n, 1], LN_EPS, None,
                      ALU.add).then_inc(nm.var, 1)


def norm_root(act, g, nm, q):
    n = nm.size
    act.wait_ge(nm.var, q + 1)
    act.activation(g.std[:, n * q:n * q + n], g.var[:, n * q:n * q + n], ACT.Sqrt).then_inc(nm.std, 1)


def norm_inverse(dve, g, nm, q):
    n = nm.size
    dve.wait_ge(nm.std, q + 1)
    dve.reciprocal(g.rstd[:, n * q:n * q + n], g.std[:, n * q:n * q + n]).then_inc(nm.rstd, 1)


def norm_apply(eng, g, nm, q):
    n = nm.size
    eng.wait_ge(nm.rstd, q + 1)
    for t in range(n * q, n * q + n):
        eng.tensor_scalar(g.XN[:, t, :], g.X[:, t, :], g.mv[:, t, 0:1], g.rstd[:, t:t + 1],
                          ALU.subtract, ALU.mult).then_inc(nm.xn, 1)


def norm_turn(pe, g, nm, q, bank):
    pe.wait_ge(nm.xn, 2 * q + 2)
    for k in range(KT):
        for j in range(2):
            mm = pe.transpose(bank[:, S * k + j * P:S * k + (j + 1) * P], g.XN[:, 2 * q + j, k * P:(k + 1) * P],
                              g.ident[:, :])
    return mm


FOLDS = 6
FOLD_SPLIT = (0, 1, 5)
UP = 64.0
UPW = 256.0


def split(ah, al, bh, bl):
    return (ah, bh), (ah, bl), (al, bh)


OUT_BANKS = (0, 1, 7, 2)


def output_share(pe, g, t, some):
    for p in some:
        for m, (xx, nx) in enumerate(split(g.XCH, g.XCL, g.NH, g.NL)):
            mm = pe.matmul(g.ps[:, OUT_BANKS[t % 4], 0:D], xx[:, p, t * P:(t + 1) * P], nx[:, p, :],
                           start=(p == 0 and m == 0), stop=(p == PAIRS - 1 and m == 2))
    return mm


def fold_product(pe, g, u, f, o):
    if f < 2:
        for h in range(2):
            mm = pe.matmul(o[:, h * DQ:(h + 1) * DQ], g.WQ[u][:, h, f * P:(f + 1) * P], g.WCQ[u][:, h, :],
                           start=True, stop=True)
    elif f == 2:
        for h in range(2):
            pe.transpose(o[:, h * HALF:(h + 1) * HALF], g.WQR[u][:, h, :, :].rearrange("j a r -> j (a r)"),
                         g.ident[0:HALF, 0:HALF])
        mm = pe.transpose(o[:, 2 * HALF:2 * HALF + DC], g.WKR[u][:, :, :].rearrange("d h r -> d (h r)"),
                          g.ident[0:DC, 0:DC])
    elif f == 3:
        for h in range(2):
            for c in range(KT):
                mm = pe.transpose(o[:, h * D + c * P:h * D + (c + 1) * P], g.WO[u][:, c, h * HK:(h + 1) * HK],
                                  g.ident[:, :])
    elif f == 4:
        for h in range(2):
            for a in range(2):
                mm = pe.matmul(o[0:HALF, (2 * h + a) * DC:(2 * h + a + 1) * DC],
                               g.RT[:, a, h * HALF:(h + 1) * HALF], g.RT[:, h, 2 * HALF:2 * HALF + DC],
                               start=True, stop=True)
    else:
        for h in range(2):
            mm = pe.matmul(o[DC * h:DC * h + DC, 0:D], g.WCV[u][:, h, :], g.WOT[:, h, :], start=True, stop=True)
    return mm


def fold_keep(act, g, r, u, f, o):
    if f < 2:
        return act.activation(g.CH[u][:, f, :], o[:, 0:2 * DQ], ACT.Copy, scale=UP)
    if f == 2:
        act.activation(g.RT[:, 0, :], o[0:R, 0:2 * HALF + DC], ACT.Copy)
        return act.activation(g.RT[:, 1, :], o[R:P, 0:2 * HALF + DC], ACT.Copy)
    if f == 3:
        return act.activation(g.WOT[:, :, :], o, ACT.Copy)
    if f == 4:
        return act.activation(g.M[u][:, :, :], o[0:HALF, 0:4 * DC], ACT.Copy, scale=1.0 / UP)
    return act.activation(g.NH[:, bass.ds(r, 1), :], o[:, 0:D], ACT.Copy, scale=UP)


def fold_rest(dve, g, r, u, f, o):
    hi, lo, w = ((g.CH[u][:, f, :], g.CL[u][:, f, :], 2 * DQ) if f < 2 else
                 (g.NH[:, bass.ds(r, 1), :], g.NL[:, bass.ds(r, 1), :], D))
    return dve.scalar_tensor_tensor(out=lo, in0=o[:, 0:w], scalar=UP, in1=hi, op0=ALU.mult, op1=ALU.subtract)


DW = 7 * 16


def load_pair(sp, g, i, r, u):
    two_heads = bass.ds(2 * r, 2)
    wqr_v = i["L1_xattn_W_qr"].rearrange("h (a j) r -> j h a r", a=2)
    sp.dma_start(g.WQ[u][:, :, :], i["L1_xattn_Wq"].rearrange("(h k) n -> k h n", k=HK)[:, two_heads, :]
                 ).then_inc(g.d_w[u], 16)
    sp.dma_start(g.WCQ[u][:, :, :], i["L1_xattn_w_kc_q"].rearrange("h k q -> k h q")[:, two_heads, :]
                 ).then_inc(g.d_w[u], 16)
    sp.dma_start(g.WCV[u][:, :, :], i["L1_xattn_w_kc_kv"].rearrange("h k d -> k h d")[:, two_heads, :]
                 ).then_inc(g.d_w[u], 16)
    for h in range(2):
        sp.dma_start(g.WQR[u][:, h, :, :], wqr_v[:, bass.ds(2 * r + h, 1), :, :]).then_inc(g.d_w[u], 16)
    sp.dma_start(g.WKR[u][:, :, :], i["L1_xattn_W_kr"].rearrange("h d r -> d h r")[:, two_heads, :]
                 ).then_inc(g.d_w[u], 16)
    sp.dma_start(g.WO[u][:, :, :], i["L1_xattn_Wo"].rearrange("(c p) n -> p c n", p=P)[
        :, :, bass.ds(2 * HK * r, 2 * HK)]).then_inc(g.d_w[u], 16)


def stage_first_layer(nc, g, i):
    with ExitStack() as ctx:
        sb = lambda name, shape, dt=F32: ctx.enter_context(nc.sbuf_tensor(name, shape, dt))
        sem = lambda name: ctx.enter_context(nc.semaphore(name))
        CT = sb("CT", [P, NT, DC])
        CTT = sb("CTT", [DC, T])
        wq = sb("wq", [DC, DC])
        wk = sb("wk", [DC, DC])
        GT = sb("GT", [DC, DC])
        V = sb("V", [DC, T])
        SIM, SIG, A, XA = [g.wide[:, u, :].rearrange("p (t s) -> p t s", t=NT) for u in range(4)]
        work = sb("work", [P, 2, S])
        m8 = sb("m8", [P, 2, ROUNDS, 8])
        raw = sb("raw", [P, 5])
        gam = sb("gam", [P, 4])
        mix = sb("mix", [P, 3, NT])
        w1 = sb("w1", [P, HID // P, D])
        w2 = sb("w2", [P, KT, HID])
        wr = sb("wr", [NBLK, D])
        rw = sb("rw", [E, D])
        shw = g.XT[:, :, :].rearrange("p k t -> p (k t)")[:, 0:3 * KT * SHARED].rearrange(
            "p (w c n) -> p w c n", w=3, c=KT)
        br = sb("br", [P, NBLK])
        W1T = sb("W1T", [P, KT, HID])
        W2T = sb("W2T", [P, HID // P, D])
        WrT = sb("WrT", [P, KT, NBLK])
        ck = sb("ck", [P, 2, DC])
        sk = sb("sk", [P, 2, DC])
        kc = sb("kc", [P, NT, DC])
        ks = sb("ks", [P, NT, DC])
        XT = [sb(f"XT{u}", [P, KT, S]) for u in range(2)]
        FS = sb("FS", [P, 2 * DQ])
        FILL = 8 - TOP_BLK
        LG = sb("LG", [P, NT, FILL + NBLK])
        RP = sb("RP", [P, NT, FILL + NBLK])
        M8 = sb("M8", [P, NT, 8])
        MK = sb("MK", [P, NT, NBLK], F16)
        GL = [sb(f"GL{u}", [P, 2, S]) for u in range(2)]
        MS = [sb(f"MS{u}", [P, 2, S]) for u in range(2)]
        HT = [sb(f"HT{u}", [P, HID // P, S]) for u in range(2)]

        d_x, d_ctx, d_wqk, d_raw, d_rope = map(sem, ["d_x", "d_ctx", "d_wqk", "d_raw", "d_rope"])
        d_w1, d_w2, d_wr, d_br, d_sh = map(sem, ["d_w1", "d_w2", "d_wr", "d_br", "d_sh"])
        id_zero, id_ok, kv_mul, kv_sum, kv_ok, lg_fill = map(
            sem, ["id_zero", "id_ok", "kv_mul", "kv_sum", "kv_ok", "lg_fill"])
        filled, hi_ok, emptied, at_ps = map(sem, ["filled", "hi_ok", "emptied", "at_ps"])
        tanh_ok, gam_ok, max_ok, rep_ok, a_ok, xa_ok = map(
            sem, ["tanh_ok", "gam_ok", "max_ok", "rep_ok", "a_ok", "xa_ok"])
        sim_ok, mix_ok, split_ok, fold_a, fold_b = map(sem, ["sim_ok", "mix_ok", "split_ok", "fold_a", "fold_b"])
        (xt_ps, xt_ok, lg_ps, lg_ok, top_ok, mark_ok, mk_ok, h_ps, gelu_ok, mask_ps, ms_ok, ht_ok, y_ps, x2_ok,
         x2t_ps, xh_ok, xl_ok) = map(
            sem, ["xt_ps", "xt_ok", "lg_ps", "lg_ok", "top_ok", "mark_ok", "mk_ok", "h_ps", "gelu_ok", "mask_ps",
                  "ms_ok", "ht_ok", "y_ps", "x2_ok", "x2t_ps", "xh_ok", "xl_ok"])
        n0, n1, n2 = Norm(sem, "n0", NT), Norm(sem, "n1", 2), Norm(sem, "n2", 2)

        x_v = i["x"].rearrange("b (t p) d -> p (b t) d", p=P)
        c_v = i["ctx_512"].rearrange("b (t p) d -> p (b t) d", p=P)
        N_CTX, N_G, N_V, N_SIM = (0, 4), 1, (2, 5), (3, 6, 7, 8)
        N_W1, N_W2, N_WR, N_KV, N_SH, N_FOLD = 9, 13, 17, 18, 20, 23
        is_split = [N_KV <= n < N_SH for n in range(N_FOLD + 2 * FOLDS)]
        splits = lambda n: sum(is_split[0:n + 1])
        plain = lambda n: n + 1 - splits(n)

        fold_bank = lambda k: g.ps[:, (N_FOLD + k) % 4, :]

        def wait_empty(eng, n):
            if is_split[n]:
                eng.wait_ge(split_ok, splits(n))
            else:
                eng.wait_ge(emptied, plain(n))

        HB, MB, AB, TB, UB, YB = 1, 3, 4, 5, 6, 7
        UNITS = HID // P // 2

        with nc.Block() as block:
            @block.sync
            def _(sp):
                sp.dma_start(CT[:, :, :], c_v).then_inc(d_ctx, 16)
                sp.dma_start(wq[:, :], i["L0_xattn_Wq"]).then_inc(d_wqk, 16)
                sp.dma_start(wk[:, :], i["L0_xattn_Wk"]).then_inc(d_wqk, 16)
                for h in range(2):
                    sp.dma_start(g.X[:, 4 * h:4 * h + 4, :], x_v[:, 4 * h:4 * h + 4, :]).then_inc(d_x, 16)
                sp.dma_start(ck[:, :, :], i["cosk"]).then_inc(d_rope, 16)
                sp.dma_start(sk[:, :, :], i["sink"]).then_inc(d_rope, 16)
                sp.dma_start(w1[:, :, :], i["L0_ffn_W1"].rearrange("(o p) n -> p o n", p=P)).then_inc(d_w1, 16)
                sp.dma_start(w2[:, :, :], i["L0_ffn_W2"].rearrange("(c p) n -> p c n", p=P)).then_inc(d_w2, 16)
                for n, (name, at) in enumerate([("g_xattn", 0), ("g_xattn", 1), ("g_ffn", 0), ("g_ffn", 1),
                                                ("L0_xattn_gamma_raw", 0)]):
                    sp.dma_start(raw[:, n:n + 1], i[name][at:at + 1].partition_broadcast(P)).then_inc(d_raw, 16)
                sp.dma_start(wr[:, :], i["L0_ffn_Wr"]).then_inc(d_wr, 16)
                sp.dma_start(rw[:, :], i["L1_ffn_router_w"]).then_inc(d_wr, 16)
                sp.dma_start(br[:, :], i["L0_ffn_br"].partition_broadcast(P)).then_inc(d_br, 16)
                sp.dma_start(g.cosq[:, :, :], i["cosq"]).then_inc(g.d_ropeq, 16)
                sp.dma_start(g.sinq[:, :, :], i["sinq"]).then_inc(g.d_ropeq, 16)
                for n, name in enumerate(["L1_ffn_shared_gate", "L1_ffn_shared_up", "L1_ffn_shared_down"]):
                    sp.dma_start(shw[:, n, :, :], i[name].rearrange("(c p) n -> p c n", p=P)).then_inc(d_sh, 16)
                for r in range(2):
                    load_pair(sp, g, i, r, r)
                for r in range(2, 4):
                    sp.wait_ge(filled, N_FOLD + FOLDS * (r - 1))
                    load_pair(sp, g, i, r, r % 2)

            @block.gpsimd
            def _(pool):
                pool.memset(g.ident[:, :], 0.0).then_inc(id_zero, 1)
                pool.wait_ge(id_zero, 1)
                pool.affine_select(out=g.ident[:, :], in_=g.ident[:, :], compare_op=ALU.not_equal,
                                   fill=1.0, base=0, pattern=[[-1, P]],
                                   channel_multiplier=1).then_inc(id_ok, 1)
                pool.wait_ge(id_ok, 1)
                pool.tensor_copy(g.ident16[:, :], g.ident[:, :]).then_inc(id_ok, 1)
                pool.memset(LG[:, :, 0:FILL], BIG).then_inc(lg_fill, 1)
                pool.wait_ge(d_ctx, 16)
                pool.wait_ge(d_rope, 32)
                lt = lambda x: x.rearrange("p (b l) d -> p b l d", l=2)
                tab = lambda x, a, z: x[:, :, a:z].unsqueeze(1).broadcast_to([P, B, 2, z - a])
                q = DC // 2
                pool.tensor_tensor(lt(kc), lt(CT), tab(ck, 0, DC), ALU.mult).then_inc(kv_mul, 1)
                pool.tensor_tensor(lt(ks)[:, :, :, 0:q], lt(CT)[:, :, :, q:DC], tab(sk, 0, q),
                                   ALU.mult).then_inc(kv_mul, 1)
                pool.tensor_tensor(lt(ks)[:, :, :, q:DC], lt(CT)[:, :, :, 0:q], tab(sk, q, DC),
                                   ALU.mult).then_inc(kv_mul, 1)
                pool.wait_ge(kv_mul, 3)
                pool.tensor_tensor(g.KV[:, :, 0, :], kc[:, :, :], ks[:, :, :], ALU.add).then_inc(kv_sum, 1)
                pool.wait_ge(kv_sum, 1)
                pool.tensor_copy(g.KV[:, :, 1, :], g.KV[:, :, 0, :]).then_inc(kv_ok, 1)
                pool.wait_ge(mix_ok, 4)
                for t in range(NT):
                    pool.tensor_scalar(XA[:, t, :], g.X[:, t, :], mix[:, 1, t:t + 1], mix[:, 2, t:t + 1],
                                       ALU.mult, ALU.add).then_inc(xa_ok, 1)

                def masked(b, n):
                    u = UNITS * b + n
                    pool.wait_ge(gelu_ok, u + 1)
                    pool.wait_ge(ms_ok, u + 1)
                    if b >= 2:
                        pool.wait_ge(y_ps, b - 1)
                    pool.tensor_tensor(HT[b % 2][:, 2 * n:2 * n + 2, :], GL[u % 2][:, :, :], MS[u % 2][:, :, :],
                                       ALU.mult).then_inc(ht_ok, 1)
                def fold_second(k):
                    r, f = k // FOLDS, k % FOLDS
                    if f in FOLD_SPLIT:
                        hi, lo, w = ((g.CH[r][:, f, :], g.CL[r][:, f, :], 2 * DQ) if f < 2 else
                                     (g.NH[:, r, :], g.NL[:, r, :], D))
                        pool.wait_ge(fold_a, len(FOLD_SPLIT) * r + FOLD_SPLIT.index(f) + 1)
                        pool.wait_ge(emptied, plain(N_FOLD + k))
                        pool.tensor_tensor(lo, FS[:, 0:w], hi, ALU.subtract).then_inc(fold_b, 1)

                for k in range(2 * FOLDS):
                    fold_second(k)
                for b in range(B):
                    for n in range(UNITS):
                        masked(b, n)

            @block.tensor
            def _(pe):
                def bank(n):
                    if n >= 4:
                        wait_empty(pe, n - 4)
                    return g.ps[:, n % 4, :]
                pe.wait_ge(id_ok, 1)
                pe.wait_ge(d_ctx, 16)
                def context(h):
                    o = bank(N_CTX[h])
                    for j in range(4):
                        mm = pe.transpose(o[0:DC, j * P:(j + 1) * P], CT[:, 4 * h + j, :], g.ident[:, :])
                    mm.then_inc(filled, 1)

                def projection(h):
                    o = bank(N_V[h])
                    wait_empty(pe, max(N_G, N_CTX[h]))
                    pe.matmul(o[0:DC, :], GT[:, :], CTT[:, 512 * h:512 * h + 512],
                              start=True, stop=True).then_inc(filled, 1)

                def similarity(b):
                    o = bank(N_SIM[b])
                    wait_empty(pe, N_V[b // 2])
                    for j in range(2):
                        mm = pe.matmul(o[:, S * j:S * j + S], CTT[:, (2 * b + j) * P:(2 * b + j + 1) * P],
                                       V[:, S * b:S * b + S], start=True, stop=True)
                    mm.then_inc(filled, 1)

                context(0)
                pe.wait_ge(d_wqk, 32)
                pe.matmul(bank(N_G)[0:DC, 0:DC], wk[:, :], wq[:, :], start=True, stop=True).then_inc(filled, 1)
                projection(0)
                similarity(0)
                context(1)
                projection(1)
                for b in range(1, B):
                    similarity(b)
                pe.wait_ge(d_w1, 16)
                for k in range(KT):
                    for h in range(2):
                        o = bank(N_W1 + 2 * k + h)
                        for j in range(4):
                            mm = pe.transpose(o[:, j * P:(j + 1) * P], w1[:, 4 * h + j, k * P:(k + 1) * P],
                                              g.ident[:, :])
                        mm.then_inc(filled, 1)
                pe.wait_ge(d_w2, 16)
                for q in range(4):
                    o = bank(N_W2 + q)
                    for j in range(2):
                        for c in range(KT):
                            mm = pe.transpose(o[:, (2 * j + c) * P:(2 * j + c + 1) * P],
                                              w2[:, c, (2 * q + j) * P:(2 * q + j + 1) * P], g.ident[:, :])
                    mm.then_inc(filled, 1)
                pe.wait_ge(d_wr, 32)
                o = bank(N_WR)
                for k in range(KT):
                    pe.transpose(o[:, k * NBLK:(k + 1) * NBLK], wr[:, k * P:(k + 1) * P], g.ident[0:NBLK, 0:NBLK])
                for k in range(KT):
                    mm = pe.transpose(o[:, S + k * E:S + (k + 1) * E], rw[:, k * P:(k + 1) * P], g.ident[0:E, 0:E])
                mm.then_inc(filled, 1)
                pe.wait_ge(kv_ok, 1)
                for h in range(2):
                    o = bank(N_KV + h)
                    for j in range(4):
                        mm = pe.transpose(o[:, j * P:(j + 1) * P],
                                          g.KV[:, 4 * h + j, :, :].rearrange("p a d -> p (a d)"), g.ident[:, :])
                    mm.then_inc(filled, 1)

                pe.wait_ge(d_sh, 48)
                for n in range(3):
                    o = bank(N_SH + n)
                    for k in range(KT):
                        for c in range(KT):
                            mm = pe.transpose(o[:, (KT * k + c) * P:(KT * k + c + 1) * P],
                                              shw[:, n, c, k * P:(k + 1) * P], g.ident[:, :])
                    mm.then_inc(filled, 1)
                def symmetric(b):
                    pe.wait_ge(a_ok, 2 * b + 2)
                    if b >= 1:
                        pe.wait_ge(lg_ok, b)
                    for j in range(2):
                        for m in range(2):
                            o = g.ps[:, AB, S * j + m * P:S * j + (m + 1) * P]
                            pe.matmul(o, A[:, 2 * b + m, j * P:(j + 1) * P], g.ident[:, :], start=True, stop=False)
                            mm = pe.matmul(o, g.ident[:, :], A[:, 2 * b + j, m * P:(m + 1) * P], start=False,
                                           stop=True)
                    mm.then_inc(at_ps, 1)

                def fold(k):
                    r, f = k // FOLDS, k % FOLDS
                    wait_empty(pe, N_FOLD + k - (2 if f >= 4 else 4))
                    if f == 0:
                        pe.wait_ge(g.d_w[r], DW)
                    fold_product(pe, g, r, f, fold_bank(k)).then_inc(filled, 1)

                def mask(b, n):
                    pe.wait_ge(mk_ok, b + 1)
                    if UNITS * b + n >= 1:
                        pe.wait_ge(ms_ok, UNITS * b + n)
                    for o in range(2):
                        for j in range(2):
                            for c in range(2):
                                block_no = 2 * (2 * n + o) + c
                                pick = MK[:, 2 * b + j, block_no:block_no + 1].broadcast_to([P, BLK])
                                mm = pe.matmul(g.ps[BLK * c:BLK * c + BLK, MB, S * o + j * P:S * o + (j + 1) * P],
                                               pick, g.ident16[:, :], start=True, stop=True)
                    mm.then_inc(mask_ps, 1)

                def second_norm(b):
                    if b >= 1:
                        pe.wait_ge(xl_ok, b)
                    norm_turn(pe, g, n2, b, g.ps[:, UB, :]).then_inc(x2t_ps, 1)

                def result(b, n):
                    pe.wait_ge(ht_ok, UNITS * b + n + 1)
                    if b >= 1 and n == 0:
                        pe.wait_ge(x2_ok, 2 * b)
                    for j in range(2):
                        for o in (2 * n, 2 * n + 1):
                            mm = pe.matmul(g.ps[:, YB, D * j:D * j + D], HT[b % 2][:, o, j * P:(j + 1) * P],
                                           W2T[:, o, :], start=(o == 0 and j == 0), stop=(o == HID // P - 1),
                                           skip_group_check=True)
                    if n == UNITS - 1:
                        mm.then_inc(y_ps, 1)

                pe.wait_ge(id_ok, 2)
                for k in range(FOLDS):
                    if k == FOLDS // 2:
                        symmetric(0)
                    fold(k)
                for b in range(B):
                    for n in range(UNITS):
                        if b >= 1:
                            result(b - 1, n)
                    if b == 0:
                        for k in range(FOLDS, 2 * FOLDS):
                            fold(k)
                    norm_turn(pe, g, n1, b, g.ps[:, TB, :]).then_inc(xt_ps, 1)
                    pe.wait_ge(xt_ok, b + 1)
                    if b == 0:
                        wait_empty(pe, N_FOLD + 2 * FOLDS - 1)
                        pe.wait_ge(split_ok, splits(N_FOLD))
                    for j in range(2):
                        for k in range(KT):
                            mm = pe.matmul(g.ps[:, AB, j * NBLK:(j + 1) * NBLK], XT[b % 2][:, k, j * P:(j + 1) * P],
                                           WrT[:, k, :], start=(k == 0), stop=(k == KT - 1))
                    mm.then_inc(lg_ps, 1)
                    for n in range(UNITS):
                        u = UNITS * b + n
                        if u >= 2:
                            pe.wait_ge(gelu_ok, u - 1)
                        for o in range(2):
                            for k in range(KT):
                                mm = pe.matmul(g.ps[:, HB + u % 2, S * o:S * o + S],
                                               W1T[:, k, (2 * n + o) * P:(2 * n + o + 1) * P],
                                               XT[b % 2][:, k, :], start=(k == 0), stop=(k == KT - 1))
                        mm.then_inc(h_ps, 1)
                        if n >= 1:
                            mask(b, n - 1)
                        if b == B - 1 and n == 1:
                            second_norm(b - 1)
                        if b == B - 1 and n >= 2:
                            result(b, n - 2)
                    if b < B - 1:
                        symmetric(b + 1)
                    mask(b, UNITS - 1)
                    if 1 <= b < B - 1:
                        second_norm(b - 1)
                result(B - 1, UNITS - 2)
                result(B - 1, UNITS - 1)
                second_norm(B - 1)

            @block.scalar
            def _(act):
                def bank(n):
                    act.wait_ge(filled, n + 1)
                    return g.ps[:, n % 4, :]
                def context(h):
                    act.activation(CTT[:, 512 * h:512 * h + 512], bank(N_CTX[h])[0:DC, :],
                                   ACT.Copy).then_inc(emptied, 1)

                def projection(h):
                    act.activation(V[:, 512 * h:512 * h + 512], bank(N_V[h])[0:DC, :], ACT.Copy,
                                   scale=1.0 / 16.0).then_inc(emptied, 1)

                def similarity(b):
                    o = bank(N_SIM[b])
                    act.activation(SIM[:, 2 * b:2 * b + 2, :], o, ACT.Copy).then_inc(sim_ok, 1)
                    act.activation(SIG[:, 2 * b:2 * b + 2, :], o, ACT.Sigmoid).then_inc(emptied, 1)

                context(0)
                act.activation(GT[:, :], bank(N_G)[0:DC, 0:DC], ACT.Copy).then_inc(emptied, 1)
                projection(0)
                similarity(0)
                context(1)
                projection(1)
                for b in range(1, B):
                    similarity(b)
                act.wait_ge(d_raw, 80)
                act.activation(g.gate[:, 0:4], raw[:, 0:4], ACT.Tanh).then_inc(tanh_ok, 1)
                act.activation(gam[:, 0:1], raw[:, 4:5], ACT.Sigmoid).then_inc(tanh_ok, 1)
                norm_root(act, g, n0, 0)
                for k in range(KT):
                    for h in range(2):
                        act.activation(W1T[:, k, 512 * h:512 * h + 512], bank(N_W1 + 2 * k + h),
                                       ACT.Copy).then_inc(emptied, 1)
                for q in range(4):
                    act.activation(W2T[:, 2 * q:2 * q + 2, :], bank(N_W2 + q), ACT.Copy).then_inc(emptied, 1)
                o = bank(N_WR)
                act.activation(WrT[:, :, :], o[:, 0:KT * NBLK], ACT.Copy)
                act.activation(g.rwT[:, :, :], o[:, S:S + KT * E], ACT.Copy).then_inc(emptied, 1)
                for h in range(2):
                    act.activation(g.KH[:, 512 * h:512 * h + 512], bank(N_KV + h), ACT.Copy,
                                   scale=-1.0).then_inc(hi_ok, 1)
                for n in range(3):
                    act.activation(g.shT[:, n, :, :], bank(N_SH + n), ACT.Copy,
                                   scale=UPW if n == 2 else 1.0).then_inc(emptied, 1)

                def fold(k):
                    r, f = k // FOLDS, k % FOLDS
                    act.wait_ge(filled, N_FOLD + k + 1)
                    o = fold_bank(k)
                    if f in FOLD_SPLIT:
                        w = 2 * DQ if f < 2 else D
                        fold_keep(act, g, r, r, f, o).then_inc(fold_a, 1)
                        split_no = len(FOLD_SPLIT) * r + FOLD_SPLIT.index(f)
                        if split_no >= 1:
                            act.wait_ge(fold_b, split_no)
                        act.activation(FS[:, 0:w], o[:, 0:w], ACT.Copy, scale=UP).then_inc(emptied, 1)
                    else:
                        fold_keep(act, g, r, r, f, o).then_inc(emptied, 1)

                def gelu(b, n):
                    u = UNITS * b + n
                    act.wait_ge(h_ps, u + 1)
                    if u >= 2:
                        act.wait_ge(ht_ok, u - 1)
                    act.activation(GL[u % 2][:, :, :], g.ps[:, HB + u % 2, :], ACT.Gelu).then_inc(gelu_ok, 1)
                    if n == 0 and b >= 1:
                        norm_root(act, g, n2, b - 1)

                def mask(b, n):
                    u = UNITS * b + n
                    act.wait_ge(mask_ps, u + 1)
                    act.activation(MS[u % 2][:, :, :], g.ps[:, MB, :], ACT.Copy).then_inc(ms_ok, 1)

                def second_norm(b):
                    act.wait_ge(x2t_ps, b + 1)
                    act.activation(g.XH[:, :, S * b:S * b + S], g.ps[:, UB, :].rearrange("p (k s) -> p k s", k=KT),
                                   ACT.Copy).then_inc(xh_ok, 1)
                for k in range(FOLDS):
                    fold(k)
                for b in range(B):
                    norm_root(act, g, n1, b)
                    if b == 0:
                        for k in range(FOLDS, 2 * FOLDS):
                            fold(k)
                    act.wait_ge(xt_ps, b + 1)
                    act.activation(XT[b % 2][:, :, :], g.ps[:, TB, :], ACT.Copy).then_inc(xt_ok, 1)
                    for n in range(UNITS):
                        gelu(b, n)
                        if n >= 1:
                            mask(b, n - 1)
                        if n == UNITS - 1:
                            mask(b, n)
                        if b >= 1 and n == (2 if b == B - 1 else UNITS - 1):
                            second_norm(b - 1)
                norm_root(act, g, n2, B - 1)
                second_norm(B - 1)

            @block.vector
            def _(dve):
                def first(b):
                    dve.wait_ge(at_ps, b + 1)
                    dve.wait_ge(xa_ok, 2 * b + 2)
                    for j in range(2):
                        t = 2 * b + j
                        dve.scalar_tensor_tensor(out=g.X[:, t, :], in0=g.ps[:, AB, S * j:S * j + S],
                                                 scalar=gam[:, 3:4], in1=XA[:, t, :], op0=ALU.mult,
                                                 op1=ALU.add).then_inc(g.x_done, 1)
                    dve.wait_ge(g.x_done, 2 * b + 2)
                    norm_stats(dve, g, n1, b)

                def route(b):
                    t = slice(2 * b, 2 * b + 2)
                    dve.wait_ge(lg_ps, b + 1)
                    if b == 0:
                        dve.wait_ge(d_br, 16)
                        dve.wait_ge(lg_fill, 1)
                    dve.tensor_tensor(LG[:, t, FILL:], g.ps[:, AB, 0:2 * NBLK].rearrange("p (t n) -> p t n", t=2),
                                      br[:, :].unsqueeze(1).broadcast_to([P, 2, NBLK]), ALU.add).then_inc(lg_ok, 1)
                    dve.wait_ge(lg_ok, b + 1)
                    for j in range(2):
                        dve.max(M8[:, 2 * b + j, :], LG[:, 2 * b + j, :]).then_inc(top_ok, 1)
                    for j in range(2):
                        dve.wait_ge(top_ok, 2 * b + j + 1)
                        dve.match_replace(RP[:, 2 * b + j, :], M8[:, 2 * b + j, :], LG[:, 2 * b + j, :],
                                          NEG).then_inc(mark_ok, 1)
                    dve.wait_ge(mark_ok, 2 * b + 2)
                    dve.tensor_tensor(MK[:, t, :], LG[:, t, FILL:], RP[:, t, FILL:],
                                      ALU.not_equal).then_inc(mk_ok, 1)

                def second(b):
                    dve.wait_ge(y_ps, b + 1)
                    for j in range(2):
                        t = 2 * b + j
                        dve.scalar_tensor_tensor(out=g.X[:, t, :], in0=g.ps[:, YB, D * j:D * j + D],
                                                 scalar=g.gate[:, 2:3], in1=g.X[:, t, :], op0=ALU.mult,
                                                 op1=ALU.add).then_inc(x2_ok, 1)
                    dve.wait_ge(x2_ok, 2 * b + 2)
                    norm_stats(dve, g, n2, b)

                def rest(b):
                    dve.wait_ge(xh_ok, b + 1)
                    dve.tensor_tensor(g.XL[:, :, S * b:S * b + S], g.ps[:, UB, :].rearrange("p (k s) -> p k s", k=KT),
                                      g.XH[:, :, S * b:S * b + S], ALU.subtract).then_inc(xl_ok, 1)

                def kv_rest():
                    for h in range(2):
                        dve.wait_ge(hi_ok, h + 1)
                        dve.scalar_tensor_tensor(out=g.KL[:, 512 * h:512 * h + 512], in0=g.ps[:, (N_KV + h) % 4, :],
                                                 scalar=-1.0, in1=g.KH[:, 512 * h:512 * h + 512], op0=ALU.mult,
                                                 op1=ALU.subtract).then_inc(split_ok, 1)

                def mixture():
                    dve.wait_ge(tanh_ok, 2)
                    dve.tensor_scalar(gam[:, 1:2], gam[:, 0:1], -1.0, 1.0, ALU.mult, ALU.add).then_inc(gam_ok, 1)
                    dve.tensor_scalar(gam[:, 3:4], gam[:, 0:1], g.gate[:, 0:1], 0.5, ALU.mult,
                                      ALU.mult).then_inc(gam_ok, 1)
                    norm_inverse(dve, g, n0, 0)
                    dve.wait_ge(gam_ok, 2)
                    dve.tensor_scalar(gam[:, 2:3], gam[:, 1:2], g.gate[:, 0:1], None, ALU.mult).then_inc(gam_ok, 1)
                    dve.wait_ge(gam_ok, 3)
                    dve.wait_ge(n0.rstd, 1)
                    dve.tensor_scalar(mix[:, 0, :], g.rstd[:, :], gam[:, 2:3], None, ALU.mult).then_inc(mix_ok, 1)
                    dve.wait_ge(mix_ok, 1)
                    dve.tensor_scalar(mix[:, 1, :], mix[:, 0, :], 1.0, None, ALU.add).then_inc(mix_ok, 1)
                    dve.tensor_tensor(mix[:, 2, :], g.mv[:, :, 0], mix[:, 0, :], ALU.mult).then_inc(mix_ok, 1)
                    dve.wait_ge(mix_ok, 3)
                    dve.tensor_scalar(mix[:, 2, :], mix[:, 2, :], -1.0, None, ALU.mult).then_inc(mix_ok, 1)

                dve.wait_ge(d_x, 32)
                norm_stats(dve, g, n0, 0)
                for b in range(B):
                    dve.wait_ge(sim_ok, b + 1)
                    for r in range(ROUNDS):
                        for j in range(2):
                            if r > 0:
                                dve.wait_ge(rep_ok, b * (ROUNDS - 1) * 2 + 2 * (r - 1) + j + 1)
                            src = SIM[:, 2 * b + j, :] if r == 0 else work[:, j, :]
                            dve.max(m8[:, j, r, :], src).then_inc(max_ok, 1)
                        if r < ROUNDS - 1:
                            for j in range(2):
                                dve.wait_ge(max_ok, b * ROUNDS * 2 + 2 * r + j + 1)
                                src = SIM[:, 2 * b + j, :] if r == 0 else work[:, j, :]
                                dve.match_replace(work[:, j, :], m8[:, j, r, :], src, NEG).then_inc(rep_ok, 1)
                        if b == 0 and r == 7:
                            mixture()
                        if b == 0 and r == 9:
                            kv_rest()
                        if b >= 3 and r == 3:
                            rest(b - 3)
                        if b >= 1 and r == 2:
                            first(b - 1)
                        if b >= 1 and r == 4:
                            norm_inverse(dve, g, n1, b - 1)
                            norm_apply(dve, g, n1, b - 1)
                        if b >= 2 and r == 5:
                            second(b - 2)
                        if b >= 1 and r == 6:
                            route(b - 1)
                        if b >= 2 and r == 8:
                            norm_inverse(dve, g, n2, b - 2)
                            norm_apply(dve, g, n2, b - 2)
                    last = (TOP_ADJ - 1) % 8
                    for j in range(2):
                        t = 2 * b + j
                        dve.wait_ge(max_ok, (b + 1) * ROUNDS * 2 - 1 + j)
                        if j == 0:
                            dve.wait_ge(emptied, plain(N_SIM[b]))
                        dve.scalar_tensor_tensor(out=A[:, t, :], in0=SIM[:, t, :],
                                                 scalar=m8[:, j, ROUNDS - 1, last:last + 1],
                                                 in1=SIG[:, t, :], op0=ALU.is_ge, op1=ALU.mult).then_inc(a_ok, 1)
                first(B - 1)
                norm_inverse(dve, g, n1, B - 1)
                norm_apply(dve, g, n1, B - 1)
                rest(B - 3)
                second(B - 2)
                route(B - 1)
                norm_inverse(dve, g, n2, B - 2)
                norm_apply(dve, g, n2, B - 2)
                rest(B - 2)
                second(B - 1)
                norm_inverse(dve, g, n2, B - 1)
                norm_apply(dve, g, n2, B - 1)
                rest(B - 1)


def stage_latent_attention(nc, g, i):
    with ExitStack() as ctx:
        sb = lambda name, shape, dt=F32: ctx.enter_context(nc.sbuf_tensor(name, shape, dt))
        sem = lambda name: ctx.enter_context(nc.semaphore(name))
        two = lambda name, shape: [sb(f"{name}{u}", shape) for u in range(2)]
        two16 = lambda name, shape: [sb(f"{name}{u}", shape, F16) for u in range(2)]
        TM = two("TM", [HALF, 4, 512])
        RO = sb("RO", [HALF, 2, 2, 2, 512])
        Q = [two16(f"Q{h}", [P, T]) for h in range(2)]
        HI = [slice(0, DC), slice(DC, P)]
        low = sb("low", [P, 2, 2])
        PB = two("PB", [P, 2, S])
        tot = sb("tot", [P, 2, 2])
        inv = sb("inv", [P, 2, 2])
        PTS = two("PTS", [P, 4, 2 * P])
        FIRST = 5
        QA, QP, SC, PTB, CXB, FO = 0, 2, 3, 5, 6, 7

        (q_ps, rope_ok, sum_ok, qc_ps, qc_ok, s_ps, low_ok, exp_ok, inv_ok, norm_ok, t_ps, t_ok, cx_ps, cx_ok,
         fold_ps, fold_ok, credit, fold_hi, qc_hi, cx_hi) = map(sem, [
             "q_ps", "rope_ok", "sum_ok", "qc_ps", "qc_ok", "s_ps", "low_ok", "exp_ok", "inv_ok", "norm_ok",
             "t_ps", "t_ok", "cx_ps", "cx_ok", "fold_ps", "fold_ok", "credit", "fold_hi", "qc_hi",
             "cx_hi"])
        EXP0, ROPE0, TPS0, TOK0, CXPS0, CXOK0, QC0, QCPS0, SUM0, FOLD0 = 2, 2, 2, 1, 2, 1, 1, 2, 4, 1
        DONE, NSPLIT = 2 * FOLDS, len(FOLD_SPLIT)
        starts = [(exp_ok, EXP0), (rope_ok, ROPE0), (t_ps, TPS0), (t_ok, TOK0), (cx_ps, CXPS0), (cx_ok, CXOK0),
                  (qc_ok, QC0), (qc_ps, QCPS0), (sum_ok, SUM0),
                  (fold_ok, DONE + FOLD0), (fold_ps, DONE), (fold_hi, 2 * NSPLIT)]

        def pairs(eng, body):
            with eng.Fori(0, (PAIRS - 2) // 2, 1) as it:
                for u in range(2):
                    body(it * 2 + u, u, True, True)
            body(PAIRS - 2, 0, False, True)
            body(PAIRS - 1, 1, False, False)

        with nc.Block() as block:
            @block.sync
            def _(sp):
                with sp.Fori(0, PAIRS // 2 - 2, 1) as it:
                    for u in range(2):
                        r = it * 2 + (4 + u)
                        sp.wait_ge(fold_ps, it * 12 + (DONE + 6 * (u + 1)))
                        load_pair(sp, g, i, r, u)

            @block.tensor
            def _(pe):
                def fold(r, u, f):
                    pe.wait_ge(fold_ok, 6 * r + (f + FOLD0))
                    if f == 0:
                        pe.wait_ge(g.d_w[u], (r + (2 - u)) * (DW // 2))
                    fold_product(pe, g, u, f, g.ps[:, FO, :]).then_inc(fold_ps, 1)

                def queries(q, u, t):
                    n, h, a = t // 4, t // 2 % 2, t % 2
                    pe.wait_ge(rope_ok, 8 * q + (t - 1 + ROPE0))
                    pe.wait_ge(fold_ok, 6 * q + (2 + FOLD0))
                    for k in range(KT):
                        for m, (cx, xx) in enumerate(split(g.CH[u], g.CL[u], g.XH, g.XL)):
                            mm = pe.matmul(g.ps[0:HALF, QA + a, :],
                                           cx[:, k, h * DQ + a * HALF:h * DQ + (a + 1) * HALF],
                                           xx[:, k, 512 * n:512 * n + 512], start=(k == 0 and m == 0),
                                           stop=(k == KT - 1 and m == 2))
                    mm.then_inc(q_ps, 1)

                def to_context(q, u, n):
                    pe.wait_ge(sum_ok, 8 * q + (4 * n + 4 + SUM0))
                    pe.wait_ge(fold_ok, 6 * q + (5 + FOLD0))
                    pe.wait_ge(qc_ok, 2 * q + (n + QC0))
                    for a in range(2):
                        for h in range(2):
                            mm = pe.matmul(g.ps[DC * h:DC * h + DC, QP, :], g.M[u][:, 2 * h + a, :],
                                           RO[:, n, h, a, :], start=(a == 0), stop=(a == 1))
                    mm.then_inc(qc_ps, 1)

                def scores(p, u, t):
                    pe.wait_ge(qc_ok, 2 * p + (t // 4 + 1 + QC0))
                    pe.wait_ge(exp_ok, 8 * p + (t - 1 + EXP0))
                    for h in range(2):
                        for m, kx in enumerate((g.KH, g.KL)):
                            mm = pe.matmul(g.ps[:, SC + t % 2, S * h:S * h + S], Q[h][u][:, t * P:(t + 1) * P],
                                           kx[:, S * (t // 2):S * (t // 2) + S], start=(m == 0), stop=(m == 1))
                    mm.then_inc(s_ps, 1)

                def turn(p, t):
                    pe.wait_ge(norm_ok, 8 * p + (t + 1))
                    pe.wait_ge(t_ok, 8 * p + (t + TOK0))
                    for j in range(4):
                        mm = pe.transpose(g.ps[:, PTB, j * P:(j + 1) * P],
                                          PB[t % 2][:, j // 2, (j % 2) * P:(j % 2 + 1) * P], g.ident[:, :])
                    mm.then_inc(t_ps, 1)

                def attend(p, b):
                    pe.wait_ge(t_ok, 8 * p + (2 * b + 2 + TOK0))
                    pe.wait_ge(cx_ok, 4 * p + (b + CXOK0))
                    for j in range(2):
                        for h in range(2):
                            mm = pe.matmul(g.ps[DC * h:DC * h + DC, CXB, 0:S], g.KV[:, 2 * b + j, 0, :],
                                           PTS[b % 2][:, 2 * h + j, :], start=(j == 0), stop=(j == 1))
                    mm.then_inc(cx_ps, 1)

                def pair(p, u, folds, asks):
                    for t in range(NT):
                        scores(p, u, t)
                        if asks:
                            queries(p + 1, 1 - u, t)
                        else:
                            if t == 0:
                                pe.wait_ge(cx_ok, 4 * p + CXOK0)
                            output_share(pe, g, t // 2, range(0, 4) if t % 2 == 0 else range(4, PAIRS - 1))
                        if t == 1:
                            to_context(p, u, 1)
                        if folds and t < 6:
                            fold(p + 2, u, t)
                        if t in (3, 5, 7):
                            attend(p, t // 2 - 1)
                        if t >= 1:
                            turn(p, t - 1)
                    if asks:
                        to_context(p + 1, 1 - u, 0)
                    turn(p, NT - 1)
                    attend(p, B - 1)

                pe.wait_ge(credit, 1)
                for t in range(NT):
                    queries(0, 0, t)
                    if t == FIRST:
                        to_context(0, 0, 0)
                pairs(pe, pair)

            @block.scalar
            def _(act):
                def fold(r, u, f):
                    act.wait_ge(fold_ps, 6 * r + (f + 1))
                    fold_keep(act, g, r, u, f, g.ps[:, FO, :]).then_inc(fold_hi if f in FOLD_SPLIT else fold_ok, 1)

                def to_context(q, u, n):
                    act.wait_ge(qc_ps, 2 * q + (n + 1 + QCPS0))
                    for h in range(2):
                        act.activation(Q[h][u][HI[h], 512 * n:512 * n + 512], g.ps[HI[h], QP, :],
                                       ACT.Copy).then_inc(qc_hi, 1)

                def softmax(p, t):
                    act.wait_ge(low_ok, 8 * p + (t + 1))
                    act.wait_ge(t_ps, 8 * p + (t - 1 + TPS0))
                    for h in range(2):
                        e = act.activation(PB[t % 2][:, h, :], g.ps[:, SC + t % 2, h * S:(h + 1) * S], ACT.Exp,
                                           bias=low[:, t % 2, h:h + 1], scale=-1.0,
                                           accum_out=tot[:, t % 2, h:h + 1])
                    e.then_inc(exp_ok, 1)

                def turned(p, t):
                    act.wait_ge(t_ps, 8 * p + (t + 1 + TPS0))
                    act.wait_ge(cx_ps, 4 * p + (t // 2 - 1 + CXPS0))
                    act.activation(PTS[t // 2 % 2][:, :, (t % 2) * P:(t % 2 + 1) * P],
                                   g.ps[:, PTB, :].rearrange("p (j n) -> p j n", j=4),
                                   ACT.Copy).then_inc(t_ok, 1)

                def attended(p, b):
                    act.wait_ge(cx_ps, 4 * p + (b + 1 + CXPS0))
                    act.activation(g.XCH[:, bass.ds(p, 1), S * b:S * b + S], g.ps[:, CXB, 0:S],
                                   ACT.Copy).then_inc(cx_hi, 1)

                def pair(p, u, folds, asks):
                    for t in range(NT):
                        softmax(p, t)
                        if t == 1:
                            to_context(p, u, 1)
                        if folds and t < 6:
                            fold(p + 2, u, t)
                        if t in (3, 5, 7):
                            attended(p, t // 2 - 1)
                        if t >= 1:
                            turned(p, t - 1)
                    if asks:
                        to_context(p + 1, 1 - u, 0)
                    turned(p, NT - 1)
                    attended(p, B - 1)

                act.wait_ge(credit, 1)
                to_context(0, 0, 0)
                pairs(act, pair)

            @block.gpsimd
            def _(pool):
                for s, v in starts:
                    pool.sem_inc(s, v)
                pool.sem_inc(credit, 2)
                with pool.Fori(0, PAIRS, 1) as q:
                    for st in range(4):
                        n, h, tm = st // 2, st % 2, TM[st % 2]
                        pool.wait_ge(rope_ok, 8 * q + (2 * st + 2 + ROPE0))
                        pool.wait_ge(qc_ps, 2 * q + (n + QCPS0 - 1))
                        pool.tensor_tensor(RO[:, n, h, 0, :], tm[:, 0, :], tm[:, 2, :],
                                           ALU.subtract).then_inc(sum_ok, 1)
                        pool.tensor_tensor(RO[:, n, h, 1, :], tm[:, 3, :], tm[:, 1, :],
                                           ALU.add).then_inc(sum_ok, 1)

            @block.vector
            def _(dve):
                def rotate(q, t):
                    st, a = t // 2, t % 2
                    dve.wait_ge(q_ps, 8 * q + (t + 1))
                    dve.wait_ge(sum_ok, 8 * q + (2 * st - 2 + SUM0))
                    batches = lambda x: x.rearrange("p (b s) -> p b s", b=2)
                    over = lambda x: x.unsqueeze(1).broadcast_to([HALF, 2, S])
                    src = batches(g.ps[0:HALF, QA + a, :])
                    c, s = (0, 1) if a == 0 else (3, 2)
                    dve.tensor_tensor(batches(TM[st % 2][:, c, :]), src, over(g.cosq[:, a, :]), ALU.mult)
                    dve.tensor_tensor(batches(TM[st % 2][:, s, :]), src, over(g.sinq[:, 1 - a, :]),
                                      ALU.mult).then_inc(rope_ok, 1)

                def fold(r, u, f):
                    if f in FOLD_SPLIT:
                        dve.wait_ge(fold_hi, 3 * r + (FOLD_SPLIT.index(f) + 1))
                        fold_rest(dve, g, r, u, f, g.ps[:, FO, :]).then_inc(fold_ok, 1)

                def to_context(q, u, n):
                    cols = slice(512 * n, 512 * n + 512)
                    dve.wait_ge(qc_hi, 4 * q + (2 * n + 2))
                    for h in range(2):
                        m = dve.tensor_tensor(Q[h][u][HI[1 - h], cols], g.ps[HI[h], QP, :], Q[h][u][HI[h], cols],
                                              ALU.subtract)
                    m.then_inc(qc_ok, 1)

                def attended(p, b):
                    dve.wait_ge(cx_hi, 4 * p + (b + 1))
                    cols = slice(S * b, S * b + S)
                    dve.tensor_tensor(g.XCL[:, bass.ds(p, 1), cols], g.ps[:, CXB, 0:S],
                                      g.XCH[:, bass.ds(p, 1), cols], ALU.subtract).then_inc(cx_ok, 1)

                def pair(p, u, folds, asks):
                    for t in range(NT):
                        dve.wait_ge(s_ps, 8 * p + (t + 1))
                        dve.tensor_reduce(low[:, t % 2, :], g.ps[:, SC + t % 2, :].rearrange("p (h s) -> p h s", h=2),
                                          AX.X, ALU.min).then_inc(low_ok, 1)
                        if asks:
                            rotate(p + 1, t)
                        dve.wait_ge(exp_ok, 8 * p + (t + 1 + EXP0))
                        dve.reciprocal(inv[:, t % 2, :], tot[:, t % 2, :]).then_inc(inv_ok, 1)
                        dve.wait_ge(inv_ok, 8 * p + (t + 1))
                        for h in range(2):
                            m = dve.tensor_scalar(PB[t % 2][:, h, :], PB[t % 2][:, h, :],
                                                  inv[:, t % 2, h:h + 1], None, ALU.mult)
                        m.then_inc(norm_ok, 1)
                        if t == 1:
                            to_context(p, u, 1)
                        if folds and t < 6:
                            fold(p + 2, u, t)
                        if t in (3, 5, 7):
                            attended(p, t // 2 - 1)
                    if asks:
                        to_context(p + 1, 1 - u, 0)
                    attended(p, B - 1)

                dve.wait_ge(credit, 1)
                dve.wait_ge(g.d_ropeq, 32)
                for t in range(NT):
                    rotate(0, t)
                    if t == FIRST + 1:
                        to_context(0, 0, 0)
                pairs(dve, pair)


def stage_moe(nc, g, i, out):
    with ExitStack() as ctx:
        sb = lambda name, shape, dt=F32: ctx.enter_context(nc.sbuf_tensor(name, shape, dt))
        sem = lambda name: ctx.enter_context(nc.semaphore(name))
        RING = 5
        GF, EF = 8 - TOP_G, 8 - TOP_E
        EP = ST_T * EPT
        eb = sb("eb", [P, E])
        EG = [sb(f"EG{n}", [P, EPT, KT, EI]) for n in range(RING)]
        EU = [sb(f"EU{n}", [P, EPT, KT, EI]) for n in range(RING)]
        ED = [sb(f"ED{n}", [P, EPT, D]) for n in range(RING)]
        XP = sb("XP", [P, 2, NT, D], F16)
        SG = sb("SG", [P, NT, E])
        SBI = sb("SBI", [P, NT, E])
        hl = sb("hl", [P, 2, NT * GROUPS, 2])
        tp = sb("tp", [P, 4, NT * GROUPS])
        GB = sb("GB", [P, NT, GF + GROUPS])
        GR = sb("GR", [P, NT, GF + GROUPS])
        g8 = sb("g8", [P, NT, 8])
        gm = sb("gm", [P, NT, GROUPS])
        mz = sb("mz", [P, NT, E])
        MB = sb("MB", [P, NT, EF + E])
        MR = sb("MR", [P, NT, EF + E])
        e8 = sb("e8", [P, NT, 8])
        MK = sb("MKE", [P, NT, E])
        MKb = sb("MKb", [P, NT, E], F16)
        wsel = sb("wsel", [P, NT, E])
        wsum = sb("wsum", [P, 3, NT])
        W = sb("W", [P, NT, E])
        WR_ = sb("WR_", [P, NT, E])
        out_gate = sb("out_gate", [P, 1])
        fin_gate = sb("fin_gate", [P, 1])
        WP = sb("WP", [P, NT, 2, EP], F16)
        place = sb("place", [P, NT, E])
        ioti = sb("ioti", [P, CAP], mybir.dt.int32)
        iotf = sb("iotf", [P, CAP])
        tri = sb("tri", [P, P], F16)
        ones = sb("ones", [P, P], F16)
        own = sb("own", [P, EPT])
        SM = sb("SM", [P, NT, E * CAP], F16)
        STT = g.wide[:, :, :].rearrange("p a n -> p (a n)").bitcast(F16)[:, 0:ST_T * T].rearrange(
            "p (n t) -> p n t", n=ST_T)
        ws = sb("ws", [P, ST_T, 2, EPT])
        wslot = sb("wslot", [P, ST_T])
        XG = sb("XG", [P, KT, E * CAP])
        SL = [sb(f"SL{u}", [P, 512]) for u in range(2)]
        HS = sb("HS", [P, KT, T])
        SE = [sb(f"SE{u}", [P, SLOTS]) for u in range(2)]
        HP = [sb(f"HP{u}", [P, EPT, SLOTS + CAP]) for u in range(2)]
        YP = sb("YP", [P, ST_T, 2, D], F16)

        count = lambda n: min(EPT, E - EPT * n)
        d_eb, stored, out_ps, gate_ok, xt_ps, xt = map(sem, ["d_eb", "stored", "out_ps", "gate_ok", "xt_ps3", "xt3"])
        n3 = Norm(sem, "n3", 2)
        d_e = [sem(f"d_e{n}") for n in range(RING)]
        (c_fill, iota_ok, iotf_ok, tri0, tri_ok, own_ok, rl_ps, sg_ok, gu_sh, sl_ok, hs_ok) = map(
            sem, ["c_fill", "iota_ok", "iotf_ok", "tri0", "tri_ok", "own_ok", "rl_ps",
                  "sg_ok", "gu_sh", "sl_ok", "hs_ok"])
        (rt, mk_ok, w_ok, wp_a, wp_b, cnt_ps, place_ok, s_ok, xp_a, xp_b, xg_ps, xg_act, xg_dve, ws_ps,
         ws_ok) = map(
            sem, ["rt", "mk_ok2", "w_ok", "wp_a", "wp_b", "cnt_ps", "place_ok", "s_ok", "xp_a", "xp_b",
                  "xg_ps", "xg_act", "xg_dve", "ws_ps", "ws_ok"])
        (gu_ps, se_ok, hp_ok, st_ps, st_ok, y_ps, yh_ok, yl_ok, acc_ps, fin_ok, hp0) = map(
            sem, ["gu_ps", "se_ok", "hp_ok", "st_ps", "st_ok", "y_ps2", "yh_ok", "yl_ok",
                  "acc_ps", "fin_ok", "hp0"])

        chunks = [(0, 11 * CAP), (11 * CAP, 22 * CAP), (22 * CAP, E * CAP)]
        gathers = [(k, c) for k in range(KT) for c in range(3)]
        GBANK = [6, 7, 0, 1, 2, 3]
        GU, Y, STB, ACC = 0, 2, 6, 4
        TURN_AFTER = (4, 6, 7)
        shared_steps = [(h, o) for h in range(2) for o in range(KT)]
        out_v = out.rearrange("b (t p) d -> p (b t) d", p=P)

        with nc.Block() as block:
            @block.sync
            def _(sp):
                sp.dma_start(eb[:, :], i["L1_ffn_e_bias"].partition_broadcast(P)).then_inc(d_eb, 16)
                for n in range(ST_T):
                    c, r = count(n), n % RING
                    if n >= RING:
                        sp.wait_ge(y_ps, n - RING + 1)
                    es = slice(EPT * n, EPT * n + c)
                    sp.dma_start(EG[r][:, 0:c], i["L1_ffn_W_gate"][es].rearrange("e (k p) n -> p e k n", p=P)
                                 ).then_inc(d_e[r], 16)
                    sp.dma_start(EU[r][:, 0:c], i["L1_ffn_W_up"][es].rearrange("e (k p) n -> p e k n", p=P)
                                 ).then_inc(d_e[r], 16)
                    sp.dma_start(ED[r][:, 0:c], i["L1_ffn_W_down"][es].rearrange("e p n -> p e n")
                                 ).then_inc(d_e[r], 16)
                for b in range(B):
                    sp.wait_ge(fin_ok, 2 * b + 2)
                    sp.dma_start(out_v[:, 2 * b:2 * b + 2, :], g.X[:, 2 * b:2 * b + 2, :]).then_inc(stored, 16)
                sp.wait_ge(stored, 16 * B)

            @block.gpsimd
            def _(pool):
                pool.memset(GB[:, :, 0:GF], BIG).then_inc(c_fill, 1)
                pool.memset(MB[:, :, 0:EF], BIG).then_inc(c_fill, 1)
                pool.memset(WP[:, :, :, E:EP], 0.0).then_inc(c_fill, 1)
                pool.iota(ioti[:, :], [[1, CAP]], base=1, channel_multiplier=0).then_inc(iota_ok, 1)
                pool.memset(ones[:, :], 1.0).then_inc(tri0, 1)
                pool.memset(tri[:, :], 1.0).then_inc(tri0, 1)
                pool.wait_ge(iota_ok, 1)
                pool.tensor_copy(iotf[:, :], ioti[:, :]).then_inc(iotf_ok, 1)
                pool.wait_ge(tri0, 2)
                pool.affine_select(out=tri[:, :], in_=tri[:, :], compare_op=ALU.is_gt, fill=0.0, base=0,
                                   pattern=[[1, P]], channel_multiplier=-1).then_inc(tri_ok, 1)
                for u in range(2):
                    pool.memset(HP[u][:, :, :], 0.0).then_inc(hp0, 1)

            @block.tensor
            def _(pe):
                def output(t):
                    if t >= 4:
                        pe.wait_ge(g.x_done, NT + t - 3)
                    output_share(pe, g, t, range(PAIRS - 1 if t < 4 else 0, PAIRS)).then_inc(out_ps, 1)

                def turn_normed(q):
                    if q >= 2:
                        pe.wait_ge(xt, q - 1)
                    norm_turn(pe, g, n3, q, g.ps[:, 4 + q % 2, :]).then_inc(xt_ps, 1)

                def shared_rows(n):
                    h, o = shared_steps[n]
                    pe.wait_ge(xt, 2 * h + 2)
                    if n >= 2:
                        pe.wait_ge(hs_ok, n - 1)
                    else:
                        pe.wait_ge(g.x_done, NT + 6 + 2 * n)
                    for w in range(2):
                        for k in range(KT):
                            mm = pe.matmul(g.ps[:, 2 * (n % 2) + w, :], g.shT[:, w, k, o * P:(o + 1) * P],
                                           g.XT[:, k, 512 * h:512 * h + 512], start=(k == 0), stop=(k == KT - 1))
                    mm.then_inc(gu_sh, 1)

                for t in range(NT):
                    output(t)
                    if t in TURN_AFTER:
                        turn_normed(TURN_AFTER.index(t))
                shared_rows(0)
                turn_normed(B - 1)
                shared_rows(1)
                pe.wait_ge(xt, B)
                for t in range(NT):
                    for k in range(KT):
                        mm = pe.matmul(g.ps[:, 6, t * E:(t + 1) * E], g.XT[:, k, t * P:(t + 1) * P], g.rwT[:, k, :],
                                       start=(k == 0), stop=(k == KT - 1))
                mm.then_inc(rl_ps, 1)
                shared_rows(2)
                shared_rows(3)
                pe.wait_ge(mk_ok, 2)
                pe.wait_ge(tri_ok, 1)
                for t in range(NT):
                    for m in range(t + 1):
                        mm = pe.matmul(g.ps[:, 5, t * E:(t + 1) * E], (tri if m == t else ones)[:, :],
                                       MKb[:, m, :], start=(m == 0), stop=(m == t))
                mm.then_inc(cnt_ps, 1)
                pe.wait_ge(hs_ok, 4)
                pe.wait_ge(xp_b, B)
                for t in range(NT):
                    pe.wait_ge(s_ok, t + 1)
                    for (k, c), bank in zip(gathers, GBANK):
                        a, z = chunks[c]
                        for part in range(2):
                            mm = pe.matmul(g.ps[:, bank, 0:z - a], XP[:, part, t, k * P:(k + 1) * P],
                                           SM[:, t, a:z], start=(t == 0 and part == 0),
                                           stop=(t == NT - 1 and part == 1))
                    if t == NT - 1:
                        mm.then_inc(xg_ps, 1)
                    if t == 0:
                        pe.wait_ge(wp_b, 1)
                        pe.wait_ge(c_fill, 3)
                    for n in range(ST_T):
                        m = CAP * count(n)
                        mm = pe.matmul(g.ps[0:m, 4, 2 * EPT * n:2 * EPT * (n + 1)],
                                       SM[:, t, SLOTS * n:SLOTS * n + m], WP[:, t, :, EPT * n:EPT * n + EPT],
                                       start=(t == 0 and n == 0), stop=(t == NT - 1), skip_group_check=True)
                mm.then_inc(ws_ps, 1)

                def gate_up(n):
                    r = n % RING
                    pe.wait_ge(d_e[r], 48 * (n // RING + 1))
                    if n >= 2:
                        pe.wait_ge(hp_ok, n - 1)
                    for j in range(count(n)):
                        xs = slice((EPT * n + j) * CAP, (EPT * n + j + 1) * CAP)
                        for w, wt in enumerate((EG[r], EU[r])):
                            for k in range(KT):
                                mm = pe.matmul(g.ps[:, GU + n % 2, w * SLOTS + j * CAP:w * SLOTS + (j + 1) * CAP],
                                               wt[:, j, k, :], XG[:, k, xs], start=(k == 0), stop=(k == KT - 1))
                    mm.then_inc(gu_ps, 1)

                def turn(n):
                    m = CAP * count(n)
                    if n >= 2:
                        pe.wait_ge(st_ok, n - 1)
                    o = g.ps[0:m, STB + n % 2, :].bitcast(F16)
                    for t in range(NT):
                        mm = pe.transpose(o[:, t * P:(t + 1) * P], SM[:, t, SLOTS * n:SLOTS * n + m],
                                          g.ident16[:, :])
                    mm.then_inc(st_ps, 1)

                def down(n):
                    m = CAP * count(n)
                    pe.wait_ge(hp_ok, n + 1)
                    if n >= 2:
                        pe.wait_ge(yl_ok, n - 1)
                    flat = HP[n % 2][:, :, :].rearrange("p j w -> p (j w)")
                    for j in range(count(n)):
                        mm = pe.matmul(g.ps[0:m, Y + n % 2, 0:D], flat[:, SLOTS * j:SLOTS * j + m],
                                       ED[n % RING][:, j, :], start=(j == 0), stop=(j == count(n) - 1))
                    mm.then_inc(y_ps, 1)

                pe.wait_ge(xg_act, 1)
                turn(0)
                pe.wait_ge(xg_dve, 1)
                turn(1)
                pe.wait_ge(xg_act, 3)
                pe.wait_ge(xg_dve, 3)
                for n in range(ST_T):
                    gate_up(n)
                    if n + 2 < ST_T:
                        turn(n + 2)
                    if n >= 1:
                        down(n - 1)
                pe.wait_ge(st_ok, ST_T)
                pe.wait_ge(ws_ok, 1)
                acc = lambda t: g.ps[:, ACC + t // 2, D * (t % 2):D * (t % 2) + D]
                for t in range(NT):
                    for k in range(KT):
                        pe.matmul(acc(t), HS[:, k, t * P:(t + 1) * P], g.shT[:, 2, k, :],
                                  start=(t % 2 == 0 and k == 0), stop=False, skip_group_check=True)
                down(ST_T - 1)

                def scatter(t, n):
                    m = CAP * count(n)
                    for part in range(2):
                        mm = pe.matmul(acc(t), STT[0:m, n, t * P:(t + 1) * P], YP[0:m, n, part, :], start=False,
                                       stop=(n == ST_T - 1 and part == 1), skip_group_check=True)
                    return mm
                pe.wait_ge(yl_ok, ST_T - 1)
                for t in range(4):
                    for n in range(ST_T - 1):
                        scatter(t, n)
                pe.wait_ge(yl_ok, ST_T)
                for t in range(NT):
                    for n in range(ST_T - 1 if t < 4 else 0, ST_T):
                        mm = scatter(t, n)
                    mm.then_inc(acc_ps, 1)

            @block.scalar
            def _(act):
                def turned_norm(q):
                    act.wait_ge(xt_ps, q + 1)
                    act.activation(g.XT[:, :, S * q:S * q + S],
                                   g.ps[:, 4 + q % 2, :].rearrange("p (k s) -> p k s", k=KT),
                                   ACT.Copy).then_inc(xt, 1)
                    act.wait_ge(n3.xn, 2 * q + 2)
                    act.activation(XP[:, 0, 2 * q:2 * q + 2, :], g.XN[:, 2 * q:2 * q + 2, :], ACT.Copy,
                                   scale=UP).then_inc(xp_a, 1)

                def shared_gate(n):
                    act.wait_ge(gu_sh, n + 1)
                    if n >= 2:
                        act.wait_ge(hs_ok, n - 1)
                    act.activation(SL[n % 2][:, :], g.ps[:, 2 * (n % 2), :], ACT.Silu).then_inc(sl_ok, 1)

                for q in range(B):
                    norm_root(act, g, n3, q)
                    if q >= 1:
                        turned_norm(q - 1)
                shared_gate(0)
                turned_norm(B - 1)
                shared_gate(1)
                act.wait_ge(rl_ps, 1)
                act.activation(SG[:, :, :], g.ps[:, 6, 0:NT * E], ACT.Sigmoid).then_inc(sg_ok, 1)
                shared_gate(2)
                shared_gate(3)
                act.wait_ge(w_ok, 1)
                act.activation(WP[:, :, 0, 0:E], W[:, :, :], ACT.Copy, scale=UPW).then_inc(wp_a, 1)
                act.wait_ge(xg_ps, 1)
                for n, ((k, c), bank) in enumerate(zip(gathers, GBANK)):
                    if n % 2 == 0:
                        a, z = chunks[c]
                        act.activation(XG[:, k, a:z], g.ps[:, bank, 0:z - a], ACT.Copy,
                                       scale=1.0 / UP).then_inc(xg_act, 1)

                def results(n):
                    m = CAP * count(n)
                    act.wait_ge(y_ps, n + 1)
                    if n == 0:
                        act.wait_ge(ws_ok, 1)
                    act.activation(YP[0:m, n, 0, :], g.ps[0:m, Y + n % 2, 0:D], ACT.Copy,
                                   scale=wslot[0:m, n:n + 1]).then_inc(yh_ok, 1)

                def turned(n):
                    m = CAP * count(n)
                    act.wait_ge(st_ps, n + 1)
                    act.wait_ge(st_ok, n)
                    act.activation(STT[0:m, n, :], g.ps[0:m, STB, :].bitcast(F16), ACT.Copy).then_inc(st_ok, 1)

                turned(0)
                for n in range(ST_T):
                    m = CAP * count(n)
                    act.wait_ge(gu_ps, n + 1)
                    if n >= 2:
                        act.wait_ge(hp_ok, n - 1)
                    act.activation(SE[n % 2][:, 0:m], g.ps[:, GU + n % 2, 0:m], ACT.Silu).then_inc(se_ok, 1)
                    if n >= 1:
                        results(n - 1)
                    if n % 2 == 0 and n + 2 < ST_T:
                        turned(n + 2)
                results(ST_T - 1)

            @block.vector
            def _(dve):
                steps = 0

                def link(ins):
                    nonlocal steps
                    steps += 1
                    ins.then_inc(rt, 1)
                    dve.wait_ge(rt, steps)

                id3 = g.ident[:, 0:SLOTS].rearrange("p (j c) -> p j c", j=EPT)
                dve.tensor_reduce(own[:, :], id3, AX.X, ALU.add).then_inc(own_ok, 1)
                link(dve.tensor_scalar(fin_gate[:, :], g.gate[:, 3:4], 1.0 / UPW, None, ALU.mult))
                link(dve.tensor_scalar(out_gate[:, :], g.gate[:, 1:2], 1.0 / UP, None, ALU.mult))

                def second_part(q):
                    t = slice(2 * q, 2 * q + 2)
                    dve.wait_ge(xp_a, q + 1)
                    dve.scalar_tensor_tensor(out=XP[:, 1, t, :], in0=g.XN[:, t, :], scalar=UP, in1=XP[:, 0, t, :],
                                             op0=ALU.mult, op1=ALU.subtract).then_inc(xp_b, 1)

                for t in range(NT):
                    dve.wait_ge(out_ps, t + 1)
                    dve.scalar_tensor_tensor(out=g.X[:, t, :], in0=g.ps[:, OUT_BANKS[t % 4], 0:D], scalar=out_gate[:, 0:1],
                                             in1=g.X[:, t, :], op0=ALU.mult, op1=ALU.add).then_inc(g.x_done, 1)
                    if t % 2 == 1:
                        dve.wait_ge(g.x_done, NT + t + 1)
                        norm_stats(dve, g, n3, t // 2)
                        norm_inverse(dve, g, n3, t // 2)
                        norm_apply(dve, g, n3, t // 2)
                    elif t >= 4:
                        second_part(t // 2 - 2)

                def shared(n):
                    h, o = shared_steps[n]
                    dve.wait_ge(sl_ok, n + 1)
                    dve.tensor_tensor(HS[:, o, 512 * h:512 * h + 512], SL[n % 2][:, :],
                                      g.ps[:, 2 * (n % 2) + 1, :], ALU.mult).then_inc(hs_ok, 1)
                shared(0)
                second_part(B - 2)
                second_part(B - 1)
                shared(1)
                dve.wait_ge(d_eb, 16)
                dve.wait_ge(sg_ok, 1)
                link(dve.tensor_tensor(SBI[:, :, :], SG[:, :, :], eb[:, :].unsqueeze(1).broadcast_to([P, NT, E]),
                                       ALU.add))
                four = SBI[:, :, :].rearrange("p t (g a b) -> p (t g) a b", a=2, b=2)
                dve.tensor_tensor(hl[:, 0, :, :], four[:, :, :, 0], four[:, :, :, 1], ALU.max)
                link(dve.tensor_tensor(hl[:, 1, :, :], four[:, :, :, 0], four[:, :, :, 1], ALU.min))
                dve.tensor_tensor(tp[:, 0, :], hl[:, 0, :, 0], hl[:, 0, :, 1], ALU.max)
                dve.tensor_tensor(tp[:, 1, :], hl[:, 0, :, 0], hl[:, 0, :, 1], ALU.min)
                link(dve.tensor_tensor(tp[:, 2, :], hl[:, 1, :, 0], hl[:, 1, :, 1], ALU.max))
                link(dve.tensor_tensor(tp[:, 3, :], tp[:, 1, :], tp[:, 2, :], ALU.max))
                dve.wait_ge(c_fill, 3)
                tg = lambda x: x.rearrange("p (t g) -> p t g", t=NT)
                link(dve.tensor_tensor(GB[:, :, GF:], tg(tp[:, 0, :]), tg(tp[:, 3, :]), ALU.add))
                for t in range(NT):
                    last = dve.max(g8[:, t, :], GB[:, t, :])
                    if t < NT - 1:
                        last.then_inc(own_ok, 1)
                link(last)
                dve.wait_ge(own_ok, NT)
                for t in range(NT):
                    last = dve.match_replace(GR[:, t, :], g8[:, t, :], GB[:, t, :], NEG)
                    if t < NT - 1:
                        last.then_inc(own_ok, 1)
                link(last)
                dve.wait_ge(own_ok, 2 * NT - 1)
                link(dve.tensor_tensor(gm[:, :, :], GB[:, :, GF:], GR[:, :, GF:], ALU.not_equal))
                shared(2)
                sp4 = lambda x: x.rearrange("p t (g a) -> p t g a", a=GE)
                link(dve.tensor_tensor(sp4(mz[:, :, :]), sp4(SBI[:, :, :]),
                                       gm[:, :, :].unsqueeze(3).broadcast_to([P, NT, GROUPS, GE]), ALU.mult))
                link(dve.tensor_scalar(MB[:, :, EF:], mz[:, :, :], 0.0, None, ALU.add))
                for t in range(NT):
                    last = dve.max(e8[:, t, :], MB[:, t, :])
                    if t < NT - 1:
                        last.then_inc(own_ok, 1)
                link(last)
                dve.wait_ge(own_ok, 3 * NT - 2)
                for t in range(NT):
                    last = dve.match_replace(MR[:, t, :], e8[:, t, :], MB[:, t, :], NEG)
                    if t < NT - 1:
                        last.then_inc(own_ok, 1)
                link(last)
                dve.wait_ge(own_ok, 4 * NT - 3)
                dve.tensor_tensor(MKb[:, :, :], MB[:, :, EF:], MR[:, :, EF:], ALU.not_equal).then_inc(mk_ok, 1)
                dve.tensor_tensor(MK[:, :, :], MB[:, :, EF:], MR[:, :, EF:], ALU.not_equal).then_inc(mk_ok, 1)
                dve.wait_ge(mk_ok, 2)
                link(dve.tensor_tensor(wsel[:, :, :], SG[:, :, :], MK[:, :, :], ALU.mult))
                link(dve.tensor_reduce(wsum[:, 0, :], wsel[:, :, :], AX.X, ALU.add))
                link(dve.tensor_scalar(wsum[:, 1, :], wsum[:, 0, :], 1e-20, None, ALU.add))
                link(dve.reciprocal(wsum[:, 2, :], wsum[:, 1, :]))
                link(dve.tensor_tensor(WR_[:, :, :], wsel[:, :, :],
                                       wsum[:, 2, :].unsqueeze(2).broadcast_to([P, NT, E]), ALU.mult))
                dve.tensor_scalar(W[:, :, :], WR_[:, :, :], ROUTE_SCALE, None, ALU.mult).then_inc(w_ok, 1)

                shared(3)
                dve.wait_ge(cnt_ps, 1)
                dve.scalar_tensor_tensor(out=place[:, :, :],
                                         in0=g.ps[:, 5, 0:NT * E].rearrange("p (t e) -> p t e", t=NT),
                                         scalar=1.0, in1=MK[:, :, :], op0=ALU.add,
                                         op1=ALU.mult).then_inc(place_ok, 1)
                dve.wait_ge(w_ok, 1)
                dve.wait_ge(wp_a, 1)
                dve.scalar_tensor_tensor(out=WP[:, :, 1, 0:E], in0=W[:, :, :], scalar=UPW, in1=WP[:, :, 0, 0:E],
                                         op0=ALU.mult, op1=ALU.subtract).then_inc(wp_b, 1)
                dve.wait_ge(place_ok, 1)
                dve.wait_ge(iotf_ok, 1)
                for t in range(NT):
                    dve.tensor_tensor(SM[:, t, :].rearrange("p (e c) -> p e c", c=CAP),
                                      place[:, t, :].unsqueeze(2).broadcast_to([P, E, CAP]),
                                      iotf[:, :].unsqueeze(1).broadcast_to([P, E, CAP]),
                                      ALU.is_equal).then_inc(s_ok, 1)
                dve.wait_ge(xg_ps, 1)
                for n, ((k, c), bank) in enumerate(zip(gathers, GBANK)):
                    if n % 2 == 1:
                        a, z = chunks[c]
                        dve.tensor_scalar(XG[:, k, a:z], g.ps[:, bank, 0:z - a], 1.0 / UP, None,
                                          ALU.mult).then_inc(xg_dve, 1)
                dve.wait_ge(ws_ps, 1)
                link(dve.tensor_tensor(ws[0:SLOTS].rearrange("p n a j -> p (n a) j"),
                                       g.ps[0:SLOTS, 4, 0:2 * EPT * ST_T].rearrange("p (n j) -> p n j", j=EPT),
                                       own[0:SLOTS, :].unsqueeze(1).broadcast_to([SLOTS, 2 * ST_T, EPT]), ALU.mult))
                dve.tensor_reduce(wslot[0:SLOTS, :], ws[0:SLOTS].rearrange("p n a j -> p n (a j)"), AX.X,
                                  ALU.add).then_inc(ws_ok, 1)

                def second(n):
                    m = CAP * count(n)
                    dve.wait_ge(yh_ok, n + 1)
                    dve.scalar_tensor_tensor(out=YP[0:m, n, 1, :], in0=g.ps[0:m, Y + n % 2, 0:D],
                                             scalar=wslot[0:m, n:n + 1], in1=YP[0:m, n, 0, :], op0=ALU.mult,
                                             op1=ALU.subtract).then_inc(yl_ok, 1)

                def turned(n):
                    m = CAP * count(n)
                    dve.wait_ge(st_ps, n + 1)
                    dve.wait_ge(st_ok, n)
                    dve.tensor_copy(STT[0:m, n, :], g.ps[0:m, STB + 1, :].bitcast(F16)).then_inc(st_ok, 1)

                turned(1)
                dve.wait_ge(hp0, 2)
                for n in range(ST_T):
                    m = CAP * count(n)
                    dve.wait_ge(se_ok, n + 1)
                    if n >= 2:
                        dve.wait_ge(y_ps, n - 1)
                    c = count(n)
                    dve.tensor_tensor(HP[n % 2][:, 0:c, 0:CAP],
                                      SE[n % 2][:, 0:m].rearrange("p (j w) -> p j w", j=c),
                                      g.ps[:, GU + n % 2, SLOTS:SLOTS + m].rearrange("p (j w) -> p j w", j=c),
                                      ALU.mult).then_inc(hp_ok, 1)
                    if n >= 1:
                        second(n - 1)
                    if n % 2 == 1 and n + 2 < ST_T:
                        turned(n + 2)
                second(ST_T - 1)
                for b in range(B):
                    dve.wait_ge(acc_ps, 2 * b + 2)
                    for t in (2 * b, 2 * b + 1):
                        dve.scalar_tensor_tensor(out=g.X[:, t, :], in0=g.ps[:, ACC + b, D * (t % 2):D * (t % 2) + D],
                                                 scalar=fin_gate[:, 0:1], in1=g.X[:, t, :], op0=ALU.mult,
                                                 op1=ALU.add).then_inc(fin_ok, 1)


def store_x(nc, g, out):
    with nc.semaphore("stored") as stored, nc.Block() as block:
        @block.sync
        def _(sp):
            sp.dma_start(out.rearrange("b (t p) d -> p (b t) d", p=P), g.X[:, :, :]).then_inc(stored, 16)
            sp.wait_ge(stored, 16)


def build(nc, i, out, stages=4):
    g = Shared()
    with ExitStack() as ctx:
        sb = lambda name, shape, dt=F32: ctx.enter_context(nc.sbuf_tensor(name, shape, dt))
        sem = lambda name: ctx.enter_context(nc.semaphore(name))
        g.ps = ctx.enter_context(nc.psum_tensor("ps", [P, 8, 512], F32))
        g.X = sb("X", [P, NT, D])
        g.XN = sb("XN", [P, NT, D])
        g.XT = sb("XT", [P, KT, T])
        g.stat, g.mv = sb("stat", [P, NT, 6]), sb("mv", [P, NT, 2])
        g.var, g.std, g.rstd = sb("var", [P, NT]), sb("std", [P, NT]), sb("rstd", [P, NT])
        g.ident, g.ident16 = sb("ident", [P, P]), sb("ident16", [P, P], F16)
        g.gate = sb("gate", [P, 4])
        g.wide = sb("wide", [P, 4, NT * S])
        g.XCH, g.XCL = [g.wide[:, 2 * u:2 * u + 2, :].rearrange("p a n -> p (a n)").bitcast(F16).rearrange(
            "p (r t) -> p r t", r=PAIRS) for u in range(2)]
        g.NH, g.NL = sb("NH", [P, PAIRS, D], F16), sb("NL", [P, PAIRS, D], F16)
        g.shT = sb("shT", [P, 3, KT, SHARED])
        g.rwT = sb("rwT", [P, KT, E])
        g.d_ropeq = sem("d_ropeq")
        g.x_done = sem("x_done")
        with ExitStack() as middle:
            mb = lambda name, shape, dt=F32: middle.enter_context(nc.sbuf_tensor(name, shape, dt))
            g.cosq, g.sinq = mb("cosq", [HALF, 2, S]), mb("sinq", [HALF, 2, S])
            g.KV = mb("KV", [P, NT, 2, DC])
            g.KH, g.KL = mb("KH", [P, T], F16), mb("KL", [P, T], F16)
            g.XH, g.XL = mb("XH", [P, KT, T], F16), mb("XL", [P, KT, T], F16)
            two = lambda name, shape, dt=F32: [mb(f"{name}{u}", shape, dt) for u in range(2)]
            g.WQ, g.WCQ, g.WCV = two("WQ", [P, 2, D]), two("WCQ", [P, 2, DQ]), two("WCV", [P, 2, DC])
            g.WQR, g.WKR, g.WO = two("WQR", [HALF, 2, 2, R]), two("WKR", [DC, 2, R]), two("WO", [P, KT, 2 * HK])
            g.RT = mb("RT", [R, 2, 2 * HALF + DC])
            g.WOT = mb("WOT", [P, 2, D])
            g.CH, g.CL = two("CH", [P, KT, 2 * DQ], F16), two("CL", [P, KT, 2 * DQ], F16)
            g.M = two("M", [HALF, 4, DC])
            g.d_w = [sem("d_w_even"), sem("d_w_odd")]
            stage_first_layer(nc, g, i)
            if stages >= 3:
                stage_latent_attention(nc, g, i)
        if stages >= 4:
            stage_moe(nc, g, i, out)
        else:
            store_x(nc, g, out)


_INS = ["x", "ctx_512", "g_xattn", "g_ffn", "L0_xattn_Wq", "L0_xattn_Wk", "L0_xattn_gamma_raw", "L0_ffn_Wr",
        "L0_ffn_br", "L0_ffn_W1", "L0_ffn_W2", "L1_xattn_Wq", "L1_xattn_w_kc_q", "L1_xattn_w_kc_kv",
        "L1_xattn_W_qr", "L1_xattn_W_kr", "L1_xattn_Wo", "L1_ffn_router_w", "L1_ffn_e_bias", "L1_ffn_W_gate",
        "L1_ffn_W_up", "L1_ffn_W_down", "L1_ffn_shared_gate", "L1_ffn_shared_up", "L1_ffn_shared_down"]


def rope_tables():
    def table(width):
        inv = (1.0 / 10000.0 ** (np.arange(0, width, 2, dtype=np.float32) / np.float32(width))).astype(np.float32)
        f = np.arange(S, dtype=np.float32)[:, None] * inv[None, :]
        return np.repeat(np.sin(f), 2, axis=-1), np.repeat(np.cos(f), 2, axis=-1)
    sq, cq = table(DQ)
    sk, ck = table(DC)
    sk = np.concatenate([-sk[:, :DC // 2], sk[:, DC // 2:]], axis=1)
    halves = lambda x: np.ascontiguousarray(x.T.reshape(2, HALF, S).transpose(1, 0, 2))
    rows = lambda x: np.ascontiguousarray(x.reshape(2, P, DC).transpose(1, 0, 2))
    return {"cosq": halves(cq), "sinq": halves(sq), "cosk": rows(ck), "sink": rows(sk)}


def kernel(**inputs):
    import concourse.bacc as _bacc
    from concourse.bass_utils import run_bass_kernel_spmd as _run

    nc = _bacc.Bacc("TRN2", target_bir_lowering=False, num_devices=1)
    arrays, args = {}, {}
    for name, a in list((n, inputs[n]) for n in _INS) + list(rope_tables().items()):
        a = np.ascontiguousarray(a)
        arrays[f"in_{name}_dram"] = a
        args[name] = nc.dram_tensor(f"in_{name}_dram", a.shape, mybir.dt.from_np(a.dtype), kind="ExternalInput").ap()
    out = nc.dram_tensor("out_0_dram", (B, S, D), F32, kind="ExternalOutput").ap()
    build(nc, args, out, STAGES)
    r = _run(nc, [arrays], core_ids=[0])
    return r.results[0]["out_0_dram"]
```
